# Optimizing a Trainium2 kernel written in Bass

```python
import numpy as np
import jax
import jax.numpy as jnp

def _softmax(x, axis=-1):
    return jax.nn.softmax(x, axis=axis)

def _gelu(x):
    return jax.nn.gelu(x, approximate=True)

def _silu(x):
    return jax.nn.silu(x)

def _sigmoid(x):
    return jax.nn.sigmoid(x)

def _layernorm(x, axis=-1, eps=1e-05):
    m = jnp.mean(x, axis=axis, keepdims=True)
    v = jnp.var(x, axis=axis, keepdims=True)
    return (x - m) / jnp.sqrt(v + eps)

def _scatter_add(tgt, idx, src, axis=0):
    return tgt.at[idx].add(src)

def _segment_sum(src, seg, n):
    return jax.ops.segment_sum(src, seg, n)
kernel_name = 'mk_adj_resnorm_d4_adj_r2_63602a'

def setup_inputs(seed: int=0):
    np.random.seed(seed)
    _w = jnp.asarray

    def _rec_inputs():
        import jax
        import jax.numpy as jnp
        _gk = jax.random.key(seed)
        x = 7.22e-05 + 1 * jax.random.normal(jax.random.fold_in(_gk, 1), (16, 512, 128), jnp.float32)
        _a = jax.random.bernoulli(jax.random.fold_in(_gk, 2), 0.0078125, (512, 512))
        _a = jnp.logical_or(_a, jnp.swapaxes(_a, -1, -2))
        _a = jnp.logical_or(_a, jnp.eye(512, dtype=bool))
        _af = _a.astype(jnp.float32)
        _af = _af * jax.random.uniform(jax.random.fold_in(_gk, 3), (512, 512), jnp.float32, 0.05, 0.000976562)
        adj = _af
        return (x, adj)
    x, adj = _rec_inputs()

    def _L0_gnn_setup():
        import jax, jax.numpy as jnp
        import numpy as np
        N_STEPS = 8
        SPATIAL_SCALE = 1.0
        key = jax.random.key(seed)
        ks = jax.random.split(key, 6)
        B, N, D = (32, 512, 128)
        x = jax.random.normal(ks[0], (B, N, D), dtype=jnp.float32)
        adj_mx = jax.random.uniform(ks[1], (N, N), dtype=jnp.float32) / N
        alpha_train = jnp.ones((N,), dtype=jnp.float32)
        w = jnp.eye(D, dtype=jnp.float32) + 0.01 * jax.random.normal(ks[2], (D, D), dtype=jnp.float32)
        d = jax.random.uniform(ks[3], (D,), dtype=jnp.float32)
        fc_in_w = jax.random.normal(ks[4], (D, D), dtype=jnp.float32) * (1.0 / np.sqrt(D))
        fc_in_b = jnp.zeros((D,), dtype=jnp.float32)
        return {'x': x, 'adj_mx': adj_mx, 'alpha_train': alpha_train, 'w': w, 'd': d, 'fc_in_w': fc_in_w, 'fc_in_b': fc_in_b, 'vt': 0}
    _L0_gnn_all = _L0_gnn_setup()
    _L0_gnn_in = {k: v for k, v in _L0_gnn_all.items() if k in ('alpha_train', 'w', 'd', 'fc_in_w', 'fc_in_b')}
    del _L0_gnn_all

    def _L1_gnn_setup():
        import jax, jax.numpy as jnp
        import numpy as np
        B, T, D, H = (64, 1024, 128, 128)
        MAX_SKIP = 4

        def _lstm_last(Wih, Whh, bih, bhh, xs):
            N, _, Hd = xs.shape
            bias = bih + bhh

            def step(carry, x_t):
                h, c = carry
                g = x_t @ Wih.T + h @ Whh.T + bias
                i, f, gg, o = jnp.split(g, 4, axis=-1)
                c = jax.nn.sigmoid(f) * c + jax.nn.sigmoid(i) * jnp.tanh(gg)
                h = jax.nn.sigmoid(o) * jnp.tanh(c)
                return ((h, c), None)
            init = (jnp.zeros((N, Hd), xs.dtype), jnp.zeros((N, Hd), xs.dtype))
            (h_last, _), _ = jax.lax.scan(step, init, jnp.swapaxes(xs, 0, 1))
            return h_last
        key = jax.random.key(seed)
        ks = jax.random.split(key, 8)
        s = 0.05
        x = jax.random.normal(ks[0], (B, T, D), jnp.float32)
        adj = jax.random.uniform(ks[1], (T, T), jnp.float32) / T
        Wg0 = jax.random.normal(ks[2], (D, H), jnp.float32) * s
        bg0 = jnp.zeros((H,), jnp.float32)
        Wg1 = jax.random.normal(ks[3], (H, H), jnp.float32) * s
        bg1 = jnp.zeros((H,), jnp.float32)
        Wih = jax.random.normal(ks[4], (MAX_SKIP, 4 * H, H), jnp.float32) * s
        Whh = jax.random.normal(ks[5], (MAX_SKIP, 4 * H, H), jnp.float32) * s
        bih = jax.random.normal(ks[6], (MAX_SKIP, 4 * H), jnp.float32) * s
        bhh = jax.random.normal(ks[7], (MAX_SKIP, 4 * H), jnp.float32) * s
        return dict(x=x, adj=adj, Wg0=Wg0, bg0=bg0, Wg1=Wg1, bg1=bg1, Wih=Wih, Whh=Whh, bih=bih, bhh=bhh)
    _L1_gnn_all = _L1_gnn_setup()
    _L1_gnn_in = {k: v for k, v in _L1_gnn_all.items() if k in ('Wg0', 'bg0', 'Wg1', 'bg1', 'Wih', 'Whh', 'bih', 'bhh')}
    del _L1_gnn_all

    def _L2_gnn_setup():
        import jax, jax.numpy as jnp
        import numpy as np
        EPS = 1e-05

        def _batchnorm(x, gamma, beta):
            mu = jnp.mean(x, axis=0)
            var = jnp.var(x, axis=0)
            return (x - mu) * jax.lax.rsqrt(var + EPS) * gamma + beta
        key = jax.random.key(seed)
        ks = jax.random.split(key, 4)
        b, n, d, h, o = (32, 1024, 128, 256, 128)
        features = jax.random.normal(ks[0], (b, n, d), dtype=jnp.float32)
        A = jax.random.uniform(ks[1], (n, n), dtype=jnp.float32)
        lim1 = float(np.sqrt(6.0 / (d + h)))
        W1 = jax.random.uniform(ks[2], (h, d), minval=-lim1, maxval=lim1, dtype=jnp.float32)
        b1 = jnp.zeros((h,), jnp.float32)
        lim2 = float(np.sqrt(6.0 / (h + o)))
        W2 = jax.random.uniform(ks[3], (o, h), minval=-lim2, maxval=lim2, dtype=jnp.float32)
        b2 = jnp.zeros((o,), jnp.float32)
        g1 = jnp.ones((h,), jnp.float32)
        be1 = jnp.zeros((h,), jnp.float32)
        g2 = jnp.ones((o,), jnp.float32)
        be2 = jnp.zeros((o,), jnp.float32)
        return {'features': features, 'A': A, 'W1': W1, 'b1': b1, 'g1': g1, 'be1': be1, 'W2': W2, 'b2': b2, 'g2': g2, 'be2': be2}
    _L2_gnn_all = _L2_gnn_setup()
    _L2_gnn_in = {k: v for k, v in _L2_gnn_all.items() if k in ('W1', 'b1', 'g1', 'be1', 'W2', 'b2', 'g2', 'be2')}
    del _L2_gnn_all

    def _L3_gnn_setup():
        import jax, jax.numpy as jnp
        import numpy as np
        BT, N, D, HEADS, E = (512, 64, 128, 4, 256)
        LRELU_SLOPE = 0.2
        EPS = 1e-08
        key = jax.random.key(seed)
        ks = jax.random.split(key, 8)
        d = D
        return {'H': jax.random.normal(ks[0], (BT, N, d), jnp.float32), 'W_lin': jax.random.normal(ks[1], (d, d), jnp.float32) / np.sqrt(d).astype(np.float32), 'W_val': jax.random.normal(ks[2], (d, d), jnp.float32) / np.sqrt(d).astype(np.float32), 'a': jax.random.normal(ks[3], (HEADS, d // HEADS), jnp.float32), 'W_out': jax.random.normal(ks[4], (d, d), jnp.float32) / np.sqrt(d).astype(np.float32), 'A0': jax.random.uniform(ks[5], (N, N), jnp.float32), 'src': jax.random.randint(ks[6], (E,), 0, N, jnp.int32), 'dst': jax.random.randint(ks[7], (E,), 0, N, jnp.int32)}
    _L3_gnn_all = _L3_gnn_setup()
    _L3_gnn_in = {k: v for k, v in _L3_gnn_all.items() if k in ('W_lin', 'W_val', 'a', 'W_out', 'src', 'dst')}
    del _L3_gnn_all
    return {'x': x, 'adj': adj, 'L0_gnn_alpha_train': _L0_gnn_in['alpha_train'], 'L0_gnn_w': _L0_gnn_in['w'], 'L0_gnn_d': _L0_gnn_in['d'], 'L0_gnn_fc_in_w': _L0_gnn_in['fc_in_w'], 'L0_gnn_fc_in_b': _L0_gnn_in['fc_in_b'], 'L1_gnn_Wg0': _L1_gnn_in['Wg0'], 'L1_gnn_bg0': _L1_gnn_in['bg0'], 'L1_gnn_Wg1': _L1_gnn_in['Wg1'], 'L1_gnn_bg1': _L1_gnn_in['bg1'], 'L1_gnn_Wih': _L1_gnn_in['Wih'], 'L1_gnn_Whh': _L1_gnn_in['Whh'], 'L1_gnn_bih': _L1_gnn_in['bih'], 'L1_gnn_bhh': _L1_gnn_in['bhh'], 'L2_gnn_W1': _L2_gnn_in['W1'], 'L2_gnn_b1': _L2_gnn_in['b1'], 'L2_gnn_g1': _L2_gnn_in['g1'], 'L2_gnn_be1': _L2_gnn_in['be1'], 'L2_gnn_W2': _L2_gnn_in['W2'], 'L2_gnn_b2': _L2_gnn_in['b2'], 'L2_gnn_g2': _L2_gnn_in['g2'], 'L2_gnn_be2': _L2_gnn_in['be2'], 'L3_gnn_W_lin': _L3_gnn_in['W_lin'], 'L3_gnn_W_val': _L3_gnn_in['W_val'], 'L3_gnn_a': _L3_gnn_in['a'], 'L3_gnn_W_out': _L3_gnn_in['W_out'], 'L3_gnn_src': _L3_gnn_in['src'], 'L3_gnn_dst': _L3_gnn_in['dst']}

def reference(x, adj, L0_gnn_alpha_train, L0_gnn_w, L0_gnn_d, L0_gnn_fc_in_w, L0_gnn_fc_in_b, L1_gnn_Wg0, L1_gnn_bg0, L1_gnn_Wg1, L1_gnn_bg1, L1_gnn_Wih, L1_gnn_Whh, L1_gnn_bih, L1_gnn_bhh, L2_gnn_W1, L2_gnn_b1, L2_gnn_g1, L2_gnn_be1, L2_gnn_W2, L2_gnn_b2, L2_gnn_g2, L2_gnn_be2, L3_gnn_W_lin, L3_gnn_W_val, L3_gnn_a, L3_gnn_W_out, L3_gnn_src, L3_gnn_dst):
    import jax
    import jax.numpy as jnp

    def _L0_gnn_ref(x, adj_mx, alpha_train, w, d, fc_in_w, fc_in_b, vt):
        import jax, jax.numpy as jnp
        import numpy as np
        N_STEPS = 8
        SPATIAL_SCALE = 1.0
        x0 = jax.lax.stop_gradient(x)
        h = jnp.einsum('bnd,ed->bne', x, fc_in_w) + fc_in_b
        alph = jax.nn.sigmoid(alpha_train)[:, None]
        d_clamped = jnp.clip(d, 0.0, 1.0)
        w_eff = w * d_clamped @ w.T
        dt = jnp.float32(SPATIAL_SCALE / N_STEPS)

        def euler_step(h, _):
            ax = jnp.einsum('nm,bmd->bnd', adj_mx, h)
            f = alph * 0.5 * (ax - h) + h @ w_eff - h + x0
            return (h + dt * f, None)
        h, _ = jax.lax.scan(euler_step, h, None, length=N_STEPS)
        return h

    def _L1_gnn_ref(x, adj, Wg0, bg0, Wg1, bg1, Wih, Whh, bih, bhh):
        import jax, jax.numpy as jnp
        import numpy as np
        B, T, D, H = (64, 1024, 128, 128)
        MAX_SKIP = 4

        def _lstm_last(Wih, Whh, bih, bhh, xs):
            N, _, Hd = xs.shape
            bias = bih + bhh

            def step(carry, x_t):
                h, c = carry
                g = x_t @ Wih.T + h @ Whh.T + bias
                i, f, gg, o = jnp.split(g, 4, axis=-1)
                c = jax.nn.sigmoid(f) * c + jax.nn.sigmoid(i) * jnp.tanh(gg)
                h = jax.nn.sigmoid(o) * jnp.tanh(c)
                return ((h, c), None)
            init = (jnp.zeros((N, Hd), xs.dtype), jnp.zeros((N, Hd), xs.dtype))
            (h_last, _), _ = jax.lax.scan(step, init, jnp.swapaxes(xs, 0, 1))
            return h_last
        h = jax.nn.relu(jnp.einsum('ts,bsh->bth', adj, x @ Wg0 + bg0))
        h = jax.nn.relu(jnp.einsum('ts,bsh->bth', adj, h @ Wg1 + bg1))
        Bv, Tv, Hd = h.shape
        for p in range(1, MAX_SKIP + 1):
            nw = Tv // p
            wins = h[:, :nw * p, :].reshape(Bv * nw, p, Hd)
            last = _lstm_last(Wih[p - 1], Whh[p - 1], bih[p - 1], bhh[p - 1], wins)
            idx = jnp.arange(nw) * p + (p - 1)
            h = h.at[:, idx, :].set(last.reshape(Bv, nw, Hd))
        return h

    def _L2_gnn_ref(features, A, W1, b1, g1, be1, W2, b2, g2, be2):
        import jax, jax.numpy as jnp
        import numpy as np
        EPS = 1e-05

        def _batchnorm(x, gamma, beta):
            mu = jnp.mean(x, axis=0)
            var = jnp.var(x, axis=0)
            return (x - mu) * jax.lax.rsqrt(var + EPS) * gamma + beta
        b, n, d = features.shape
        A_norm = A + jnp.eye(n, dtype=A.dtype)
        deg = jnp.sum(A_norm, axis=0) + jnp.sum(A_norm, axis=1) - jnp.diagonal(A_norm)
        dinv = jax.lax.rsqrt(deg)
        A_hat = A_norm * dinv[:, None] * dinv[None, :]
        agg = jnp.einsum('nm,bmd->bnd', A_hat, features)
        x = agg.reshape(-1, d)
        h = jax.nn.relu(_batchnorm(x @ W1.T + b1, g1, be1))
        out = h @ W2.T + b2
        out = _batchnorm(out, g2, be2)
        return out.reshape(b, n, -1)

    def _L3_gnn_ref(H, W_lin, W_val, a, W_out, A0, src, dst):
        import jax, jax.numpy as jnp
        import numpy as np
        BT, N, D, HEADS, E = (512, 64, 128, 4, 256)
        LRELU_SLOPE = 0.2
        EPS = 1e-08
        bt, n, d = H.shape
        h, dh = a.shape
        Xq = (H @ W_lin.T).reshape(bt, n, h, dh)
        Xv = (H @ W_val.T).reshape(bt, n, h, dh)
        Qs = Xq[:, src]
        Kt = Xq[:, dst]
        e = jnp.einsum('behd,hd->beh', jax.nn.leaky_relu(Qs + Kt, LRELU_SLOPE), a)
        e = e + jnp.log(A0[src, dst] + EPS)[None, :, None]
        e_t = e.transpose(1, 0, 2)
        m = jax.ops.segment_max(e_t, src, num_segments=n)
        ex = jnp.exp(e_t - m[src])
        denom = jax.ops.segment_sum(ex, src, num_segments=n)
        attn = ex / denom[src]
        Vt = Xv[:, dst].transpose(1, 0, 2, 3)
        Y = jax.ops.segment_sum(attn[..., None] * Vt, src, num_segments=n)
        Y = Y.transpose(1, 0, 2, 3).reshape(bt, n, d)
        return Y @ W_out.T
    x = _layernorm(x + _L0_gnn_ref(x, adj, L0_gnn_alpha_train, L0_gnn_w, L0_gnn_d, L0_gnn_fc_in_w, L0_gnn_fc_in_b, 0), axis=-1)
    x = _layernorm(x + _L1_gnn_ref(x, adj, L1_gnn_Wg0, L1_gnn_bg0, L1_gnn_Wg1, L1_gnn_bg1, L1_gnn_Wih, L1_gnn_Whh, L1_gnn_bih, L1_gnn_bhh), axis=-1)
    x = _layernorm(x + _L2_gnn_ref(x, adj, L2_gnn_W1, L2_gnn_b1, L2_gnn_g1, L2_gnn_be1, L2_gnn_W2, L2_gnn_b2, L2_gnn_g2, L2_gnn_be2), axis=-1)
    x = _layernorm(x + _L3_gnn_ref(x, L3_gnn_W_lin, L3_gnn_W_val, L3_gnn_a, L3_gnn_W_out, adj, L3_gnn_src, L3_gnn_dst), axis=-1)
    return x

_drawn_inputs = setup_inputs


def setup_inputs(seed=0):
    import zlib

    import numpy as np

    out = dict(_drawn_inputs(seed))
    spreads = {'L0_gnn_alpha_train': (1.0, 0.6),
     'L0_gnn_fc_in_b': (0.0, 0.376),
     'L1_gnn_bg0': (0.0, 0.8),
     'L1_gnn_bg1': (0.0, 0.8),
     'L2_gnn_b1': (0.0, 0.8),
     'L2_gnn_g1': (1.0, 0.2),
     'L2_gnn_be1': (0.0, 0.1),
     'L2_gnn_b2': (0.0, 0.8),
     'L2_gnn_g2': (1.0, 0.2),
     'L2_gnn_be2': (0.0, 0.1)}
    factors = {'L1_gnn_Wg0': 8.0,
     'L1_gnn_Wg1': 8.0,
     'L1_gnn_Wih': 8.0,
     'L1_gnn_Whh': 8.0,
     'L1_gnn_bhh': 2.689}
    for name, (base, spread) in spreads.items():
        noise = np.random.default_rng([zlib.crc32(name.encode()), seed]).standard_normal(out[name].shape)
        drawn = base * np.exp(spread * noise) if base else spread * noise
        out[name] = jnp.asarray(drawn.astype(out[name].dtype))
    for name, factor in factors.items():
        out[name] = (out[name] * factor).astype(out[name].dtype)
    return out
```

```python
import math
from contextlib import ExitStack

import concourse.bass as bass
from concourse import mybir

ALU = mybir.AluOpType
ACT = mybir.ActivationFunctionType
AX = mybir.AxisListType
F32 = mybir.dt.float32
F32R = mybir.dt.float32r
I32 = mybir.dt.int32

P = 128
EPS = 1e-5
N_STEPS = 8
DT = 1.0 / N_STEPS
BABY = 3
NCO = N_STEPS + 1
MAX_SKIP = 4
QB = 4
LOWEST = -3.0e38


def binom(n, k):
    return float(math.comb(n, k))


class Shared:
    pass


def wait(eng, sem, value):
    if not isinstance(value, int) or value > 0:
        eng.wait_ge(sem, value)


def peeled(eng, n, step):
    step(0, n == 1)
    if n > 2:
        with eng.Fori(1, n - 1) as i:
            step(i, False)
    if n > 1:
        step(n - 1, True)


def product(pe, out, lhs, rhs, start=True, stop=True):
    pe.matmul(out, lhs[0], rhs[0], start=start, stop=False)
    pe.matmul(out, lhs[0], rhs[1], start=False, stop=False)
    return pe.matmul(out, lhs[1], rhs[0], start=False, stop=stop)


def low_part(eng, out, full, high):
    return eng.tensor_tensor(out, full, high.bitcast(F32), ALU.subtract)


def allocators(nc, ctx):
    def sb(name, shape, dt=F32):
        return ctx.enter_context(nc.sbuf_tensor(name, shape, dt))

    def sem(name):
        return ctx.enter_context(nc.semaphore(name))

    return sb, sem


def phase_operators(nc, sh, d):
    C, D, N = sh.C, sh.D, sh.N
    with ExitStack() as ctx:
        sb, sem = allocators(nc, ctx)
        w_nat = sb("w_nat", [P, D])
        wT = sb("wT", [P, D])
        wTd = sb("wTd", [P, D])
        fcw = sb("fcw", [P, D])
        dcol = sb("dcol", [P, 1])
        dclip = sb("dclip", [P, 1])
        bcol = sb("bcol", [P, 1])
        alpha = sb("alpha", [P, C])
        gate = sb("gate", [P, C])
        kappa = sb("kappa", [P, C])
        ldiag = sb("ldiag", [P, C])
        L = sb("L", [P, C, N])
        Lh = sb("Lh", [P, C, N], F32R)
        Ll = sb("Ll", [P, C, N], F32R)
        RP = sb("RP", [P, NCO, D])
        Ef = sb("Ef", [P, NCO, D])
        bsel = sb("bsel", [P, NCO, NCO])
        V = sb("V", [NCO, D])
        U = sb("U", [P, C, NCO])
        UT = sb("UT", [NCO, C, P])
        names = ("w_in", "fc_in", "a_in", "small_in", "x_in", "idn", "memsets", "pe_tile", "dve_tile",
                 "hi_done", "gate_done", "l_done", "lh_done", "ll_done", "own", "bsel_done", "eh_done", "e_done")
        S = {n: sem(n) for n in names}

        order = (["wT"] + ["R"] + [f"LT{j}" for j in range(C)] + ["R2", "R34", "R58", "FR03", "FR47", "FR8V"]
                 + [f"L2T{j}" for j in range(C)] + [f"L3T{j}" for j in range(C)]
                 + ["U13", "U46", "U78", "UT", "BIAS"])
        at = {n: i for i, n in enumerate(order)}
        his = [f"LT{j}" for j in range(C)] + [f"L2T{j}" for j in range(C)] + [f"L3T{j}" for j in range(C)]

        def bank(name):
            return sh.psum[:, at[name] % 8, :]

        block = ctx.enter_context(nc.Block())

        @block.sync
        def _(sp):
            sp.dma_start(w_nat[:, :], d["L0_gnn_w"]).then_inc(S["w_in"], 16)
            sp.dma_start(sh.A[:, :, :], d["adj"].rearrange("(c p) m -> p c m", p=P)).then_inc(S["a_in"], 16)
            xv = d["x"].rearrange("b (c p) d -> p c b d", p=P)
            for q in range(sh.NB // QB):
                for c in range(C):
                    sp.dma_start(sh.X[:, c, q * QB:(q + 1) * QB, :], xv[:, c, q * QB:(q + 1) * QB, :])\
                        .then_inc(S["x_in"], 16)
            sp.wait_ge(S["x_in"], 16 * C * (sh.NB // QB))

        @block.gpsimd
        def _(pool):
            pool.memset(sh.ident[:, :], 0.0).then_inc(S["memsets"], 1)
            pool.memset(bsel[:, :, :], 0.0).then_inc(S["memsets"], 1)
            pool.memset(U[:, :, 0:1], 1.0).then_inc(S["memsets"], 1)
            pool.wait_ge(S["memsets"], 1)
            pool.affine_select(out=sh.ident[:, :], in_=sh.ident[:, :], compare_op=ALU.not_equal, fill=1.0,
                               base=0, pattern=[[-1, P]], channel_multiplier=1).then_inc(S["idn"], 1)
            for k, value in enumerate(sh.const_values):
                pool.memset(sh.const[:, k, :], value).then_inc(S["memsets"], 1)

        @block.scalar
        def _(act):
            act.dma_start(alpha[:, :], d["L0_gnn_alpha_train"].rearrange("(c p) -> p c", p=P))\
                .then_inc(S["small_in"], 16)
            act.dma_start(dcol[:, :], d["L0_gnn_d"].rearrange("(p o) -> p o", o=1)).then_inc(S["small_in"], 16)
            act.dma_start(bcol[:, :], d["L0_gnn_fc_in_b"].rearrange("(p o) -> p o", o=1))\
                .then_inc(S["small_in"], 16)
            act.dma_start(fcw[:, :], d["L0_gnn_fc_in_w"]).then_inc(S["fc_in"], 16)
            act.wait_ge(S["small_in"], 48)
            act.activation(gate[:, :], alpha[:, :], ACT.Sigmoid).then_inc(S["gate_done"], 1)
            for c in range(C):
                act.wait_ge(S["l_done"], c + 1)
                act.activation(Lh[:, c, :], L[:, c, :], ACT.Copy).then_inc(S["lh_done"], 1)
            for k, name in enumerate(his):
                act.wait_ge(S["pe_tile"], at[name] + 1)
                act.activation(sh.LT[k // C][0][:, k % C, :], bank(name), ACT.Copy).then_inc(S["hi_done"], 1)
                if name == f"L2T{C - 1}":
                    act.wait_ge(S["e_done"], 1)
                    act.activation(sh.E[0][:, :, :, :], Ef[:, :, :].rearrange("p (i r) d -> p r i d", r=BABY),
                                   ACT.Copy).then_inc(S["eh_done"], 1)

        @block.vector
        def _(dve):
            chain = [0]

            def link(ins):
                chain[0] += 1
                ins.then_inc(S["own"], 1)
                dve.wait_ge(S["own"], chain[0])

            def tile(name):
                dve.wait_ge(S["pe_tile"], at[name] + 1)

            dve.wait_ge(S["gate_done"], 1)
            link(dve.tensor_scalar(kappa[:, :], gate[:, :], 0.5 * DT, None, ALU.mult))
            dve.tensor_scalar(dclip[:, :], dcol[:, :], 0.0, 1.0, ALU.max, ALU.min)
            link(dve.tensor_scalar(ldiag[:, :], kappa[:, :], -1.0, 1.0 - DT, ALU.mult, ALU.add))
            tile("wT")
            link(dve.tensor_copy(wT[:, :], bank("wT")[:, 0:D]))
            dve.tensor_scalar(wTd[:, :], wT[:, :], dclip[:, 0:1], DT, ALU.mult, ALU.mult)\
                .then_inc(S["dve_tile"], 1)
            dve.wait_ge(S["a_in"], 16)
            dve.wait_ge(S["idn"], 1)
            for c in range(C):
                link(dve.tensor_scalar(L[:, c, :], sh.A[:, c, :], kappa[:, c:c + 1], None, ALU.mult))
                own = L[:, c, c * P:(c + 1) * P]
                dve.scalar_tensor_tensor(own, sh.ident[:, :], ldiag[:, c:c + 1], own, ALU.mult, ALU.add)\
                    .then_inc(S["l_done"], 1)
            for c in range(C):
                dve.wait_ge(S["lh_done"], c + 1)
                low_part(dve, Ll[:, c, :], L[:, c, :], Lh[:, c, :]).then_inc(S["ll_done"], 1)
            tile("R")
            dve.tensor_copy(RP[:, 0, :], sh.ident[:, :])
            dve.tensor_copy(RP[:, 1, :], bank("R")[:, 0:D]).then_inc(S["dve_tile"], 1)

            def split(k, name):
                dve.wait_ge(S["hi_done"], k + 1)
                low_part(dve, sh.LT[k // C][1][:, k % C, :], bank(name), sh.LT[k // C][0][:, k % C, :])\
                    .then_inc(S["dve_tile"], 1)

            for k in range(C):
                split(k, his[k])
            tile("R2")
            dve.tensor_copy(RP[:, 2, :], bank("R2")[:, 0:D]).then_inc(S["dve_tile"], 1)
            tile("R34")
            dve.tensor_copy(RP[:, 3:5, :], bank("R34")[:, 0:2 * D].rearrange("p (k d) -> p k d", d=D))\
                .then_inc(S["dve_tile"], 1)
            tile("R58")
            dve.tensor_copy(RP[:, 5:9, :], bank("R58").rearrange("p (k d) -> p k d", d=D))\
                .then_inc(S["dve_tile"], 1)
            dve.wait_ge(S["memsets"], 3)
            for j in range(NCO):
                ins = dve.tensor_scalar(bsel[:, j, j:j + 1], bcol[:, 0:1], binom(N_STEPS, j), None, ALU.mult)
            ins.then_inc(S["bsel_done"], 1)
            for name, k0, n in (("FR03", 0, 4), ("FR47", 4, 4), ("FR8V", 8, 1)):
                tile(name)
                for k in range(n):
                    j = N_STEPS - k0 - k
                    ins = dve.tensor_scalar(Ef[:, j, :], bank(name)[:, k * D:(k + 1) * D], binom(N_STEPS, j),
                                            None, ALU.mult)
                if name == "FR8V":
                    ins = dve.tensor_copy(V[:, :], bank(name)[0:NCO, D:2 * D])
                ins.then_inc(S["dve_tile"], 1)
                chain_base = at[name] + 1
            dve.wait_ge(S["dve_tile"], chain_base)
            for i in range(N_STEPS):
                for j in range(N_STEPS - i):
                    ins = dve.scalar_tensor_tensor(Ef[:, j, :], RP[:, i, :], DT * binom(i + j, j), Ef[:, j, :],
                                                   ALU.mult, ALU.add)
                if i < N_STEPS - 1:
                    link(ins)
            ins.then_inc(S["e_done"], 1)
            for k in range(C, 2 * C):
                split(k, his[k])
            dve.wait_ge(S["eh_done"], 1)
            low_part(dve, sh.E[1][:, :, :, :], Ef[:, :, :].rearrange("p (i r) d -> p r i d", r=BABY),
                     sh.E[0][:, :, :, :])
            for k in range(2 * C, 3 * C):
                split(k, his[k])
            tile("U13")
            dve.tensor_copy(U[:, :, 1:4], bank("U13")[:, 0:3 * C].rearrange("p (c j) -> p c j", j=3))\
                .then_inc(S["dve_tile"], 1)
            tile("U46")
            dve.tensor_copy(U[:, :, 4:7], bank("U46")[:, 0:3 * C].rearrange("p (c j) -> p c j", j=3))\
                .then_inc(S["dve_tile"], 1)
            tile("U78")
            dve.tensor_copy(U[:, :, 7:9], bank("U78")[:, 0:2 * C].rearrange("p (c j) -> p c j", j=2))\
                .then_inc(S["dve_tile"], 1)
            tile("UT")
            dve.tensor_copy(UT[:, :, :], bank("UT")[0:NCO, :].rearrange("p (c n) -> p c n", n=P))\
                .then_inc(S["dve_tile"], 1)
            tile("BIAS")
            dve.tensor_copy(sh.bias0[:, :, :], bank("BIAS").rearrange("p (c d) -> p c d", d=D))\
                .then_inc(S["dve_tile"], 1)

        @block.tensor
        def _(pe):
            def begin(name, needs=()):
                upto = max([at[name] - 7] + [at[n] + 1 for n in needs])
                if upto > 0:
                    pe.wait_ge(S["dve_tile"], upto)

            def done(ins):
                ins.then_inc(S["pe_tile"], 1)

            pe.wait_ge(S["w_in"], 16)
            pe.wait_ge(S["idn"], 1)
            done(pe.transpose(bank("wT")[:, 0:D], w_nat[:, :], sh.ident[:, :]))
            begin("R", ["wT"])
            done(pe.matmul(bank("R")[:, 0:D], wTd[:, :], wT[:, :], start=True, stop=True))
            pe.wait_ge(S["l_done"], C)
            for j in range(C):
                for c in range(C):
                    ins = pe.transpose(bank(f"LT{j}")[:, c * P:(c + 1) * P], L[:, c, j * P:(j + 1) * P],
                                       sh.ident[:, :])
                done(ins)
            begin("R2", ["R"])
            done(pe.matmul(bank("R2")[:, 0:D], RP[:, 1, :], RP[:, 1, :], start=True, stop=True))
            begin("R34", ["R2"])
            done(pe.matmul(bank("R34")[:, 0:2 * D], RP[:, 2, :], RP[:, 1:3, :], start=True, stop=True))
            begin("R58", ["R34"])
            done(pe.matmul(bank("R58"), RP[:, 4, :], RP[:, 1:5, :], start=True, stop=True))
            begin("FR03", ["R58"])
            pe.wait_ge(S["fc_in"], 16)
            done(pe.matmul(bank("FR03"), fcw[:, :], RP[:, 0:4, :], start=True, stop=True))
            begin("FR47")
            done(pe.matmul(bank("FR47"), fcw[:, :], RP[:, 4:8, :], start=True, stop=True))
            begin("FR8V")
            pe.matmul(bank("FR8V")[:, 0:D], fcw[:, :], RP[:, 8, :], start=True, stop=True)
            pe.wait_ge(S["bsel_done"], 1)
            for j in range(NCO):
                ins = pe.matmul(bank("FR8V")[0:NCO, D:2 * D], bsel[:, j, :], RP[:, N_STEPS - j, :],
                                start=(j == 0), stop=(j == NCO - 1))
            done(ins)
            pe.wait_ge(S["ll_done"], C)
            for r in (2, 3):
                for j in range(C):
                    begin(f"L{r}T{j}", [f"LT{C - 1}" if r == 2 else f"L2T{C - 1}"])
                    for k in range(C):
                        rows = slice(j * P, (j + 1) * P)
                        ins = product(pe, bank(f"L{r}T{j}"), (Lh[:, k, rows], Ll[:, k, rows]),
                                      (sh.LT[r - 2][0][:, k, :], sh.LT[r - 2][1][:, k, :]),
                                      start=(k == 0), stop=(k == C - 1))
                    done(ins)

            def powers(name, lts, u, n):
                for c2 in range(C):
                    for r, (hi, lo) in enumerate(lts):
                        for k in range(C):
                            o = bank(name)[:, c2 * len(lts) * n + r * n:c2 * len(lts) * n + (r + 1) * n]
                            cols = slice(c2 * P, (c2 + 1) * P)
                            pe.matmul(o, hi[:, k, cols].bitcast(F32), U[:, k, u:u + n], start=(k == 0),
                                      stop=False)
                            ins = pe.matmul(o, lo[:, k, cols].bitcast(F32), U[:, k, u:u + n], start=False,
                                            stop=(k == C - 1))
                done(ins)

            begin("U13", [f"L3T{C - 1}"])
            powers("U13", sh.LT, 0, 1)
            begin("U46", ["U13"])
            powers("U46", sh.LT[2:], 1, 3)
            begin("U78", ["U46"])
            powers("U78", sh.LT[2:], 4, 2)
            begin("UT", ["U78"])
            for c in range(C):
                ins = pe.transpose(bank("UT")[0:NCO, c * P:(c + 1) * P], U[:, c, :], sh.ident[:, :])
            done(ins)
            begin("BIAS", ["UT"])
            for c in range(C):
                ins = pe.matmul(bank("BIAS")[:, c * D:(c + 1) * D], UT[:, c, :], V[:, :], start=True, stop=True)
            done(ins)


def norm_stats(dve, stats, rows):
    for b in range(rows.shape[1]):
        ins = dve.bn_stats(stats[:, b, :], rows[:, b, :])
    return ins


NORM_LINKS = 5


def norm_scales(pool, sh, n, stats, work, mean, rstd, own, before):
    a, b, c = (work[:, k, 0:n] for k in range(3))

    def const(k):
        return sh.const[:, k, 0:n]

    def link(k, ins):
        ins.then_inc(own, 1)
        pool.wait_ge(own, before + k)

    pool.tensor_tensor(a, stats[:, :, 1], stats[:, :, 4], ALU.add)
    pool.tensor_tensor(b, stats[:, :, 1], stats[:, :, 4], ALU.subtract)
    link(1, pool.tensor_tensor(c, stats[:, :, 2], stats[:, :, 5], ALU.add))
    pool.tensor_tensor(mean, a, const(sh.HALF), ALU.mult)
    pool.tensor_tensor(c, c, const(sh.PER_D), ALU.mult)
    link(2, pool.tensor_tensor(b, b, b, ALU.mult))
    link(3, pool.tensor_tensor(b, b, const(sh.QUARTER), ALU.mult))
    link(4, pool.tensor_tensor(b, b, c, ALU.add))
    link(5, pool.tensor_tensor(b, b, const(sh.EPS), ALU.add))
    return pool.tensor_tensor(rstd, b, const(sh.ROOT), ALU.pow)


def phase_diffusion(nc, sh, d):
    C, D, N = sh.C, sh.D, sh.N
    NQ = sh.NB // QB
    with ExitStack() as ctx:
        sb, sem = allocators(nc, ctx)
        Xh = sb("Xh", [P, C, QB, D], F32R)
        Xl = sb("Xl", [P, C, QB, D], F32R)
        yh = sb("yh", [P, 2, BABY, N], F32R)
        yl = sb("yl", [P, 2, BABY, N], F32R)
        B2h = sb("B2h", [P, C, QB, D], F32R)
        B2l = sb("B2l", [P, C, QB, D], F32R)
        B01 = sb("B01", [P, C, QB, 2, D])
        tq = sb("tq", [P, C, QB, D])
        th = sb("th", [P, C, QB, D], F32R)
        tl = sb("tl", [P, C, QB, D], F32R)
        stats = sb("stats", [P, C * QB, 6])
        work3 = sb("work3", [P, 3, C * QB])
        mean = sb("mean", [P, C * QB])
        rstd = sb("rstd", [P, C * QB])
        names = ("pe_tile", "dve_tile", "hi_done", "xh_done", "xl_done", "xb_done", "th_done", "tl_done",
                 "sum2", "stat_done", "norm_own", "rstd_done", "x1_done")
        S = {n: sem("d_" + n) for n in names}

        work = [("B", 0), ("Y", 2), ("B", 1), ("Y", 3), ("B", 2), ("B", 3), ("Y+", 0), ("T", 0), ("Y+", 1),
                ("S", 0)]
        TILES = 4 * len(work)
        HEAD = 8
        HIS = {"Y": 3, "Y+": 3, "B": 4, "T": 0, "S": 0}
        HI_QUAD = sum(HIS[k] for k, _ in work)
        HI_HEAD = 6

        def steps(g, last):
            hi = 0
            for i, (kind, b) in enumerate(work):
                if not (last and kind == "Y+"):
                    skipped = sum(k == "Y+" for k, _ in work[:i]) if last else 0
                    yield kind, b, HEAD + g * TILES + 4 * (i - skipped), 4 * (i - skipped) % 8, \
                        HI_HEAD + g * HI_QUAD + hi
                    hi += HIS[kind]

        block = ctx.enter_context(nc.Block())

        def ready(eng, n, k):
            eng.wait_ge(S["pe_tile"], n + k + 1)

        @block.tensor
        def _(pe):
            def free(n, k, first=False):
                if not first:
                    pe.wait_ge(S["dve_tile"], n + k - 7)

            def Y(b, n, bk, first=False):
                for k in range(4):
                    free(n, k, first)
                    o = sh.psum[:, bk + k, :]
                    if k < 2:
                        src = (Xh, Xl)[k]
                        for c in range(C):
                            ins = pe.transpose(o[:, c * P:(c + 1) * P], src[:, c, b, :].bitcast(F32),
                                               sh.ident[:, :])
                    else:
                        for c in range(C):
                            ins = product(pe, o, (Xh[:, c, b, :], Xl[:, c, b, :]),
                                          (sh.LT[k - 2][0][:, c, :], sh.LT[k - 2][1][:, c, :]),
                                          start=(c == 0), stop=(c == C - 1))
                    ins.then_inc(S["pe_tile"], 1)

            def B(b, n, bk, y_end):
                pe.wait_ge(S["dve_tile"], y_end)
                for c in range(C):
                    free(n, c)
                    cols = slice(c * P, (c + 1) * P)
                    for r in range(BABY):
                        ins = product(pe, sh.psum[:, bk + c, 0:BABY * D],
                                      (yh[:, b % 2, r, cols], yl[:, b % 2, r, cols]),
                                      (sh.E[0][:, r, :, :], sh.E[1][:, r, :, :]),
                                      start=(r == 0), stop=(r == BABY - 1))
                    ins.then_inc(S["pe_tile"], 1)

            def horner(n, bk, hi, lo):
                for c2 in range(C):
                    free(n, c2)
                    cols = slice(c2 * P, (c2 + 1) * P)
                    for c in range(C):
                        ins = product(pe, sh.psum[:, bk + c2, :],
                                      (sh.LT[2][0][:, c, cols], sh.LT[2][1][:, c, cols]),
                                      (hi[:, c, :, :], lo[:, c, :, :]), start=(c == 0), stop=(c == C - 1))
                    ins.then_inc(S["pe_tile"], 1)

            def quad(g, last):
                start = HEAD + g * TILES
                y_end = {0: start - 4, 1: start}
                for kind, b, n, bk, _ in steps(g, last):
                    if kind in ("Y", "Y+"):
                        if kind == "Y+" and b == 0:
                            pe.wait_ge(S["xl_done"], C * (g + 2))
                        Y(b, n, bk)
                        y_end[b] = n + 4
                    elif kind == "B":
                        B(b, n, bk, y_end[b])
                        b_end = n + 4
                    elif kind == "T":
                        pe.wait_ge(S["dve_tile"], b_end)
                        horner(n, bk, B2h, B2l)
                    else:
                        pe.wait_ge(S["tl_done"], C * (g + 1))
                        horner(n, bk, th, tl)

            pe.wait_ge(S["xl_done"], C)
            Y(0, 0, 0, first=True)
            Y(1, 4, 4, first=True)
            with pe.Fori(0, NQ - 1) as g:
                quad(g, False)
            quad(NQ - 1, True)

        @block.scalar
        def _(act):
            def split_x(g):
                for c in range(C):
                    act.activation(Xh[:, c, :, :], sh.X[:, c, bass.ds(QB * g, QB), :], ACT.Copy)\
                        .then_inc(S["xh_done"], 1)

            def Y(b, n, bk):
                for k, r in ((0, 0), (2, 1), (3, 2)):
                    ready(act, n, k)
                    act.activation(yh[:, b % 2, r, :], sh.psum[:, bk + k, :], ACT.Copy)\
                        .then_inc(S["hi_done"], 1)

            def quad(g, last):
                for kind, b, n, bk, _ in steps(g, last):
                    if kind in ("Y", "Y+"):
                        Y(b, n, bk)
                        if kind == "Y" and b == QB - 1 and not last:
                            split_x(g + 1)
                    elif kind == "B":
                        if b == 0:
                            act.wait_ge(S["dve_tile"], n)
                        for c in range(C):
                            ready(act, n, c)
                            act.activation(B2h[:, c, b, :], sh.psum[:, bk + c, 2 * D:3 * D], ACT.Copy)
                            act.activation(B01[:, c, b, :, :],
                                           sh.psum[:, bk + c, 0:2 * D].rearrange("p (i d) -> p i d", d=D),
                                           ACT.Copy).then_inc(S["hi_done"], 1)
                    elif kind == "T":
                        for c in range(C):
                            act.wait_ge(S["dve_tile"], n + c + 1)
                            act.activation(th[:, c, :, :], tq[:, c, :, :], ACT.Copy).then_inc(S["th_done"], 1)

            split_x(0)
            Y(0, 0, 0)
            Y(1, 4, 4)
            with act.Fori(0, NQ - 1) as g:
                quad(g, False)
            quad(NQ - 1, True)

        @block.vector
        def _(dve):
            def Y(b, n, bk, hi):
                dve.wait_ge(S["hi_done"], hi + 1)
                ready(dve, n, 1)
                dve.tensor_copy(yl[:, b % 2, 0, :], sh.psum[:, bk + 1, :]).then_inc(S["dve_tile"], 2)
                for k in (2, 3):
                    dve.wait_ge(S["hi_done"], hi + k)
                    low_part(dve, yl[:, b % 2, k - 1, :], sh.psum[:, bk + k, :], yh[:, b % 2, k - 1, :])\
                        .then_inc(S["dve_tile"], 1)

            def quad(g, last):
                for kind, b, n, bk, hi in steps(g, last):
                    if kind in ("Y", "Y+"):
                        Y(b, n, bk, hi)
                    elif kind == "B":
                        for c in range(C):
                            dve.wait_ge(S["hi_done"], hi + c + 1)
                            low_part(dve, B2l[:, c, b, :], sh.psum[:, bk + c, 2 * D:3 * D], B2h[:, c, b, :])\
                                .then_inc(S["dve_tile"], 1)
                    elif kind == "T":
                        for c in range(C):
                            ready(dve, n, c)
                            dve.tensor_tensor(tq[:, c, :, :],
                                              sh.psum[:, bk + c, :].rearrange("p (b d) -> p b d", d=D),
                                              B01[:, c, :, 1, :], ALU.add).then_inc(S["dve_tile"], 1)
                    else:
                        for c in range(C):
                            ready(dve, n, c)
                            dve.tensor_tensor(tq[:, c, :, :],
                                              sh.psum[:, bk + c, :].rearrange("p (b d) -> p b d", d=D),
                                              B01[:, c, :, 0, :], ALU.add).then_inc(S["dve_tile"], 1)
                            if c == 0:
                                dve.wait_ge(S["xb_done"], C * (g + 1))
                            dve.wait_ge(S["dve_tile"], n + c + 1)
                            dve.tensor_tensor(tq[:, c, :, :], tq[:, c, :, :],
                                              sh.X[:, c, bass.ds(QB * g, QB), :], ALU.add)\
                                .then_inc(S["sum2"], 1)
                            dve.wait_ge(S["sum2"], C * g + c + 1)
                            norm_stats(dve, stats[:, c * QB:(c + 1) * QB, :], tq[:, c, :, :])\
                                .then_inc(S["stat_done"], 1)
                        dve.wait_ge(S["rstd_done"], g + 1)
                        for c in range(C):
                            for b in range(QB):
                                ins = dve.tensor_scalar(sh.X[:, c, bass.ds(QB * g + b, 1), :],
                                                        tq[:, c, b:b + 1, :], mean[:, c * QB + b:c * QB + b + 1],
                                                        rstd[:, c * QB + b:c * QB + b + 1], ALU.subtract,
                                                        ALU.mult)
                        ins.then_inc(S["x1_done"], 1)

            Y(0, 0, 0, 0)
            Y(1, 4, 4, 3)
            with dve.Fori(0, NQ - 1) as g:
                quad(g, False)
            quad(NQ - 1, True)

        @block.gpsimd
        def _(pool):
            def split_x(g):
                for c in range(C):
                    pool.wait_ge(S["xh_done"], C * g + c + 1)
                    low_part(pool, Xl[:, c, :, :], sh.X[:, c, bass.ds(QB * g, QB), :], Xh[:, c, :, :])\
                        .then_inc(S["xl_done"], 1)

            def quad(g, last):
                pool.wait_ge(S["xl_done"], C * (g + 1))
                for c in range(C):
                    xq = sh.X[:, c, bass.ds(QB * g, QB), :]
                    pool.tensor_tensor(xq, xq, sh.bias0[:, c:c + 1, :].broadcast_to([P, QB, D]), ALU.add)\
                        .then_inc(S["xb_done"], 1)
                if not last:
                    split_x(g + 1)
                for c in range(C):
                    pool.wait_ge(S["th_done"], C * g + c + 1)
                    low_part(pool, tl[:, c, :, :], tq[:, c, :, :], th[:, c, :, :]).then_inc(S["tl_done"], 1)
                pool.wait_ge(S["stat_done"], C * (g + 1))
                norm_scales(pool, sh, C * QB, stats, work3, mean[:, :], rstd[:, :], S["norm_own"],
                            NORM_LINKS * g).then_inc(S["rstd_done"], 1)

            split_x(0)
            with pool.Fori(0, NQ - 1) as g:
                quad(g, False)
            quad(NQ - 1, True)


def phase_recurrent(nc, sh, d):
    C, D, N = sh.C, sh.D, sh.N
    NQ = sh.NB // QB
    I, F, G, O = range(4)
    with ExitStack() as ctx:
        sb, sem = allocators(nc, ctx)
        AT = (sb("ATh", [P, C, N], F32R), sb("ATl", [P, C, N], F32R))
        ATh, ATl = AT
        Wg = [sb(f"Wg{i}", [P, D]) for i in (0, 1)]
        Wgs = [(sb(f"Wg{i}h", [P, D], F32R), sb(f"Wg{i}l", [P, D], F32R)) for i in (0, 1)]
        bg0 = sb("bg0", [P, D])
        bg1 = sb("bg1", [P, 1])
        WI = (sb("WIh", [P, MAX_SKIP, 4, D], F32R), sb("WIl", [P, MAX_SKIP, 4, D], F32R))
        WH = (sb("WHh", [P, MAX_SKIP - 1, 4, D], F32R), sb("WHl", [P, MAX_SKIP - 1, 4, D], F32R))
        bi = sb("bi", [P, MAX_SKIP, 4])
        bh = sb("bh", [P, MAX_SKIP, 4])
        gbias = sb("gbias", [P, MAX_SKIP, 4])
        ones = sb("ones", [P, P])
        rs = sb("rs", [P, C])
        diag = sb("diag", [P, C, P])
        RB0 = sb("RB0", [P, C, D])
        RB1 = sb("RB1", [P, N])
        Xh = sb("rXh", [P, C, QB, D], F32R)
        Xl = sb("rXl", [P, C, QB, D], F32R)
        ych = sb("ych", [P, 2, N], F32R)
        ycl = sb("ycl", [P, 2, N], F32R)
        u = sb("u", [P, 2, C, D])
        h1h = sb("h1h", [P, C, QB, D], F32R)
        h1l = sb("h1l", [P, C, QB, D], F32R)
        Hin = sb("Hin", [P, QB, N])
        Hq = sb("Hq", [P, QB, N])
        xh = sb("xh", [P, 2, N], F32R)
        xl = sb("xl", [P, 2, N], F32R)
        hh = sb("hh", [P, 2, N], F32R)
        hl = sb("hl", [P, 2, N], F32R)
        cell = sb("cell", [P, 2, N])
        gates = sb("gates", [P, 4, N])
        tc = sb("tc", [P, N])
        hn = sb("hn", [P, N])
        sq = sb("sq", [P, QB, C, D])
        stats = sb("rstats", [P, QB * C, 6])
        work3 = sb("rwork3", [P, 3, QB * C])
        mean = sb("rmean", [P, QB * C])
        rstd = sb("rrstd", [P, QB * C])
        names = ("w_in", "g_in", "ones_done", "set_mm", "set_free", "set_hi", "own", "gbias_done", "wg_hi", "wg_done", "rb_done",
                 "xh_done", "xl_done", "ring_mm", "ring_free", "conv_hi", "relu_done", "h1l_done",
                 "hq_done", "xs_done", "x_hi", "hs_done", "c_own", "c_own2", "c_done", "tanh_done", "h_done",
                 "stat_done", "norm_own", "rstd_done", "x2_done")
        S = {n: sem("r_" + n) for n in names}
        gate_mm = [sem(f"gate_mm_{n}") for n in "ifgo"]
        gate_act = [sem(f"gate_act_{n}") for n in "ifgo"]

        steps = [(1, 0, u_) for u_ in range(QB)]
        for p_ in range(2, MAX_SKIP + 1):
            steps += [(p_, t, s) for t in range(p_) for s in (0, 1)]
        NS = len(steps)
        NF = sum(t > 0 for _, t, _ in steps)

        def view(p_, t, s):
            if p_ == 1:
                return Hq[:, s, :], N
            nw = N // p_
            return Hq[:, 2 * s:2 * s + 2, t:t + (nw - 1) * p_ + 1:p_], 2 * nw

        def like(ap, p_, n):
            return ap[..., 0:n] if p_ == 1 else ap[..., 0:n].rearrange("p (b w) -> p b w", b=2)

        def gates_of(t):
            return (G, I, O) if t == 0 else (G, I, F, O)

        def uses(k, gate):
            return sum(gate in gates_of(t) for _, t, _ in steps[:k])

        conv = [("Y0", 0), ("Y0", 1), ("W0", 0), ("Y0", 2), ("low", 0), ("W0", 1), ("Y0", 3), ("low", 1),
                ("W0", 2), ("Y1", 0), ("low", 2), ("W0", 3), ("Y1", 1), ("low", 3), ("W1", 0), ("Y1", 2),
                ("W1", 1), ("Y1", 3), ("W1", 2), ("W1", 3)]
        resid = [("R", b) for b in range(QB)]
        CONV, RESID = 4 * QB, QB

        TAIL = 3

        def mixed(with_conv, norm_before):
            left = list(conv) if with_conv else []
            for k in range(NS):
                yield ("L", k)
                if norm_before and k in (1, 4):
                    yield ("stats" if k == 1 else "norm", 0)
                if len(left) > TAIL:
                    yield left.pop(0)
            yield from resid
            yield from left

        NO_TILE = ("L", "low", "stats", "norm")

        def numbered(items, base):
            n = 0
            for kind, b in items:
                yield kind, b, base + n, 4 + n % 4
                n += kind not in NO_TILE

        HS = sum(t < p_ - 1 for p_, t, _ in steps)

        def hs_before(k):
            return sum(t < p_ - 1 for p_, t, _ in steps[:k])

        def ring_base(g):
            return CONV + g * (CONV + RESID)

        def sq_end(g):
            return ring_base(g) + RESID + (0 if isinstance(g, int) and g == NQ - 1 else CONV - TAIL)

        block = ctx.enter_context(nc.Block())

        @block.sync
        def _(sp):
            sp.dma_start(Hq[:, :, :].rearrange("p k (g h) -> p k g h", g=4),
                         d["L1_gnn_Wih"].rearrange("k (g p) h -> p k g h", p=P)).then_inc(S["w_in"], 16)
            sp.dma_start(Hin[:, 0:MAX_SKIP - 1, :].rearrange("p k (g h) -> p k g h", g=4),
                         d["L1_gnn_Whh"][1:MAX_SKIP].rearrange("k (g p) h -> p k g h", p=P))\
                .then_inc(S["w_in"], 16)
            for i in (0, 1):
                sp.dma_start(Wg[i][:, :], d[f"L1_gnn_Wg{i}"]).then_inc(S["g_in"], 16)
            sp.dma_start(bg0[:, :], d["L1_gnn_bg0"].rearrange("(o h) -> o h", o=1).broadcast_to([P, D]))\
                .then_inc(S["g_in"], 16)
            sp.dma_start(bg1[:, :], d["L1_gnn_bg1"].rearrange("(h o) -> h o", o=1)).then_inc(S["g_in"], 16)
            sp.dma_start(bi[:, :, :], d["L1_gnn_bih"].rearrange("k (g p) -> p k g", p=P)).then_inc(S["g_in"], 16)
            sp.dma_start(bh[:, :, :], d["L1_gnn_bhh"].rearrange("k (g p) -> p k g", p=P)).then_inc(S["g_in"], 16)

        set_tiles = [("A", j) for j in range(C)] + [("WI", k) for k in range(MAX_SKIP)] \
            + [("WH", k) for k in range(MAX_SKIP - 1)] + [("rs", 0)]

        def set_target(kind, j, part):
            return {"A": AT[part], "WI": WI[part], "WH": WH[part]}[kind][:, j]

        def bank_like(n, kind):
            o = sh.psum[:, n % 8, :]
            return o if kind == "A" else o.rearrange("p (g h) -> p g h", g=4)

        @block.tensor
        def _(pe):
            for n, (kind, j) in enumerate(set_tiles):
                if n >= 8:
                    pe.wait_ge(S["set_free"], n - 7)
                if n == C:
                    pe.wait_ge(S["w_in"], 32)
                o = sh.psum[:, n % 8, :]
                if kind == "rs":
                    pe.wait_ge(S["ones_done"], 1)
                    ins = pe.matmul(o, ones[:, :], diag[:, :, :], start=True, stop=True)
                for c in range(4 if kind != "rs" else 0):
                    src = {"A": sh.A[:, c, j * P:(j + 1) * P],
                           "WI": Hq[:, j, c * P:(c + 1) * P], "WH": Hin[:, min(j, MAX_SKIP - 2), c * P:(c + 1) * P]}[kind]
                    ins = pe.transpose(o[:, c * P:(c + 1) * P], src, sh.ident[:, :])
                ins.then_inc(S["set_mm"], 1)
            pe.wait_ge(S["set_free"], len(set_tiles))
            pe.wait_ge(S["wg_done"], 1)

            def item(kind, b, n, bk, q, h_base):
                o = sh.psum[:, bk, :]
                if kind == "R":
                    pe.wait_ge(S["h_done"], h_base + NS - 1 + b // 2)
                wait(pe, S["ring_free"], n - 3)
                if kind in ("Y0", "Y1"):
                    if kind == "Y0" and b == 0:
                        pe.wait_ge(S["xl_done"], C * (q + 1))
                    if kind == "Y1":
                        pe.wait_ge(S["h1l_done"], QB * q + b + 1)
                    hi, lo = (Xh, Xl) if kind == "Y0" else (h1h, h1l)
                    for c in range(C):
                        ins = product(pe, o, (hi[:, c, b, :], lo[:, c, b, :]), (ATh[:, c, :], ATl[:, c, :]),
                                      start=(c == 0), stop=(c == C - 1))
                elif kind == "W0":
                    for c in range(C):
                        cols = slice(c * P, (c + 1) * P)
                        ins = product(pe, o[:, cols], (ych[:, b % 2, cols], ycl[:, b % 2, cols]),
                                      (Wgs[0][0][:, :], Wgs[0][1][:, :]))
                elif kind == "W1":
                    ins = product(pe, o, (Wgs[1][0][:, :], Wgs[1][1][:, :]), (ych[:, b % 2, :], ycl[:, b % 2, :]))
                else:
                    for c in range(C):
                        ins = pe.transpose(o[:, c * P:(c + 1) * P], Hq[:, b, c * P:(c + 1) * P], sh.ident[:, :])
                ins.then_inc(S["ring_mm"], 1)

            def lstm(k, g):
                p_, t, s = steps[k]
                n = view(p_, t, s)[1]
                pe.wait_ge(S["xs_done"], NS * g + k + 1)
                for gate in gates_of(t):
                    per = NF if gate == F else NS
                    wait(pe, gate_act[gate], per * g + uses(k, gate))
                    ins = product(pe, sh.psum[:, gate, 0:n], (WI[0][:, p_ - 1, gate, :], WI[1][:, p_ - 1, gate, :]),
                                  (xh[:, s % 2, 0:n], xl[:, s % 2, 0:n]), stop=(t == 0))
                    if t == 0:
                        ins.then_inc(gate_mm[gate], 1)
                if t > 0:
                    pe.wait_ge(S["hs_done"], HS * g + hs_before(k - 2) + 1)
                    for gate in gates_of(t):
                        product(pe, sh.psum[:, gate, 0:n], (WH[0][:, p_ - 2, gate, :], WH[1][:, p_ - 2, gate, :]),
                                (hh[:, s % 2, 0:n], hl[:, s % 2, 0:n]), start=False).then_inc(gate_mm[gate], 1)

            def run(items, base, q, g):
                waiting = {}
                for kind, b, n, bk in numbered(items, base):
                    if kind == "L":
                        lstm(b, g)
                    elif kind not in NO_TILE:
                        if kind in ("W0", "W1"):
                            pe.wait_ge(S["ring_free"], waiting["Y" + kind[1], b] + 1)
                        waiting[kind, b] = n
                        item(kind, b, n, bk, q, None if g is None else NS * g)

            run(conv, 0, 0, None)
            run(mixed(True, False), ring_base(0), 1, 0)
            with pe.Fori(1, NQ - 1) as g:
                run(mixed(True, True), ring_base(g), g + 1, g)
            run(mixed(False, True), ring_base(NQ - 1), None, NQ - 1)

        @block.scalar
        def _(act):
            for i in (0, 1):
                if i == 0:
                    act.wait_ge(S["g_in"], 96)
                act.activation(Wgs[i][0][:, :], Wg[i][:, :], ACT.Copy).then_inc(S["wg_hi"], 1)
            for n, (kind, j) in enumerate(set_tiles[:-1]):
                act.wait_ge(S["set_mm"], n + 1)
                act.activation(set_target(kind, j, 0), bank_like(n, kind), ACT.Copy).then_inc(S["set_hi"], 1)
            act.wait_ge(S["gbias_done"], 1)

            def split_x(q):
                for c in range(C):
                    act.activation(Xh[:, c, :, :], sh.X[:, c, bass.ds(QB * q, QB), :], ACT.Copy)\
                        .then_inc(S["xh_done"], 1)

            def split_h(k, g):
                p_, t, s = steps[k]
                hv, n = view(p_, t, s)
                if p_ == 1:
                    act.wait_ge(S["hq_done"], QB * g + s + 1)
                elif t == 0:
                    last = max(i for i in range(k) if steps[i][0] == p_ - 1
                               and (steps[i][2] == s if p_ > 2 else steps[i][2] // 2 == s))
                    act.wait_ge(S["h_done"], NS * g + last + 1)
                wait(act, gate_mm[O], NS * g + max(k - 1, 0))
                act.activation(like(xh[:, s % 2, :], p_, n), hv, ACT.Copy).then_inc(S["x_hi"], 1)

            def lstm(k, g):
                p_, t, s = steps[k]
                n = view(p_, t, s)[1]
                for gate in gates_of(t):
                    if gate == gates_of(t)[2] and 1 <= k < NS - 1:
                        split_h(k + 1, g)
                    per = NF if gate == F else NS
                    act.wait_ge(gate_mm[gate], per * g + uses(k, gate) + 1)
                    wait(act, S["h_done" if gate == O else "c_done"], NS * g + k)
                    act.activation(gates[:, gate, 0:n], sh.psum[:, gate, 0:n],
                                   ACT.Tanh if gate == G else ACT.Sigmoid,
                                   bias=gbias[:, p_ - 1, gate:gate + 1]).then_inc(gate_act[gate], 1)
                act.wait_ge(S["c_done"], NS * g + k + 1)
                act.activation(tc[:, 0:n], cell[:, s % 2, 0:n], ACT.Tanh).then_inc(S["tanh_done"], 1)

            def run(items, base, q, g):
                hi = 0
                for kind, b, n, bk in numbered(items, base):
                    if kind == "L":
                        lstm(b, g)
                    elif kind in ("Y0", "Y1"):
                        act.wait_ge(S["ring_mm"], n + 1)
                        act.activation(ych[:, b % 2, :], sh.psum[:, bk, :], ACT.Copy).then_inc(S["conv_hi"], 1)
                    elif kind == "W0":
                        act.wait_ge(S["ring_free"], n + 1)
                        act.activation(h1h[:, :, b, :], u[:, b % 2, :, :], ACT.Relu).then_inc(S["relu_done"], 1)

            split_x(0)
            run(conv, 0, 0, None)
            split_h(0, 0)
            split_h(1, 0)
            split_x(1)
            run(mixed(True, False), ring_base(0), 1, 0)
            with act.Fori(1, NQ - 1) as g:
                split_h(0, g)
                split_h(1, g)
                split_x(g + 1)
                run(mixed(True, True), ring_base(g), g + 1, g)
            split_h(0, NQ - 1)
            split_h(1, NQ - 1)
            run(mixed(False, True), ring_base(NQ - 1), None, NQ - 1)

        @block.vector
        def _(dve):
            for c in range(C):
                ins = dve.reduce_sum(rs[:, c:c + 1], sh.A[:, c, :], AX.X)
            ins.then_inc(S["own"], 1)
            dve.memset(ones[:, :], 1.0)
            dve.wait_ge(S["own"], 1)
            for c in range(C):
                ins = dve.tensor_scalar(diag[:, c, :], sh.ident[:, :], rs[:, c:c + 1], None, ALU.mult)
            ins.then_inc(S["ones_done"], 1)
            dve.wait_ge(S["g_in"], 96)
            dve.tensor_tensor(gbias[:, :, :], bi[:, :, :], bh[:, :, :], ALU.add).then_inc(S["gbias_done"], 1)
            for c in range(C):
                ins = dve.tensor_scalar(RB0[:, c, :], bg0[:, :], rs[:, c:c + 1], None, ALU.mult)
            ins.then_inc(S["rb_done"], 1)
            for i in (0, 1):
                dve.wait_ge(S["wg_hi"], i + 1)
                ins = low_part(dve, Wgs[i][1][:, :], Wg[i][:, :], Wgs[i][0][:, :])
            ins.then_inc(S["wg_done"], 1)
            for n, (kind, j) in enumerate(set_tiles[:-1]):
                dve.wait_ge(S["set_hi"], n + 1)
                low_part(dve, set_target(kind, j, 1), bank_like(n, kind), set_target(kind, j, 0))\
                    .then_inc(S["set_free"], 1)
            dve.wait_ge(S["set_mm"], len(set_tiles))
            dve.tensor_scalar(RB1[:, :], sh.psum[:, (len(set_tiles) - 1) % 8, :], bg1[:, 0:1], None, ALU.mult)\
                .then_inc(S["set_free"], 1)
            dve.wait_ge(S["rb_done"], 1)
            dve.wait_ge(S["set_free"], len(set_tiles))

            def relu_h(g, b):
                dve.wait_ge(S["ring_free"], ring_base(g))
                dve.tensor_scalar(Hq[:, b, :], Hin[:, b, :], 0.0, None, ALU.max).then_inc(S["hq_done"], 1)

            def lstm(k, g):
                p_, t, s = steps[k]
                hv, n = view(p_, t, s)
                c_ = cell[:, s % 2, 0:n]

                def gate_is_there(gate):
                    per = NF if gate == F else NS
                    dve.wait_ge(gate_act[gate], per * g + uses(k, gate) + 1)

                gate_is_there(I)
                if t == 0:
                    dve.tensor_tensor(c_, gates[:, I, 0:n], gates[:, G, 0:n], ALU.mult).then_inc(S["c_done"], 1)
                else:
                    dve.tensor_tensor(gates[:, I, 0:n], gates[:, I, 0:n], gates[:, G, 0:n], ALU.mult)
                    gate_is_there(F)
                    dve.tensor_tensor(gates[:, F, 0:n], gates[:, F, 0:n], c_, ALU.mult).then_inc(S["c_own"], 1)
                    dve.wait_ge(S["c_own"], NF * g + uses(k, F) + 1)
                    dve.tensor_tensor(c_, gates[:, F, 0:n], gates[:, I, 0:n], ALU.add).then_inc(S["c_done"], 1)
                dve.wait_ge(S["tanh_done"], NS * g + k + 1)
                if t == p_ - 1:
                    dve.tensor_tensor(hv, like(gates[:, O, :], p_, n), like(tc, p_, n), ALU.mult)\
                        .then_inc(S["h_done"], 1)
                else:
                    dve.tensor_tensor(hn[:, 0:n], gates[:, O, 0:n], tc[:, 0:n], ALU.mult).then_inc(S["h_done"], 1)
                    dve.wait_ge(S["h_done"], NS * g + k + 1)
                    dve.tensor_copy(hh[:, s % 2, 0:n], hn[:, 0:n]).then_inc(S["c_own2"], 1)
                    dve.wait_ge(S["c_own2"], HS * g + hs_before(k) + 1)
                    low_part(dve, hl[:, s % 2, 0:n], hn[:, 0:n], hh[:, s % 2, 0:n]).then_inc(S["hs_done"], 1)

            def run(items, base, q, g):
                hi = 0
                for kind, b, n, bk in numbered(items, base):
                    o = sh.psum[:, bk, :]
                    if kind == "L":
                        lstm(b, g)
                    elif kind == "stats":
                        take_stats(g - 1)
                    elif kind == "norm":
                        normalise(g - 1)
                    elif kind in ("Y0", "Y1"):
                        hi += 1
                        dve.wait_ge(S["conv_hi"], 2 * QB * q + hi)
                        low_part(dve, ycl[:, b % 2, :], o, ych[:, b % 2, :]).then_inc(S["ring_free"], 1)
                    elif kind == "W0":
                        dve.wait_ge(S["ring_mm"], n + 1)
                        dve.tensor_tensor(u[:, b % 2, :, :], o.rearrange("p (c d) -> p c d", c=C), RB0[:, :, :],
                                          ALU.add).then_inc(S["ring_free"], 1)
                    elif kind == "low":
                        dve.wait_ge(S["relu_done"], QB * q + b + 1)
                        dve.scalar_tensor_tensor(h1l[:, :, b, :], u[:, b % 2, :, :], 0.0,
                                                 h1h[:, :, b, :].bitcast(F32), ALU.max, ALU.subtract)\
                            .then_inc(S["h1l_done"], 1)
                    elif kind == "W1":
                        dve.wait_ge(S["ring_mm"], n + 1)
                        dve.tensor_tensor(Hin[:, b, :], o, RB1[:, :], ALU.add).then_inc(S["ring_free"], 1)
                    else:
                        dve.wait_ge(S["ring_mm"], n + 1)
                        dve.tensor_tensor(sq[:, b, :, :], o.rearrange("p (c d) -> p c d", c=C),
                                          sh.X[:, :, bass.ds(QB * g + b, 1), :].rearrange("p c o d -> p c (o d)"),
                                          ALU.add).then_inc(S["ring_free"], 1)

            def take_stats(g):
                dve.wait_ge(S["ring_free"], sq_end(g))
                for b in range(QB):
                    ins = norm_stats(dve, stats[:, b * C:(b + 1) * C, :], sq[:, b, :, :])
                ins.then_inc(S["stat_done"], 1)

            def normalise(g):
                dve.wait_ge(S["rstd_done"], g + 1)
                for b in range(QB):
                    for c in range(C):
                        k = b * C + c
                        ins = dve.tensor_scalar(sh.X[:, c, bass.ds(QB * g + b, 1), :], sq[:, b, c:c + 1, :],
                                                mean[:, k:k + 1], rstd[:, k:k + 1], ALU.subtract, ALU.mult)
                ins.then_inc(S["x2_done"], 1)

            run(conv, 0, 0, None)
            def quad(items, q, g):
                for b in range(QB):
                    relu_h(g, b)
                run(items, ring_base(g), q, g)

            quad(mixed(True, False), 1, 0)
            with dve.Fori(1, NQ - 1) as g:
                quad(mixed(True, True), g + 1, g)
            quad(mixed(False, True), None, NQ - 1)
            take_stats(NQ - 1)
            normalise(NQ - 1)

        @block.gpsimd
        def _(pool):
            def split_x(q):
                for c in range(C):
                    pool.wait_ge(S["xh_done"], C * q + c + 1)
                    low_part(pool, Xl[:, c, :, :], sh.X[:, c, bass.ds(QB * q, QB), :], Xh[:, c, :, :])\
                        .then_inc(S["xl_done"], 1)

            def lstm(k, g):
                p_, t, s = steps[k]
                hv, n = view(p_, t, s)
                pool.wait_ge(S["x_hi"], NS * g + k + 1)
                low_part(pool, like(xl[:, s % 2, :], p_, n), hv, like(xh[:, s % 2, :], p_, n))\
                    .then_inc(S["xs_done"], 1)

            def norm(g):
                pool.wait_ge(S["stat_done"], g + 1)
                norm_scales(pool, sh, QB * C, stats, work3, mean[:, :], rstd[:, :], S["norm_own"],
                            NORM_LINKS * g).then_inc(S["rstd_done"], 1)

            def quad(g, last, norm_before=True):
                for k in range(NS):
                    lstm(k, g)
                    if k == 1 and not last:
                        split_x(g + 1)
                    if k == 3 and norm_before:
                        norm(g - 1)

            split_x(0)
            quad(0, False, False)
            with pool.Fori(1, NQ - 1) as g:
                quad(g, False)
            quad(NQ - 1, True)
            norm(NQ - 1)


def phase_batchnorm(nc, sh, d):
    C, D, N, NB = sh.C, sh.D, sh.N, sh.NB
    NP = NB // 2
    J = d["L2_gnn_W1"].shape[0] // P
    with ExitStack() as ctx:
        sb, sem = allocators(nc, ctx)
        H1 = sb("H1", [P, J, NB, N])
        O2 = sb("O2", [P, NB, N])
        AhT = (sb("AhTh", [P, C, N], F32R), sb("AhTl", [P, C, N], F32R))
        HI = sb("HI", [P, 4, N], F32R)
        LO = sb("LO", [P, 4, N], F32R)
        tmp = sb("tmp", [P, 4, N])
        wn = sb("wn", [P, 4, P])
        WT = (sb("WTh", [P, 4, P], F32R), sb("WTl", [P, 4, P], F32R))
        ones = sb("bones", [P, P])
        rsum = sb("brs", [P, C])
        dsum = sb("bds", [P, C])
        deg = sb("deg", [P, C])
        dinv = sb("dinv", [P, C])
        dblock = sb("dblock", [P, C, P])
        drow = sb("drow", [P, N])
        par1 = sb("par1", [P, 3, J])
        par2 = sb("par2", [P, 3, 1])
        st1 = sb("st1", [P, J, NB, 6])
        st2 = sb("st2", [P, 1, NB, 6])
        bmv = sb("bmv", [P, J + 1, 2])
        bsc = sb("bsc", [P, J + 1])
        bsh = sb("bsh", [P, J + 1])
        sq = sb("bsq", [P, 2, C, D])
        stats = sb("bst", [P, 2 * C, 6])
        work3 = sb("bwork3", [P, 3, 2 * C])
        mean = sb("bmean", [P, 2 * C])
        rstd = sb("brstd", [P, 2 * C])
        names = ("w_in", "p_in", "ones_done", "set_mm", "set_free", "set_hi", "own", "deg_done", "dinv_done", "ah_done",
                 "ah_hi", "ah_lo", "xh_done", "xl_done", "y_mm", "y_hi", "y_lo", "w_mm", "w_out", "st_done",
                 "bmv_done", "bve", "brstd", "bn_done", "u_done", "t_hi", "t_lo", "o_mm", "o_out", "ost_done",
                 "z_done", "z_mm", "z_add", "stat_done", "norm_own", "rstd_done", "x_done")
        S = {n: sem("b_" + n) for n in names}
        block = ctx.enter_context(nc.Block())

        def xb(b):
            return sh.X[:, :, bass.ds(b, 1), :].rearrange("p c o d -> p c (o d)")

        def by_chunk(ap):
            return ap.rearrange("p (c d) -> p c d", c=C)

        @block.sync
        def _(sp):
            sp.dma_start(wn[:, 0:J, :], d["L2_gnn_W1"].rearrange("(j p) d -> p j d", p=P)).then_inc(S["w_in"], 16)
            sp.dma_start(wn[:, J:2 * J, :], d["L2_gnn_W2"].rearrange("o (j h) -> o j h", j=J))\
                .then_inc(S["w_in"], 16)
            for k, name in enumerate(("b", "g", "be")):
                sp.dma_start(par1[:, k, :], d[f"L2_gnn_{name}1"].rearrange("(j p) -> p j", p=P))\
                    .then_inc(S["p_in"], 16)
                sp.dma_start(par2[:, k, :], d[f"L2_gnn_{name}2"].rearrange("(p o) -> p o", o=1))\
                    .then_inc(S["p_in"], 16)

        @block.tensor
        def _(pe):
            pe.wait_ge(S["ones_done"], 1)
            for c2 in range(C):
                for c in range(C):
                    ins = pe.matmul(sh.psum[:, 0, c2:c2 + 1], sh.A[:, c, c2 * P:(c2 + 1) * P], ones[:, 0:1],
                                    start=(c == 0), stop=(c == C - 1))
            ins.then_inc(S["set_mm"], 1)
            pe.wait_ge(S["w_in"], 32)
            for k in range(2 * J):
                ins = pe.transpose(sh.psum[:, 1, k * P:(k + 1) * P], wn[:, k, :], sh.ident[:, :])
            ins.then_inc(S["set_mm"], 1)
            for j in range(C):
                for c in range(C):
                    ins = pe.transpose(sh.psum[:, 3 + j, c * P:(c + 1) * P], sh.A[:, c, j * P:(j + 1) * P],
                                       sh.ident[:, :])
            ins.then_inc(S["set_mm"], 1)
            pe.wait_ge(S["deg_done"], 2)
            pe.matmul(sh.psum[:, 2, :], ones[:, :], dblock[:, :, :], start=True, stop=True)\
                .then_inc(S["set_mm"], 1)
            pe.wait_ge(S["ah_lo"], C)
            pe.wait_ge(S["set_free"], 2)

            def first(i, last):
                for s in (0, 1):
                    pe.wait_ge(S["xl_done"], 2 * i + s + 1)
                    for c in range(C):
                        cols = slice(c * D, (c + 1) * D)
                        ins = product(pe, sh.psum[:, s, :], (HI[:, s, cols], LO[:, s, cols]),
                                      (AhT[0][:, c, :], AhT[1][:, c, :]), start=(c == 0), stop=(c == C - 1))
                    ins.then_inc(S["y_mm"], 1)
                wait(pe, S["w_out"], 4 * i)
                for s in (0, 1):
                    pe.wait_ge(S["y_lo"], 2 * i + s + 1)
                    for j in range(J):
                        product(pe, sh.psum[:, 2 + 2 * s + j, :], (WT[0][:, j, :], WT[1][:, j, :]),
                                (HI[:, 2 + s, :], LO[:, 2 + s, :])).then_inc(S["w_mm"], 1)

            def second(i, last):
                for s in (0, 1):
                    pe.wait_ge(S["t_lo"], 4 * i + 2 * s + 2)
                    wait(pe, S["o_out"], 2 * i)
                    for j in range(J):
                        ins = product(pe, sh.psum[:, 6 + s, :], (WT[0][:, J + j, :], WT[1][:, J + j, :]),
                                      (HI[:, 2 * s + j, :], LO[:, 2 * s + j, :]), start=(j == 0),
                                      stop=(j == J - 1))
                    ins.then_inc(S["o_mm"], 1)

            def third(i, last):
                for s in (0, 1):
                    pe.wait_ge(S["z_done"], 2 * i + s + 1)
                    wait(pe, S["z_add"], 2 * i)
                    for c in range(C):
                        cols = slice(c * P, (c + 1) * P)
                        ins = pe.transpose(sh.psum[:, s, cols], tmp[:, s, cols], sh.ident[:, :])
                    ins.then_inc(S["z_mm"], 1)

            peeled(pe, NP, first)
            peeled(pe, NP, second)
            peeled(pe, NP, third)

        @block.scalar
        def _(act):
            act.wait_ge(S["set_mm"], 2)
            act.activation(WT[0][:, :, :], sh.psum[:, 1, :].rearrange("p (k h) -> p k h", h=P), ACT.Copy)\
                .then_inc(S["set_hi"], 1)
            for j in range(C):
                act.wait_ge(S["ah_done"], j + 1)
                act.activation(AhT[0][:, j, :], tmp[:, j, :], ACT.Copy).then_inc(S["ah_hi"], 1)

            def split_x(b, s):
                act.activation(by_chunk(HI[:, s, :]), xb(b), ACT.Copy).then_inc(S["xh_done"], 1)

            def first(i, last):
                for s in (0, 1):
                    act.wait_ge(S["y_mm"], 2 * i + s + 1)
                    act.activation(HI[:, 2 + s, :], sh.psum[:, s, :], ACT.Copy).then_inc(S["y_hi"], 1)
                    if not last:
                        split_x(2 * i + 2 + s, s)
                for s in (0, 1):
                    for j in range(J):
                        act.wait_ge(S["w_mm"], 4 * i + 2 * s + j + 1)
                        act.activation(H1[:, j, bass.ds(2 * i + s, 1), :], sh.psum[:, 2 + 2 * s + j, :],
                                       ACT.Identity, bias=par1[:, 0, j:j + 1]).then_inc(S["w_out"], 1)

            def second(i, last):
                for s in (0, 1):
                    for j in range(J):
                        act.wait_ge(S["u_done"], 4 * i + 2 * s + j + 1)
                        wait(act, S["o_mm"], 2 * i)
                        act.activation(HI[:, 2 * s + j, :], tmp[:, 2 * s + j, :], ACT.Relu)\
                            .then_inc(S["t_hi"], 1)
                for s in (0, 1):
                    act.wait_ge(S["o_mm"], 2 * i + s + 1)
                    act.activation(O2[:, bass.ds(2 * i + s, 1), :], sh.psum[:, 6 + s, :], ACT.Identity,
                                   bias=par2[:, 0, 0:1]).then_inc(S["o_out"], 1)

            def third(i, last):
                for s in (0, 1):
                    wait(act, S["z_mm"], 2 * i)
                    act.activation(tmp[:, s, :], O2[:, bass.ds(2 * i + s, 1), :], ACT.Identity,
                                   bias=bsh[:, J:J + 1], scale=bsc[:, J:J + 1]).then_inc(S["z_done"], 1)

            for s in (0, 1):
                split_x(s, s)
            act.wait_ge(S["p_in"], 96)
            peeled(act, NP, first)
            peeled(act, NP, second)
            act.wait_ge(S["bn_done"], 2)
            peeled(act, NP, third)

        @block.vector
        def _(dve):
            chain = [0]

            def link(ins):
                chain[0] += 1
                ins.then_inc(S["own"], 1)
                dve.wait_ge(S["own"], chain[0])

            dve.memset(ones[:, :], 1.0).then_inc(S["ones_done"], 1)
            for c in range(C):
                dve.reduce_sum(rsum[:, c:c + 1], sh.A[:, c, :], AX.X)
            for c in range(C):
                ins = dve.tensor_tensor(dblock[:, c, :], sh.A[:, c, c * P:(c + 1) * P], sh.ident[:, :], ALU.mult)
            link(ins)
            link(dve.reduce_sum(dsum[:, :], dblock[:, :, :], AX.X))
            link(dve.scalar_tensor_tensor(rsum[:, :], rsum[:, :], 1.0, dsum[:, :], ALU.add, ALU.subtract))
            dve.wait_ge(S["set_mm"], 1)
            dve.tensor_tensor(deg[:, :], sh.psum[:, 0, 0:C], rsum[:, :], ALU.add).then_inc(S["deg_done"], 1)
            dve.wait_ge(S["dinv_done"], 1)
            for c in range(C):
                ins = dve.tensor_scalar(dblock[:, c, :], sh.ident[:, :], dinv[:, c:c + 1], None, ALU.mult)
            ins.then_inc(S["deg_done"], 1)
            dve.wait_ge(S["set_hi"], 1)
            low_part(dve, WT[1][:, :, :], sh.psum[:, 1, :].rearrange("p (k h) -> p k h", h=P), WT[0][:, :, :])\
                .then_inc(S["set_free"], 1)
            dve.wait_ge(S["set_mm"], 4)
            dve.tensor_copy(drow[:, :], sh.psum[:, 2, :]).then_inc(S["set_free"], 1)
            dve.wait_ge(S["set_free"], 2)
            dve.wait_ge(S["deg_done"], 2)
            for j in range(C):
                link(dve.tensor_scalar(tmp[:, j, :], sh.psum[:, 3 + j, :], dinv[:, j:j + 1], None, ALU.mult))
                own = tmp[:, j, j * P:(j + 1) * P]
                link(dve.tensor_tensor(own, own, dblock[:, j, :], ALU.add))
                dve.tensor_tensor(tmp[:, j, :], tmp[:, j, :], drow[:, :], ALU.mult).then_inc(S["ah_done"], 1)
            for j in range(C):
                dve.wait_ge(S["ah_hi"], j + 1)
                low_part(dve, AhT[1][:, j, :], tmp[:, j, :], AhT[0][:, j, :]).then_inc(S["ah_lo"], 1)

            def first(i, last):
                for s in (0, 1):
                    dve.wait_ge(S["y_hi"], 2 * i + s + 1)
                    low_part(dve, LO[:, 2 + s, :], sh.psum[:, s, :], HI[:, 2 + s, :]).then_inc(S["y_lo"], 1)
                for s in (0, 1):
                    for j in range(J):
                        dve.wait_ge(S["w_out"], 4 * i + 2 * s + j + 1)
                        dve.bn_stats(st1[:, j, bass.ds(2 * i + s, 1), :], H1[:, j, bass.ds(2 * i + s, 1), :])\
                            .then_inc(S["st_done"], 1)

            def norm(js, k):
                st, par = (st1, par1) if k == 0 else (st2, par2)
                for j in js:
                    ins = dve.bn_aggr(bmv[:, j, :], st[:, j - js[0], :, :].rearrange("p b s -> p (b s)"))
                ins.then_inc(S["bmv_done"], 1)
                dve.wait_ge(S["brstd"], k + 1)
                cols = slice(js[0], js[-1] + 1)
                link(dve.tensor_tensor(bsc[:, cols], bsc[:, cols], par[:, 1, :], ALU.mult))
                link(dve.tensor_tensor(bsh[:, cols], bmv[:, cols, 0], bsc[:, cols], ALU.mult))
                dve.tensor_tensor(bsh[:, cols], par[:, 2, :], bsh[:, cols], ALU.subtract)\
                    .then_inc(S["bn_done"], 1)
                dve.wait_ge(S["bn_done"], k + 1)

            def second(i, last):
                wait(dve, S["t_lo"], 4 * i)
                for s in (0, 1):
                    for j in range(J):
                        dve.tensor_scalar(tmp[:, 2 * s + j, :], H1[:, j, bass.ds(2 * i + s, 1), :], bsc[:, j:j + 1],
                                          bsh[:, j:j + 1], ALU.mult, ALU.add).then_inc(S["u_done"], 1)
                for s in (0, 1):
                    for j in range(J):
                        dve.wait_ge(S["t_hi"], 4 * i + 2 * s + j + 1)
                        dve.scalar_tensor_tensor(LO[:, 2 * s + j, :], tmp[:, 2 * s + j, :], 0.0,
                                                 HI[:, 2 * s + j, :].bitcast(F32), ALU.max, ALU.subtract)\
                            .then_inc(S["t_lo"], 1)
                for s in (0, 1):
                    dve.wait_ge(S["o_out"], 2 * i + s + 1)
                    dve.bn_stats(st2[:, 0, bass.ds(2 * i + s, 1), :], O2[:, bass.ds(2 * i + s, 1), :])\
                        .then_inc(S["ost_done"], 1)

            def third(i, last):
                wait(dve, S["x_done"], i)
                for s in (0, 1):
                    dve.wait_ge(S["z_mm"], 2 * i + s + 1)
                    dve.tensor_tensor(sq[:, s, :, :], by_chunk(sh.psum[:, s, :]), xb(2 * i + s), ALU.add)\
                        .then_inc(S["z_add"], 1)
                    dve.wait_ge(S["z_add"], 2 * i + s + 1)
                    norm_stats(dve, stats[:, s * C:(s + 1) * C, :], sq[:, s, :, :]).then_inc(S["stat_done"], 1)
                dve.wait_ge(S["rstd_done"], i + 1)
                for s in (0, 1):
                    for c in range(C):
                        ins = dve.tensor_scalar(sh.X[:, c, bass.ds(2 * i + s, 1), :], sq[:, s, c:c + 1, :],
                                                mean[:, s * C + c:s * C + c + 1],
                                                rstd[:, s * C + c:s * C + c + 1], ALU.subtract, ALU.mult)
                ins.then_inc(S["x_done"], 1)

            peeled(dve, NP, first)
            dve.wait_ge(S["st_done"], 2 * J * NP)
            norm(list(range(J)), 0)
            peeled(dve, NP, second)
            dve.wait_ge(S["ost_done"], 2 * NP)
            norm([J], 1)
            peeled(dve, NP, third)

        @block.gpsimd
        def _(pool):
            pool.wait_ge(S["deg_done"], 1)
            pool.tensor_tensor(dinv[:, :], deg[:, :], sh.const[:, sh.ROOT, 0:C], ALU.pow).then_inc(S["dinv_done"], 1)

            def split_x(b, s, n):
                pool.wait_ge(S["xh_done"], n)
                low_part(pool, by_chunk(LO[:, s, :]), xb(b), by_chunk(HI[:, s, :])).then_inc(S["xl_done"], 1)

            for s in (0, 1):
                split_x(s, s, s + 1)
            with pool.Fori(0, NP - 1) as i:
                for s in (0, 1):
                    split_x(2 * i + 2 + s, s, 2 * i + s + 3)

            def norm(cols, k):
                pool.wait_ge(S["bmv_done"], k + 1)
                n = cols.stop - cols.start
                pool.tensor_tensor(bsc[:, cols], bmv[:, cols, 1], sh.const[:, sh.EPS, 0:n], ALU.add).then_inc(S["bve"], 1)
                pool.wait_ge(S["bve"], k + 1)
                pool.tensor_tensor(bsc[:, cols], bsc[:, cols], sh.const[:, sh.ROOT, 0:n], ALU.pow).then_inc(S["brstd"], 1)

            norm(slice(0, J), 0)
            norm(slice(J, J + 1), 1)
            with pool.Fori(0, NP) as i:
                pool.wait_ge(S["stat_done"], 2 * i + 2)
                norm_scales(pool, sh, 2 * C, stats, work3, mean[:, :], rstd[:, :], S["norm_own"],
                            NORM_LINKS * i).then_inc(S["rstd_done"], 1)


def phase_attention(nc, sh, d, out):
    C, D, N, NB = sh.C, sh.D, sh.N, sh.NB
    NE = d["L3_gnn_src"].shape[0]
    K = NE // P
    NH, DH = d["L3_gnn_a"].shape
    NQ, NP = NB // QB, NB // 2
    R = QB * NH
    with ExitStack() as ctx:
        sb, sem = allocators(nc, ctx)
        ir = sb("ir", [P, 2, NE], I32)
        icol = sb("icol", [P, 2, K], I32)
        irf = sb("irf", [P, 2, NE])
        icf = sb("icf", [P, 2, K])
        iota = sb("iota", [P, N], I32)
        iotac = sb("iotac", [P, C], I32)
        iof = sb("iof", [P, N])
        ioc = sb("ioc", [P, C])
        keyr = sb("keyr", [P, NE])
        keyc = sb("keyc", [P, K])
        less = sb("less", [P, K, NE])
        pos = sb("pos", [P, K])
        perm = sb("perm", [P, K, NE])
        idxb = sb("idxb", [P, 2, K, P])
        ss = sb("ss", [P, 2, NE])
        sc = sb("sc", [P, K])
        Gs = sb("Gs", [P, C, NE])
        GZ = sb("GZ", [P, C, 2, NE], F32R)
        GsT = sb("GsT", [P, K, N], F32R)
        ones = sb("aones", [P, P])
        sel = sb("sel", [P, C, NE])
        lg = sb("lg", [R, NE])
        tiny = sb("tiny", [P, 1])
        ne = sb("ne", [R, NE])
        pf = sb("pf", [R, QB, NE])
        pr = sb("pr", [R, QB, NE])
        kf = sb("kf", [R, QB, NE])
        wn = sb("awn", [P, 3, P])
        WT = (sb("aWTh", [P, 3, P], F32R), sb("aWTl", [P, 3, P], F32R))
        acol = sb("acol", [P, 1])
        wide = sb("wide", [P, 2 * R - NH])
        XH = sb("aXH", [P, 2, N], F32R)
        XL = sb("aXL", [P, 2, N], F32R)
        ZH = sb("ZH", [P, 2, N], F32R)
        ZL = sb("ZL", [P, 2, N], F32R)
        uq = sb("uq", [P, 2, NE])
        lr = sb("lr", [P, 2, NE])
        V = sb("aV", [P, NB, K, D])
        sco = sb("sco", [R, QB, NE])
        s1 = sb("s1", [R, QB, NE])
        s2 = sb("s2", [R, QB, NE])
        aT = sb("aT", [P, K, NB, NH])
        va = sb("va", [P, 2, K, D])
        vah = sb("vah", [P, 2, K, D], F32R)
        val = sb("val", [P, 2, K, D], F32R)
        sq = sb("asq", [P, 2, C, D])
        stats = sb("ast", [P, 2 * C, 6])
        work3 = sb("awork3", [P, 3, 2 * C])
        mean = sb("amean", [P, 2 * C])
        rstd = sb("arstd", [P, 2 * C])
        names = ("i_in", "w_in", "iota_done", "own", "perm_done", "set_mm", "ss_done", "g_done", "sel_done", "lg_done",
                 "w_hi", "w_lo", "wide0", "wide_done", "xh_done", "xl_done", "z_mm", "z_hi", "z_lo", "uv_mm", "uv_out",
                 "lr_done", "sc_mm", "sc_done", "sd_done", "ex_done", "soft", "at_mm", "at_done", "va_done",
                 "va_hi", "va_lo", "y_mm", "y_hi", "y_lo", "o_mm", "o_add", "stat_done", "norm_own",
                 "rstd_done", "x_done", "stored")
        S = {n: sem("a_" + n) for n in names}
        block = ctx.enter_context(nc.Block())

        def xb(b):
            return sh.X[:, :, bass.ds(b, 1), :].rearrange("p c o d -> p c (o d)")

        def by_chunk(ap):
            return ap.rearrange("p (c d) -> p c d", c=C)

        @block.sync
        def _(sp):
            for k, name in enumerate(("src", "dst")):
                sp.dma_start(ir[:, k, :], d[f"L3_gnn_{name}"].rearrange("(o e) -> o e", o=1)
                             .broadcast_to([P, NE])).then_inc(S["i_in"], 16)
                sp.dma_start(icol[:, k, :], d[f"L3_gnn_{name}"].rearrange("(k p) -> p k", p=P))\
                    .then_inc(S["i_in"], 16)
            for k, name in enumerate(("W_lin", "W_val", "W_out")):
                sp.dma_start(wn[:, k, :], d[f"L3_gnn_{name}"]).then_inc(S["w_in"], 16)
            sp.dma_start(acol[:, :], d["L3_gnn_a"].rearrange("h (e o) -> (h e) o", o=1)).then_inc(S["w_in"], 16)
            ov = out.rearrange("b (c p) d -> p c b d", p=P)
            with sp.Fori(0, NP) as i:
                sp.wait_ge(S["x_done"], i + 1)
                for c in range(C):
                    sp.dma_start(ov[:, c, bass.ds(2 * i, 2), :], sh.X[:, c, bass.ds(2 * i, 2), :])\
                        .then_inc(S["stored"], 16)
            sp.wait_ge(S["stored"], 16 * C * NP)

        @block.gpsimd
        def _(pool):
            pool.iota(iota[:, :], pattern=[[1, N]], base=0, channel_multiplier=0).then_inc(S["iota_done"], 1)
            pool.iota(iotac[:, :], pattern=[[P, C]], base=0, channel_multiplier=1).then_inc(S["iota_done"], 1)
            pool.memset(wide[:, :], 0.0).then_inc(S["wide0"], 1)
            pool.memset(tiny[:, :], 1e-8).then_inc(S["wide0"], 1)

            def split_x(b, s, n):
                pool.wait_ge(S["xh_done"], n)
                low_part(pool, by_chunk(XL[:, s, :]), xb(b), by_chunk(XH[:, s, :])).then_inc(S["xl_done"], 1)

            for s in (0, 1):
                split_x(s, s, s + 1)
            with pool.Fori(0, NP - 1) as i:
                for s in (0, 1):
                    split_x(2 * i + 2 + s, s, 2 * i + s + 3)
            with pool.Fori(0, NP) as i:
                pool.wait_ge(S["stat_done"], 2 * i + 2)
                norm_scales(pool, sh, 2 * C, stats, work3, mean[:, :], rstd[:, :], S["norm_own"],
                            NORM_LINKS * i).then_inc(S["rstd_done"], 1)

        @block.scalar
        def _(act):
            act.wait_ge(S["set_mm"], 1)
            act.activation(WT[0][:, :, :], sh.psum[:, 0, 0:3 * P].rearrange("p (k h) -> p k h", h=P), ACT.Copy)\
                .then_inc(S["w_hi"], 1)
            act.wait_ge(S["set_mm"], 4)
            act.wait_ge(S["wide0"], 2)
            act.activation(lg[:, :], sh.psum[0:R, 4, 0:NE], ACT.Ln, bias=tiny[0:R, 0:1]).then_inc(S["lg_done"], 1)

            def split_x(b, s):
                act.activation(by_chunk(XH[:, s, :]), xb(b), ACT.Copy).then_inc(S["xh_done"], 1)

            def gather(g, h, last):
                for s in (0, 1):
                    n = QB * g + 2 * h + s
                    act.wait_ge(S["z_mm"], n + 1)
                    act.activation(ZH[:, s, :], sh.psum[:, s, :], ACT.Copy).then_inc(S["z_hi"], 1)
                    if not last:
                        split_x(n + 2, s)
                for s in (0, 1):
                    n = QB * g + 2 * h + s
                    act.wait_ge(S["uv_mm"], n + 1)
                    wait(act, S["lr_done"], QB * g + 2 * h)
                    act.activation(uq[:, s, :], sh.psum[:, 2 + s, 0:NE], ACT.Copy).then_inc(S["uv_out"], 1)
                    act.activation(V[:, bass.ds(n, 1), :, :],
                                   sh.psum[:, 2 + s, NE:2 * NE].rearrange("p (k d) -> p k d", k=K), ACT.Copy)\
                        .then_inc(S["uv_out"], 1)

            for s in (0, 1):
                split_x(s, s)

            def gather_quad(g, last):
                gather(g, 0, False)
                gather(g, 1, last)

            peeled(act, NQ, gather_quad)
            act.wait_ge(S["sd_done"], 1)
            act.activation(s2[:, :, :], s1[:, :, :], ACT.Exp).then_inc(S["ex_done"], 1)

            def weigh(i, last):
                for s in (0, 1):
                    act.wait_ge(S["va_done"], 2 * i + s + 1)
                    wait(act, S["y_mm"], 2 * i)
                    act.activation(vah[:, s, :, :], va[:, s, :, :], ACT.Copy).then_inc(S["va_hi"], 1)
                for s in (0, 1):
                    act.wait_ge(S["y_mm"], 2 * i + s + 1)
                    act.activation(ZH[:, s, :], sh.psum[:, s, :], ACT.Copy).then_inc(S["y_hi"], 1)

            peeled(act, NP, weigh)

        @block.vector
        def _(dve):
            chain = [0]

            def link(ins):
                chain[0] += 1
                ins.then_inc(S["own"], 1)
                dve.wait_ge(S["own"], chain[0])

            dve.wait_ge(S["iota_done"], 2)
            dve.wait_ge(S["i_in"], 64)
            dve.memset(ones[:, :], 1.0)
            dve.tensor_copy(iof[:, :], iota[:, :])
            dve.tensor_copy(ioc[:, :], iotac[:, :])
            dve.tensor_copy(icf[:, :, :], icol[:, :, :])
            link(dve.tensor_copy(irf[:, :, :], ir[:, :, :]))
            dve.scalar_tensor_tensor(keyr[:, :], irf[:, 0, :], float(NE), iof[:, 0:NE], ALU.mult, ALU.add)
            link(dve.scalar_tensor_tensor(keyc[:, :], icf[:, 0, :], float(NE), ioc[:, 0:K], ALU.mult, ALU.add))
            for k in range(K):
                ins = dve.tensor_scalar(less[:, k, :], keyr[:, :], keyc[:, k:k + 1], None, ALU.is_lt)
            link(ins)
            link(dve.reduce_sum(pos[:, :], less[:, :, :], AX.X))
            for k in range(K):
                dve.tensor_scalar(perm[:, k, :], iof[:, 0:NE], pos[:, k:k + 1], None, ALU.is_equal)
                for j in (0, 1):
                    ins = dve.tensor_scalar(idxb[:, j, k, :], ones[:, :], icf[:, j, k:k + 1], None, ALU.mult)
            ins.then_inc(S["perm_done"], 1)
            dve.wait_ge(S["w_hi"], 1)
            low_part(dve, WT[1][:, :, :], sh.psum[:, 0, 0:3 * P].rearrange("p (k h) -> p k h", h=P), WT[0][:, :, :])\
                .then_inc(S["w_lo"], 1)
            dve.wait_ge(S["wide0"], 2)
            dve.wait_ge(S["w_in"], 64)
            for h in range(NH):
                rows = slice(h * DH, (h + 1) * DH)
                ins = dve.tensor_copy(wide[rows, R - NH + h:R - NH + h + 1], acol[rows, 0:1])
            ins.then_inc(S["wide_done"], 1)
            dve.wait_ge(S["set_mm"], 2)
            dve.tensor_copy(sc[:, :], sh.psum[:, 2, 0:K])
            link(dve.tensor_copy(ss[:, :, :], sh.psum[:, 1, :].rearrange("p (j e) -> p j e", j=2)))
            for c in range(C):
                dve.tensor_scalar(Gs[:, c, :], ss[:, 0, :], ioc[:, c:c + 1], None, ALU.is_equal)
                ins = dve.tensor_scalar(GZ[:, c, 1, :], ss[:, 1, :], ioc[:, c:c + 1], None, ALU.is_equal)
            link(ins)
            dve.tensor_tensor(GZ[:, :, 0, :], Gs[:, :, :], GZ[:, :, 1, :].bitcast(F32), ALU.add)
            for k in range(K):
                ins = dve.tensor_scalar(GsT[:, k, :], iof[:, :], sc[:, k:k + 1], None, ALU.is_equal)
            ins.then_inc(S["g_done"], 1)
            dve.wait_ge(S["set_mm"], 3)
            dve.tensor_tensor(sel[:, :, :], sh.psum[:, 5:7, :].rearrange("p t (c e) -> p (t c) e", e=NE),
                              GZ[:, :, 1, :].bitcast(F32), ALU.mult).then_inc(S["sel_done"], 1)
            link(dve.tensor_tensor(ne[:, 1:NE], ss[0:R, 0, 1:NE], ss[0:R, 0, 0:NE - 1], ALU.not_equal))
            for q in range(QB):
                dve.tensor_scalar(pf[:, q, 1:NE], ne[:, 1:NE], LOWEST, None, ALU.mult)
                dve.tensor_scalar(kf[:, q, 1:NE], ne[:, 1:NE], -1.0, 1.0, ALU.mult, ALU.add)
                dve.tensor_scalar(pr[:, q, 0:NE - 1], ne[:, 1:NE], LOWEST, None, ALU.mult)
            dve.memset(pf[:, :, 0:1], LOWEST)
            dve.memset(kf[:, :, 0:1], 0.0)
            dve.memset(pr[:, :, NE - 1:NE], LOWEST)

            def gather(g, h, last):
                for s in (0, 1):
                    n = QB * g + 2 * h + s
                    dve.wait_ge(S["z_hi"], n + 1)
                    low_part(dve, ZL[:, s, :], sh.psum[:, s, :], ZH[:, s, :]).then_inc(S["z_lo"], 1)
                for s in (0, 1):
                    n = QB * g + 2 * h + s
                    dve.wait_ge(S["uv_out"], 2 * n + 1)
                    dve.scalar_tensor_tensor(lr[:, s, :], uq[:, s, :], 0.2, uq[:, s, :], ALU.mult, ALU.max)\
                        .then_inc(S["lr_done"], 1)

            def scores(g):
                dve.wait_ge(S["sc_mm"], QB * g + QB)
                dve.tensor_tensor(sco[:, bass.ds(g, 1), :].rearrange("p o e -> p (o e)"), sh.psum[0:R, 4, 0:NE],
                                  lg[:, :], ALU.add).then_inc(S["sc_done"], 1)

            dve.wait_ge(S["lg_done"], 1)

            def gather_quad(g, last):
                for h in (0, 1):
                    wait(dve, S["sc_mm"], QB * g + 2 * h)
                    gather(g, h, False)
                scores(g)

            peeled(dve, NQ, gather_quad)

            def flat(t):
                return t[:, :, :].rearrange("p q e -> p (q e)")

            soft = [0]

            def then(ins):
                soft[0] += 1
                ins.then_inc(S["soft"], 1)
                dve.wait_ge(S["soft"], soft[0])

            dve.wait_ge(S["sc_done"], NQ)
            then(dve.tensor_tensor_scan(flat(s1), flat(pf), flat(sco), LOWEST, ALU.add, ALU.max))
            then(dve.tensor_tensor_scan(flat(s2)[:, ::-1], flat(pr)[:, ::-1], flat(s1)[:, ::-1], LOWEST,
                                        ALU.add, ALU.max))
            dve.tensor_tensor(flat(s1), flat(sco), flat(s2), ALU.subtract).then_inc(S["sd_done"], 1)
            dve.wait_ge(S["ex_done"], 1)
            then(dve.tensor_tensor_scan(flat(s1), flat(kf), flat(s2), 0.0, ALU.mult, ALU.add))
            then(dve.tensor_tensor_scan(flat(sco)[:, ::-1], flat(pr)[:, ::-1], flat(s1)[:, ::-1], 0.0,
                                        ALU.add, ALU.max))
            then(dve.reciprocal(flat(s1), flat(sco)))
            dve.tensor_tensor(flat(sco), flat(s2), flat(s1), ALU.mult).then_inc(S["soft"], 1)
            dve.wait_ge(S["at_mm"], 1)
            dve.tensor_copy(aT[:, :, :, :].rearrange("p k (q b) h -> p k q (b h)", q=NQ),
                            sh.psum[:, 5, 0:NQ * K * R].rearrange("p (k q r) -> p k q r", k=K, q=NQ))\
                .then_inc(S["at_done"], 1)
            dve.wait_ge(S["at_done"], 1)

            def weigh(b, s):
                for k in range(K):
                    ins = dve.tensor_tensor(
                        va[:, s, k, :].rearrange("p (h e) -> p h e", h=NH),
                        V[:, bass.ds(b, 1), k, :].rearrange("p o (h e) -> p (o h) e", h=NH),
                        aT[:, k, bass.ds(b, 1), :].rearrange("p o h -> p (o h)").unsqueeze(2)
                        .broadcast_to([P, NH, DH]), ALU.mult)
                ins.then_inc(S["va_done"], 1)

            def attend(i, last):
                wait(dve, S["va_lo"], 2 * i)
                wait(dve, S["x_done"], i)
                for s in (0, 1):
                    weigh(2 * i + s, s)
                for s in (0, 1):
                    dve.wait_ge(S["va_hi"], 2 * i + s + 1)
                    low_part(dve, val[:, s, :, :], va[:, s, :, :], vah[:, s, :, :]).then_inc(S["va_lo"], 1)
                for s in (0, 1):
                    dve.wait_ge(S["y_hi"], 2 * i + s + 1)
                    low_part(dve, ZL[:, s, :], sh.psum[:, s, :], ZH[:, s, :]).then_inc(S["y_lo"], 1)
                for s in (0, 1):
                    dve.wait_ge(S["o_mm"], 2 * i + s + 1)
                    dve.tensor_tensor(sq[:, s, :, :], by_chunk(sh.psum[:, 2 + s, :]), xb(2 * i + s), ALU.add)\
                        .then_inc(S["o_add"], 1)
                    dve.wait_ge(S["o_add"], 2 * i + s + 1)
                    norm_stats(dve, stats[:, s * C:(s + 1) * C, :], sq[:, s, :, :]).then_inc(S["stat_done"], 1)
                dve.wait_ge(S["rstd_done"], i + 1)
                for s in (0, 1):
                    for c in range(C):
                        ins = dve.tensor_scalar(sh.X[:, c, bass.ds(2 * i + s, 1), :], sq[:, s, c:c + 1, :],
                                                mean[:, s * C + c:s * C + c + 1],
                                                rstd[:, s * C + c:s * C + c + 1], ALU.subtract, ALU.mult)
                ins.then_inc(S["x_done"], 1)

            peeled(dve, NP, attend)

        @block.tensor
        def _(pe):
            pe.wait_ge(S["w_in"], 64)
            for k in range(3):
                ins = pe.transpose(sh.psum[:, 0, k * P:(k + 1) * P], wn[:, k, :], sh.ident[:, :])
            ins.then_inc(S["set_mm"], 1)
            pe.wait_ge(S["perm_done"], 1)
            for j in (0, 1):
                for k in range(K):
                    pe.matmul(sh.psum[:, 1, j * NE:(j + 1) * NE], idxb[:, j, k, :], perm[:, k, :], start=(k == 0),
                              stop=(k == K - 1))
            for q in range(K):
                for k in range(K):
                    ins = pe.matmul(sh.psum[:, 2, q:q + 1], perm[:, k, q * P:(q + 1) * P], icf[:, 0, k:k + 1],
                                    start=(k == 0), stop=(k == K - 1))
            ins.then_inc(S["set_mm"], 1)
            pe.wait_ge(S["g_done"], 1)
            for m in range(C):
                for c in range(C):
                    ins = pe.matmul(sh.psum[:, 5 + m // 2, (m % 2) * NE:(m % 2 + 1) * NE],
                                    sh.A[:, c, m * P:(m + 1) * P], Gs[:, c, :], start=(c == 0), stop=(c == C - 1))
            ins.then_inc(S["set_mm"], 1)
            pe.wait_ge(S["sel_done"], 1)
            for c in range(C):
                ins = pe.matmul(sh.psum[0:R, 4, 0:NE], ones[:, 0:R], sel[:, c, :], start=(c == 0),
                                stop=(c == C - 1))
            ins.then_inc(S["set_mm"], 1)
            pe.wait_ge(S["w_lo"], 1)
            pe.wait_ge(S["wide_done"], 1)
            pe.wait_ge(S["lg_done"], 1)

            def gather_quad(g, last):
                for h in (0, 1):
                    n = QB * g + 2 * h
                    for s in (0, 1):
                        pe.wait_ge(S["xl_done"], n + s + 1)
                        for c in range(C):
                            cols = slice(c * D, (c + 1) * D)
                            for part in (XH, XL):
                                ins = pe.matmul(sh.psum[:, s, :], part[:, s, cols], GZ[:, c, :, :],
                                                start=(c == 0 and part is XH), stop=(c == C - 1 and part is XL))
                        ins.then_inc(S["z_mm"], 1)
                    wait(pe, S["uv_out"], 2 * n)
                    for s in (0, 1):
                        pe.wait_ge(S["z_lo"], n + s + 1)
                        product(pe, sh.psum[:, 2 + s, 0:NE], (WT[0][:, 0, :], WT[1][:, 0, :]),
                                (ZH[:, s, 0:NE], ZL[:, s, 0:NE]))
                        for k in range(K):
                            cols = slice(NE + k * P, NE + (k + 1) * P)
                            ins = product(pe, sh.psum[:, 2 + s, cols], (ZH[:, s, cols], ZL[:, s, cols]),
                                          (WT[0][:, 1, :], WT[1][:, 1, :]))
                        ins.then_inc(S["uv_mm"], 1)
                    if h == 0:
                        wait(pe, S["sc_done"], g)
                    for s in (0, 1):
                        pe.wait_ge(S["lr_done"], n + s + 1)
                        b = 2 * h + s
                        pe.matmul(sh.psum[0:R, 4, 0:NE], wide[:, R - NH - NH * b:2 * R - NH - NH * b], lr[:, s, :],
                                  start=(b == 0), stop=(b == QB - 1)).then_inc(S["sc_mm"], 1)

            peeled(pe, NQ, gather_quad)
            pe.wait_ge(S["soft"], 6)
            for k in range(K):
                for q in range(NQ):
                    at = (k * NQ + q) * R
                    ins = pe.transpose(sh.psum[:, 5, at:at + R], sco[:, q, k * P:(k + 1) * P],
                                       sh.ident[0:R, 0:R])
            ins.then_inc(S["at_mm"], 1)

            def attend(i, last):
                for s in (0, 1):
                    pe.wait_ge(S["va_lo"], 2 * i + s + 1)
                    for k in range(K):
                        for part in (vah, val):
                            ins = pe.matmul(sh.psum[:, s, :], part[:, s, k, :], GsT[:, k, :],
                                            start=(k == 0 and part is vah), stop=(k == K - 1 and part is val))
                    ins.then_inc(S["y_mm"], 1)
                wait(pe, S["o_add"], 2 * i)
                for s in (0, 1):
                    pe.wait_ge(S["y_lo"], 2 * i + s + 1)
                    for c in range(C):
                        cols = slice(c * P, (c + 1) * P)
                        ins = product(pe, sh.psum[:, 2 + s, cols], (ZH[:, s, cols], ZL[:, s, cols]),
                                      (WT[0][:, 2, :], WT[1][:, 2, :]))
                    ins.then_inc(S["o_mm"], 1)

            peeled(pe, NP, attend)


def diffusion_gnn_stack(nc, out, **d):
    sh = Shared()
    sh.NB, sh.N, sh.D = d["x"].shape
    sh.C = sh.N // P
    assert sh.D == P and sh.NB % QB == 0 and sh.N == 512
    with ExitStack() as ctx:
        ctx.enter_context(nc.allow_non_contiguous_dma(reason="a few hundred elements of columns"))
        sb, _ = allocators(nc, ctx)
        sh.X = sb("X", [P, sh.C, sh.NB, sh.D])
        sh.ident = sb("ident", [P, P])
        sh.HALF, sh.PER_D, sh.QUARTER, sh.EPS, sh.ROOT = range(5)
        sh.const_values = (0.5, 1.0 / sh.D, 0.25, EPS, -0.5)
        sh.const = sb("const", [P, len(sh.const_values), sh.C * QB])
        sh.psum = ctx.enter_context(nc.psum_tensor("psum", [P, 8, 512], F32))
        sh.A = sb("A", [P, sh.C, sh.N])
        with ExitStack() as early:
            esb, _ = allocators(nc, early)
            sh.bias0 = esb("bias0", [P, sh.C, sh.D])
            sh.LT = [(esb(f"LT{r}h", [P, sh.C, sh.N], F32R), esb(f"LT{r}l", [P, sh.C, sh.N], F32R))
                     for r in range(BABY)]
            sh.E = (esb("Eh", [P, BABY, NCO // BABY, sh.D], F32R), esb("El", [P, BABY, NCO // BABY, sh.D], F32R))
            phase_operators(nc, sh, d)
            phase_diffusion(nc, sh, d)

        phase_recurrent(nc, sh, d)
        phase_batchnorm(nc, sh, d)
        phase_attention(nc, sh, d, out)


OUTPUT_SHAPE = (16, 512, 128)


def kernel(**inputs):
    import numpy as np
    import concourse.bacc as bacc
    from concourse.bass_utils import run_bass_kernel_spmd

    nc = bacc.Bacc("TRN2", target_bir_lowering=False, num_devices=1)
    arrays, tensors = {}, {}
    for name, value in inputs.items():
        a = np.ascontiguousarray(value)
        arrays[f"in_{name}"] = a
        tensors[name] = nc.dram_tensor(f"in_{name}", a.shape, mybir.dt.from_np(a.dtype), kind="ExternalInput").ap()
    out = nc.dram_tensor("out", OUTPUT_SHAPE, F32, kind="ExternalOutput").ap()
    diffusion_gnn_stack(nc, out, **tensors)
    results = run_bass_kernel_spmd(nc, [arrays], core_ids=[0])
    return results.results[0]["out"]
```

```python
import math
from contextlib import ExitStack

import concourse.bass as bass
from concourse import mybir

ALU = mybir.AluOpType
ACT = mybir.ActivationFunctionType
AX = mybir.AxisListType
F32 = mybir.dt.float32
F32R = mybir.dt.float32r
I32 = mybir.dt.int32

P = 128
EPS = 1e-5
N_STEPS = 8
DT = 1.0 / N_STEPS
BABY = 3
NCO = N_STEPS + 1
MAX_SKIP = 4
QB = 4
LOWEST = -3.0e38


def binom(n, k):
    return float(math.comb(n, k))


class Shared:
    pass


def wait(eng, sem, value):
    if not isinstance(value, int) or value > 0:
        eng.wait_ge(sem, value)


def peeled(eng, n, step):
    step(0, n == 1)
    if n > 2:
        with eng.Fori(1, n - 1) as i:
            step(i, False)
    if n > 1:
        step(n - 1, True)


def product(pe, out, lhs, rhs, start=True, stop=True):
    pe.matmul(out, lhs[0], rhs[0], start=start, stop=False)
    pe.matmul(out, lhs[0], rhs[1], start=False, stop=False)
    return pe.matmul(out, lhs[1], rhs[0], start=False, stop=stop)


def low_part(eng, out, full, high):
    return eng.tensor_tensor(out, full, high.bitcast(F32), ALU.subtract)


def allocators(nc, ctx):
    def sb(name, shape, dt=F32):
        return ctx.enter_context(nc.sbuf_tensor(name, shape, dt))

    def sem(name):
        return ctx.enter_context(nc.semaphore(name))

    return sb, sem


def phase_operators(nc, sh, d):
    C, D, N = sh.C, sh.D, sh.N
    with ExitStack() as ctx:
        sb, sem = allocators(nc, ctx)
        w_nat = sb("w_nat", [P, D])
        wT = sb("wT", [P, D])
        wTd = sb("wTd", [P, D])
        fcw = sb("fcw", [P, D])
        dcol = sb("dcol", [P, 1])
        dclip = sb("dclip", [P, 1])
        bcol = sb("bcol", [P, 1])
        alpha = sb("alpha", [P, C])
        gate = sb("gate", [P, C])
        kappa = sb("kappa", [P, C])
        ldiag = sb("ldiag", [P, C])
        L = sb("L", [P, C, N])
        Lh = sb("Lh", [P, C, N], F32R)
        Ll = sb("Ll", [P, C, N], F32R)
        RP = sb("RP", [P, NCO, D])
        Ef = sb("Ef", [P, NCO, D])
        bsel = sb("bsel", [P, NCO, NCO])
        V = sb("V", [NCO, D])
        U = sb("U", [P, C, NCO])
        UT = sb("UT", [NCO, C, P])
        names = ("w_in", "fc_in", "a_in", "small_in", "x_in", "idn", "memsets", "pe_tile", "dve_tile",
                 "hi_done", "gate_done", "l_done", "lh_done", "ll_done", "own", "bsel_done", "eh_done", "e_done")
        S = {n: sem(n) for n in names}

        order = (["wT"] + ["R"] + [f"LT{j}" for j in range(C)] + ["R2", "R34", "R58", "FR03", "FR47", "FR8V"]
                 + [f"L2T{j}" for j in range(C)] + [f"L3T{j}" for j in range(C)]
                 + ["U13", "U46", "U78", "UT", "BIAS"])
        at = {n: i for i, n in enumerate(order)}
        his = [f"LT{j}" for j in range(C)] + [f"L2T{j}" for j in range(C)] + [f"L3T{j}" for j in range(C)]

        def bank(name):
            return sh.psum[:, at[name] % 8, :]

        block = ctx.enter_context(nc.Block())

        @block.sync
        def _(sp):
            sp.dma_start(w_nat[:, :], d["L0_gnn_w"]).then_inc(S["w_in"], 16)
            sp.dma_start(sh.A[:, :, :], d["adj"].rearrange("(c p) m -> p c m", p=P)).then_inc(S["a_in"], 16)
            xv = d["x"].rearrange("b (c p) d -> p c b d", p=P)
            for q in range(sh.NB // QB):
                for c in range(C):
                    sp.dma_start(sh.X[:, c, q * QB:(q + 1) * QB, :], xv[:, c, q * QB:(q + 1) * QB, :])\
                        .then_inc(S["x_in"], 16)
            sp.wait_ge(S["x_in"], 16 * C * (sh.NB // QB))

        @block.gpsimd
        def _(pool):
            pool.memset(sh.ident[:, :], 0.0).then_inc(S["memsets"], 1)
            pool.memset(bsel[:, :, :], 0.0).then_inc(S["memsets"], 1)
            pool.memset(U[:, :, 0:1], 1.0).then_inc(S["memsets"], 1)
            pool.wait_ge(S["memsets"], 1)
            pool.affine_select(out=sh.ident[:, :], in_=sh.ident[:, :], compare_op=ALU.not_equal, fill=1.0,
                               base=0, pattern=[[-1, P]], channel_multiplier=1).then_inc(S["idn"], 1)
            for k, value in enumerate(sh.const_values):
                pool.memset(sh.const[:, k, :], value).then_inc(S["memsets"], 1)

        @block.scalar
        def _(act):
            act.dma_start(alpha[:, :], d["L0_gnn_alpha_train"].rearrange("(c p) -> p c", p=P))\
                .then_inc(S["small_in"], 16)
            act.dma_start(dcol[:, :], d["L0_gnn_d"].rearrange("(p o) -> p o", o=1)).then_inc(S["small_in"], 16)
            act.dma_start(bcol[:, :], d["L0_gnn_fc_in_b"].rearrange("(p o) -> p o", o=1))\
                .then_inc(S["small_in"], 16)
            act.dma_start(fcw[:, :], d["L0_gnn_fc_in_w"]).then_inc(S["fc_in"], 16)
            act.wait_ge(S["small_in"], 48)
            act.activation(gate[:, :], alpha[:, :], ACT.Sigmoid).then_inc(S["gate_done"], 1)
            for c in range(C):
                act.wait_ge(S["l_done"], c + 1)
                act.activation(Lh[:, c, :], L[:, c, :], ACT.Copy).then_inc(S["lh_done"], 1)
            for k, name in enumerate(his):
                act.wait_ge(S["pe_tile"], at[name] + 1)
                act.activation(sh.LT[k // C][0][:, k % C, :], bank(name), ACT.Copy).then_inc(S["hi_done"], 1)
                if name == f"L2T{C - 1}":
                    act.wait_ge(S["e_done"], 1)
                    act.activation(sh.E[0][:, :, :, :], Ef[:, :, :].rearrange("p (i r) d -> p r i d", r=BABY),
                                   ACT.Copy).then_inc(S["eh_done"], 1)

        @block.vector
        def _(dve):
            chain = [0]

            def link(ins):
                chain[0] += 1
                ins.then_inc(S["own"], 1)
                dve.wait_ge(S["own"], chain[0])

            def tile(name):
                dve.wait_ge(S["pe_tile"], at[name] + 1)

            dve.wait_ge(S["gate_done"], 1)
            link(dve.tensor_scalar(kappa[:, :], gate[:, :], 0.5 * DT, None, ALU.mult))
            dve.tensor_scalar(dclip[:, :], dcol[:, :], 0.0, 1.0, ALU.max, ALU.min)
            link(dve.tensor_scalar(ldiag[:, :], kappa[:, :], -1.0, 1.0 - DT, ALU.mult, ALU.add))
            tile("wT")
            link(dve.tensor_copy(wT[:, :], bank("wT")[:, 0:D]))
            dve.tensor_scalar(wTd[:, :], wT[:, :], dclip[:, 0:1], DT, ALU.mult, ALU.mult)\
                .then_inc(S["dve_tile"], 1)
            dve.wait_ge(S["a_in"], 16)
            dve.wait_ge(S["idn"], 1)
            for c in range(C):
                link(dve.tensor_scalar(L[:, c, :], sh.A[:, c, :], kappa[:, c:c + 1], None, ALU.mult))
                own = L[:, c, c * P:(c + 1) * P]
                dve.scalar_tensor_tensor(own, sh.ident[:, :], ldiag[:, c:c + 1], own, ALU.mult, ALU.add)\
                    .then_inc(S["l_done"], 1)
            for c in range(C):
                dve.wait_ge(S["lh_done"], c + 1)
                low_part(dve, Ll[:, c, :], L[:, c, :], Lh[:, c, :]).then_inc(S["ll_done"], 1)
            tile("R")
            dve.tensor_copy(RP[:, 0, :], sh.ident[:, :])
            dve.tensor_copy(RP[:, 1, :], bank("R")[:, 0:D]).then_inc(S["dve_tile"], 1)

            def split(k, name):
                dve.wait_ge(S["hi_done"], k + 1)
                low_part(dve, sh.LT[k // C][1][:, k % C, :], bank(name), sh.LT[k // C][0][:, k % C, :])\
                    .then_inc(S["dve_tile"], 1)

            for k in range(C):
                split(k, his[k])
            tile("R2")
            dve.tensor_copy(RP[:, 2, :], bank("R2")[:, 0:D]).then_inc(S["dve_tile"], 1)
            tile("R34")
            dve.tensor_copy(RP[:, 3:5, :], bank("R34")[:, 0:2 * D].rearrange("p (k d) -> p k d", d=D))\
                .then_inc(S["dve_tile"], 1)
            tile("R58")
            dve.tensor_copy(RP[:, 5:9, :], bank("R58").rearrange("p (k d) -> p k d", d=D))\
                .then_inc(S["dve_tile"], 1)
            dve.wait_ge(S["memsets"], 3)
            for j in range(NCO):
                ins = dve.tensor_scalar(bsel[:, j, j:j + 1], bcol[:, 0:1], binom(N_STEPS, j), None, ALU.mult)
            ins.then_inc(S["bsel_done"], 1)
            for name, k0, n in (("FR03", 0, 4), ("FR47", 4, 4), ("FR8V", 8, 1)):
                tile(name)
                for k in range(n):
                    j = N_STEPS - k0 - k
                    ins = dve.tensor_scalar(Ef[:, j, :], bank(name)[:, k * D:(k + 1) * D], binom(N_STEPS, j),
                                            None, ALU.mult)
                if name == "FR8V":
                    ins = dve.tensor_copy(V[:, :], bank(name)[0:NCO, D:2 * D])
                ins.then_inc(S["dve_tile"], 1)
                chain_base = at[name] + 1
            dve.wait_ge(S["dve_tile"], chain_base)
            for i in range(N_STEPS):
                for j in range(N_STEPS - i):
                    ins = dve.scalar_tensor_tensor(Ef[:, j, :], RP[:, i, :], DT * binom(i + j, j), Ef[:, j, :],
                                                   ALU.mult, ALU.add)
                if i < N_STEPS - 1:
                    link(ins)
            ins.then_inc(S["e_done"], 1)
            for k in range(C, 2 * C):
                split(k, his[k])
            dve.wait_ge(S["eh_done"], 1)
            low_part(dve, sh.E[1][:, :, :, :], Ef[:, :, :].rearrange("p (i r) d -> p r i d", r=BABY),
                     sh.E[0][:, :, :, :])
            for k in range(2 * C, 3 * C):
                split(k, his[k])
            tile("U13")
            dve.tensor_copy(U[:, :, 1:4], bank("U13")[:, 0:3 * C].rearrange("p (c j) -> p c j", j=3))\
                .then_inc(S["dve_tile"], 1)
            tile("U46")
            dve.tensor_copy(U[:, :, 4:7], bank("U46")[:, 0:3 * C].rearrange("p (c j) -> p c j", j=3))\
                .then_inc(S["dve_tile"], 1)
            tile("U78")
            dve.tensor_copy(U[:, :, 7:9], bank("U78")[:, 0:2 * C].rearrange("p (c j) -> p c j", j=2))\
                .then_inc(S["dve_tile"], 1)
            tile("UT")
            dve.tensor_copy(UT[:, :, :], bank("UT")[0:NCO, :].rearrange("p (c n) -> p c n", n=P))\
                .then_inc(S["dve_tile"], 1)
            tile("BIAS")
            dve.tensor_copy(sh.bias0[:, :, :], bank("BIAS").rearrange("p (c d) -> p c d", d=D))\
                .then_inc(S["dve_tile"], 1)

        @block.tensor
        def _(pe):
            def begin(name, needs=()):
                upto = max([at[name] - 7] + [at[n] + 1 for n in needs])
                if upto > 0:
                    pe.wait_ge(S["dve_tile"], upto)

            def done(ins):
                ins.then_inc(S["pe_tile"], 1)

            pe.wait_ge(S["w_in"], 16)
            pe.wait_ge(S["idn"], 1)
            done(pe.transpose(bank("wT")[:, 0:D], w_nat[:, :], sh.ident[:, :]))
            begin("R", ["wT"])
            done(pe.matmul(bank("R")[:, 0:D], wTd[:, :], wT[:, :], start=True, stop=True))
            pe.wait_ge(S["l_done"], C)
            for j in range(C):
                for c in range(C):
                    ins = pe.transpose(bank(f"LT{j}")[:, c * P:(c + 1) * P], L[:, c, j * P:(j + 1) * P],
                                       sh.ident[:, :])
                done(ins)
            begin("R2", ["R"])
            done(pe.matmul(bank("R2")[:, 0:D], RP[:, 1, :], RP[:, 1, :], start=True, stop=True))
            begin("R34", ["R2"])
            done(pe.matmul(bank("R34")[:, 0:2 * D], RP[:, 2, :], RP[:, 1:3, :], start=True, stop=True))
            begin("R58", ["R34"])
            done(pe.matmul(bank("R58"), RP[:, 4, :], RP[:, 1:5, :], start=True, stop=True))
            begin("FR03", ["R58"])
            pe.wait_ge(S["fc_in"], 16)
            done(pe.matmul(bank("FR03"), fcw[:, :], RP[:, 0:4, :], start=True, stop=True))
            begin("FR47")
            done(pe.matmul(bank("FR47"), fcw[:, :], RP[:, 4:8, :], start=True, stop=True))
            begin("FR8V")
            pe.matmul(bank("FR8V")[:, 0:D], fcw[:, :], RP[:, 8, :], start=True, stop=True)
            pe.wait_ge(S["bsel_done"], 1)
            for j in range(NCO):
                ins = pe.matmul(bank("FR8V")[0:NCO, D:2 * D], bsel[:, j, :], RP[:, N_STEPS - j, :],
                                start=(j == 0), stop=(j == NCO - 1))
            done(ins)
            pe.wait_ge(S["ll_done"], C)
            for r in (2, 3):
                for j in range(C):
                    begin(f"L{r}T{j}", [f"LT{C - 1}" if r == 2 else f"L2T{C - 1}"])
                    for k in range(C):
                        rows = slice(j * P, (j + 1) * P)
                        ins = product(pe, bank(f"L{r}T{j}"), (Lh[:, k, rows], Ll[:, k, rows]),
                                      (sh.LT[r - 2][0][:, k, :], sh.LT[r - 2][1][:, k, :]),
                                      start=(k == 0), stop=(k == C - 1))
                    done(ins)

            def powers(name, lts, u, n):
                for c2 in range(C):
                    for r, (hi, lo) in enumerate(lts):
                        for k in range(C):
                            o = bank(name)[:, c2 * len(lts) * n + r * n:c2 * len(lts) * n + (r + 1) * n]
                            cols = slice(c2 * P, (c2 + 1) * P)
                            pe.matmul(o, hi[:, k, cols].bitcast(F32), U[:, k, u:u + n], start=(k == 0),
                                      stop=False)
                            ins = pe.matmul(o, lo[:, k, cols].bitcast(F32), U[:, k, u:u + n], start=False,
                                            stop=(k == C - 1))
                done(ins)

            begin("U13", [f"L3T{C - 1}"])
            powers("U13", sh.LT, 0, 1)
            begin("U46", ["U13"])
            powers("U46", sh.LT[2:], 1, 3)
            begin("U78", ["U46"])
            powers("U78", sh.LT[2:], 4, 2)
            begin("UT", ["U78"])
            for c in range(C):
                ins = pe.transpose(bank("UT")[0:NCO, c * P:(c + 1) * P], U[:, c, :], sh.ident[:, :])
            done(ins)
            begin("BIAS", ["UT"])
            for c in range(C):
                ins = pe.matmul(bank("BIAS")[:, c * D:(c + 1) * D], UT[:, c, :], V[:, :], start=True, stop=True)
            done(ins)


def norm_stats(dve, stats, rows):
    for b in range(rows.shape[1]):
        ins = dve.bn_stats(stats[:, b, :], rows[:, b, :])
    return ins


NORM_LINKS = 5
SHIFT_LINKS = 6


def norm_scales(pool, sh, n, stats, work, mean, rstd, own, before, shift=None):
    a, b, c = (work[:, k, 0:n] for k in range(3))

    def const(k):
        return sh.const[:, k, 0:n]

    def link(k, ins):
        ins.then_inc(own, 1)
        pool.wait_ge(own, before + k)

    pool.tensor_tensor(a, stats[:, :, 1], stats[:, :, 4], ALU.add)
    pool.tensor_tensor(b, stats[:, :, 1], stats[:, :, 4], ALU.subtract)
    link(1, pool.tensor_tensor(c, stats[:, :, 2], stats[:, :, 5], ALU.add))
    pool.tensor_tensor(mean, a, const(sh.HALF), ALU.mult)
    pool.tensor_tensor(c, c, const(sh.PER_D), ALU.mult)
    link(2, pool.tensor_tensor(b, b, b, ALU.mult))
    link(3, pool.tensor_tensor(b, b, const(sh.QUARTER), ALU.mult))
    link(4, pool.tensor_tensor(b, b, c, ALU.add))
    link(5, pool.tensor_tensor(b, b, const(sh.EPS), ALU.add))
    if shift is None:
        return pool.tensor_tensor(rstd, b, const(sh.ROOT), ALU.pow)
    pool.tensor_tensor(mean, mean, const(sh.MINUS), ALU.mult)
    link(6, pool.tensor_tensor(rstd, b, const(sh.ROOT), ALU.pow))
    return pool.tensor_tensor(shift, mean, rstd, ALU.mult)


class NormBuffers:

    def __init__(self, sb, sh):
        self.sh = sh
        self.rows = QB * sh.C
        self.stats = sb("nstats", [P, sh.NB * sh.C, 6])
        self.work = sb("nwork", [P, 3, self.rows])
        self.mean = sb("nmean", [P, self.rows])
        self.scale = sb("nscale", [P, self.rows])
        self.shift = sb("nshift", [P, self.rows])

    def take_stats(self, dve, n):
        C = self.sh.C
        for c in range(C):
            ins = dve.bn_stats(self.stats[:, bass.ds(C * n + c, 1), :], self.sh.X[:, c, bass.ds(n, 1), :])
        return ins

    def scales(self, pool, g, own, before):
        return norm_scales(pool, self.sh, self.rows, self.stats[:, bass.ds(self.rows * g, self.rows), :],
                           self.work, self.mean[:, :], self.scale[:, :], own, before, self.shift[:, :])

    def apply(self, act, n, b):
        C = self.sh.C
        for c in range(C):
            k = b * C + c
            row = self.sh.X[:, c, bass.ds(n, 1), :]
            ins = act.activation(row, row, ACT.Identity, bias=self.shift[:, k:k + 1], scale=self.scale[:, k:k + 1])
        return ins


def phase_diffusion(nc, sh, d):
    C, D, N = sh.C, sh.D, sh.N
    NQ = sh.NB // QB
    with ExitStack() as ctx:
        sb, sem = allocators(nc, ctx)
        Xh = sb("Xh", [P, C, QB, D], F32R)
        Xl = sb("Xl", [P, C, QB, D], F32R)
        yh = sb("yh", [P, 2, BABY, N], F32R)
        yl = sb("yl", [P, 2, BABY, N], F32R)
        B2h = sb("B2h", [P, C, QB, D], F32R)
        B2l = sb("B2l", [P, C, QB, D], F32R)
        B01 = sb("B01", [P, C, QB, 2, D])
        tq = sb("tq", [P, C, QB, D])
        th = sb("th", [P, C, QB, D], F32R)
        tl = sb("tl", [P, C, QB, D], F32R)
        stats = sb("stats", [P, C * QB, 6])
        work3 = sb("work3", [P, 3, C * QB])
        mean = sb("mean", [P, C * QB])
        rstd = sb("rstd", [P, C * QB])
        names = ("pe_tile", "dve_tile", "hi_done", "xh_done", "xl_done", "xb_done", "th_done", "tl_done",
                 "sum2", "stat_done", "norm_own", "rstd_done", "x1_done")
        S = {n: sem("d_" + n) for n in names}

        work = [("B", 0), ("Y", 2), ("B", 1), ("Y", 3), ("B", 2), ("B", 3), ("Y+", 0), ("T", 0), ("Y+", 1),
                ("S", 0)]
        TILES = 4 * len(work)
        HEAD = 8
        HIS = {"Y": 3, "Y+": 3, "B": 4, "T": 0, "S": 0}
        HI_QUAD = sum(HIS[k] for k, _ in work)
        HI_HEAD = 6

        def steps(g, last):
            hi = 0
            for i, (kind, b) in enumerate(work):
                if not (last and kind == "Y+"):
                    skipped = sum(k == "Y+" for k, _ in work[:i]) if last else 0
                    yield kind, b, HEAD + g * TILES + 4 * (i - skipped), 4 * (i - skipped) % 8, \
                        HI_HEAD + g * HI_QUAD + hi
                    hi += HIS[kind]

        block = ctx.enter_context(nc.Block())

        def ready(eng, n, k):
            eng.wait_ge(S["pe_tile"], n + k + 1)

        @block.tensor
        def _(pe):
            def free(n, k, first=False):
                if not first:
                    pe.wait_ge(S["dve_tile"], n + k - 7)

            def Y(b, n, bk, first=False):
                for k in range(4):
                    free(n, k, first)
                    o = sh.psum[:, bk + k, :]
                    if k < 2:
                        src = (Xh, Xl)[k]
                        for c in range(C):
                            ins = pe.transpose(o[:, c * P:(c + 1) * P], src[:, c, b, :].bitcast(F32),
                                               sh.ident[:, :])
                    else:
                        for c in range(C):
                            ins = product(pe, o, (Xh[:, c, b, :], Xl[:, c, b, :]),
                                          (sh.LT[k - 2][0][:, c, :], sh.LT[k - 2][1][:, c, :]),
                                          start=(c == 0), stop=(c == C - 1))
                    ins.then_inc(S["pe_tile"], 1)

            def B(b, n, bk, y_end):
                pe.wait_ge(S["dve_tile"], y_end)
                for c in range(C):
                    free(n, c)
                    cols = slice(c * P, (c + 1) * P)
                    for r in range(BABY):
                        ins = product(pe, sh.psum[:, bk + c, 0:BABY * D],
                                      (yh[:, b % 2, r, cols], yl[:, b % 2, r, cols]),
                                      (sh.E[0][:, r, :, :], sh.E[1][:, r, :, :]),
                                      start=(r == 0), stop=(r == BABY - 1))
                    ins.then_inc(S["pe_tile"], 1)

            def horner(n, bk, hi, lo):
                for c2 in range(C):
                    free(n, c2)
                    cols = slice(c2 * P, (c2 + 1) * P)
                    for c in range(C):
                        ins = product(pe, sh.psum[:, bk + c2, :],
                                      (sh.LT[2][0][:, c, cols], sh.LT[2][1][:, c, cols]),
                                      (hi[:, c, :, :], lo[:, c, :, :]), start=(c == 0), stop=(c == C - 1))
                    ins.then_inc(S["pe_tile"], 1)

            def quad(g, last):
                start = HEAD + g * TILES
                y_end = {0: start - 4, 1: start}
                for kind, b, n, bk, _ in steps(g, last):
                    if kind in ("Y", "Y+"):
                        if kind == "Y+" and b == 0:
                            pe.wait_ge(S["xl_done"], C * (g + 2))
                        Y(b, n, bk)
                        y_end[b] = n + 4
                    elif kind == "B":
                        B(b, n, bk, y_end[b])
                        b_end = n + 4
                    elif kind == "T":
                        pe.wait_ge(S["dve_tile"], b_end)
                        horner(n, bk, B2h, B2l)
                    else:
                        pe.wait_ge(S["tl_done"], C * (g + 1))
                        horner(n, bk, th, tl)

            pe.wait_ge(S["xl_done"], C)
            Y(0, 0, 0, first=True)
            Y(1, 4, 4, first=True)
            with pe.Fori(0, NQ - 1) as g:
                quad(g, False)
            quad(NQ - 1, True)

        @block.scalar
        def _(act):
            def split_x(g):
                for c in range(C):
                    act.activation(Xh[:, c, :, :], sh.X[:, c, bass.ds(QB * g, QB), :], ACT.Copy)\
                        .then_inc(S["xh_done"], 1)

            def Y(b, n, bk):
                for k, r in ((0, 0), (2, 1), (3, 2)):
                    ready(act, n, k)
                    act.activation(yh[:, b % 2, r, :], sh.psum[:, bk + k, :], ACT.Copy)\
                        .then_inc(S["hi_done"], 1)

            def quad(g, last):
                for kind, b, n, bk, _ in steps(g, last):
                    if kind in ("Y", "Y+"):
                        Y(b, n, bk)
                        if kind == "Y" and b == QB - 1 and not last:
                            split_x(g + 1)
                    elif kind == "B":
                        if b == 0:
                            act.wait_ge(S["dve_tile"], n)
                        for c in range(C):
                            ready(act, n, c)
                            act.activation(B2h[:, c, b, :], sh.psum[:, bk + c, 2 * D:3 * D], ACT.Copy)
                            act.activation(B01[:, c, b, :, :],
                                           sh.psum[:, bk + c, 0:2 * D].rearrange("p (i d) -> p i d", d=D),
                                           ACT.Copy).then_inc(S["hi_done"], 1)
                    elif kind == "T":
                        for c in range(C):
                            act.wait_ge(S["dve_tile"], n + c + 1)
                            act.activation(th[:, c, :, :], tq[:, c, :, :], ACT.Copy).then_inc(S["th_done"], 1)

            split_x(0)
            Y(0, 0, 0)
            Y(1, 4, 4)
            with act.Fori(0, NQ - 1) as g:
                quad(g, False)
            quad(NQ - 1, True)

        @block.vector
        def _(dve):
            def Y(b, n, bk, hi):
                dve.wait_ge(S["hi_done"], hi + 1)
                ready(dve, n, 1)
                dve.tensor_copy(yl[:, b % 2, 0, :], sh.psum[:, bk + 1, :]).then_inc(S["dve_tile"], 2)
                for k in (2, 3):
                    dve.wait_ge(S["hi_done"], hi + k)
                    low_part(dve, yl[:, b % 2, k - 1, :], sh.psum[:, bk + k, :], yh[:, b % 2, k - 1, :])\
                        .then_inc(S["dve_tile"], 1)

            def quad(g, last):
                for kind, b, n, bk, hi in steps(g, last):
                    if kind in ("Y", "Y+"):
                        Y(b, n, bk, hi)
                    elif kind == "B":
                        for c in range(C):
                            dve.wait_ge(S["hi_done"], hi + c + 1)
                            low_part(dve, B2l[:, c, b, :], sh.psum[:, bk + c, 2 * D:3 * D], B2h[:, c, b, :])\
                                .then_inc(S["dve_tile"], 1)
                    elif kind == "T":
                        for c in range(C):
                            ready(dve, n, c)
                            dve.tensor_tensor(tq[:, c, :, :],
                                              sh.psum[:, bk + c, :].rearrange("p (b d) -> p b d", d=D),
                                              B01[:, c, :, 1, :], ALU.add).then_inc(S["dve_tile"], 1)
                    else:
                        for c in range(C):
                            ready(dve, n, c)
                            dve.tensor_tensor(tq[:, c, :, :],
                                              sh.psum[:, bk + c, :].rearrange("p (b d) -> p b d", d=D),
                                              B01[:, c, :, 0, :], ALU.add).then_inc(S["dve_tile"], 1)
                            if c == 0:
                                dve.wait_ge(S["xb_done"], C * (g + 1))
                            dve.wait_ge(S["dve_tile"], n + c + 1)
                            dve.tensor_tensor(tq[:, c, :, :], tq[:, c, :, :],
                                              sh.X[:, c, bass.ds(QB * g, QB), :], ALU.add)\
                                .then_inc(S["sum2"], 1)
                            dve.wait_ge(S["sum2"], C * g + c + 1)
                            norm_stats(dve, stats[:, c * QB:(c + 1) * QB, :], tq[:, c, :, :])\
                                .then_inc(S["stat_done"], 1)
                        dve.wait_ge(S["rstd_done"], g + 1)
                        for c in range(C):
                            for b in range(QB):
                                ins = dve.tensor_scalar(sh.X[:, c, bass.ds(QB * g + b, 1), :],
                                                        tq[:, c, b:b + 1, :], mean[:, c * QB + b:c * QB + b + 1],
                                                        rstd[:, c * QB + b:c * QB + b + 1], ALU.subtract,
                                                        ALU.mult)
                        ins.then_inc(S["x1_done"], 1)

            Y(0, 0, 0, 0)
            Y(1, 4, 4, 3)
            with dve.Fori(0, NQ - 1) as g:
                quad(g, False)
            quad(NQ - 1, True)

        @block.gpsimd
        def _(pool):
            def split_x(g):
                for c in range(C):
                    pool.wait_ge(S["xh_done"], C * g + c + 1)
                    low_part(pool, Xl[:, c, :, :], sh.X[:, c, bass.ds(QB * g, QB), :], Xh[:, c, :, :])\
                        .then_inc(S["xl_done"], 1)

            def quad(g, last):
                pool.wait_ge(S["xl_done"], C * (g + 1))
                for c in range(C):
                    xq = sh.X[:, c, bass.ds(QB * g, QB), :]
                    pool.tensor_tensor(xq, xq, sh.bias0[:, c:c + 1, :].broadcast_to([P, QB, D]), ALU.add)\
                        .then_inc(S["xb_done"], 1)
                if not last:
                    split_x(g + 1)
                for c in range(C):
                    pool.wait_ge(S["th_done"], C * g + c + 1)
                    low_part(pool, tl[:, c, :, :], tq[:, c, :, :], th[:, c, :, :]).then_inc(S["tl_done"], 1)
                pool.wait_ge(S["stat_done"], C * (g + 1))
                norm_scales(pool, sh, C * QB, stats, work3, mean[:, :], rstd[:, :], S["norm_own"],
                            NORM_LINKS * g).then_inc(S["rstd_done"], 1)

            split_x(0)
            with pool.Fori(0, NQ - 1) as g:
                quad(g, False)
            quad(NQ - 1, True)


def phase_recurrent(nc, sh, d):
    C, D, N = sh.C, sh.D, sh.N
    NQ = sh.NB // QB
    I, F, G, O = range(4)
    with ExitStack() as ctx:
        sb, sem = allocators(nc, ctx)
        AT = (sb("ATh", [P, C, N], F32R), sb("ATl", [P, C, N], F32R))
        ATh, ATl = AT
        Wg = [sb(f"Wg{i}", [P, D]) for i in (0, 1)]
        Wgs = [(sb(f"Wg{i}h", [P, D], F32R), sb(f"Wg{i}l", [P, D], F32R)) for i in (0, 1)]
        bg0 = sb("bg0", [P, D])
        bg1 = sb("bg1", [P, 1])
        WI = (sb("WIh", [P, MAX_SKIP, 4, D], F32R), sb("WIl", [P, MAX_SKIP, 4, D], F32R))
        WH = (sb("WHh", [P, MAX_SKIP - 1, 4, D], F32R), sb("WHl", [P, MAX_SKIP - 1, 4, D], F32R))
        bi = sb("bi", [P, MAX_SKIP, 4])
        bh = sb("bh", [P, MAX_SKIP, 4])
        gbias = sb("gbias", [P, MAX_SKIP, 4])
        ones = sb("ones", [P, P])
        rs = sb("rs", [P, C])
        diag = sb("diag", [P, C, P])
        RB0 = sb("RB0", [P, C, D])
        RB1 = sb("RB1", [P, N])
        Xh = sb("rXh", [P, C, QB, D], F32R)
        Xl = sb("rXl", [P, C, QB, D], F32R)
        ych = sb("ych", [P, 2, N], F32R)
        ycl = sb("ycl", [P, 2, N], F32R)
        u = sb("u", [P, 2, C, D])
        h1h = sb("h1h", [P, C, QB, D], F32R)
        h1l = sb("h1l", [P, C, QB, D], F32R)
        Hin = sb("Hin", [P, QB, N])
        Hq = sb("Hq", [P, QB, N])
        xh = sb("xh", [P, 2, N], F32R)
        xl = sb("xl", [P, 2, N], F32R)
        hh = sb("hh", [P, 2, N], F32R)
        hl = sb("hl", [P, 2, N], F32R)
        cell = sb("cell", [P, 2, N])
        gates = sb("gates", [P, 4, N])
        tc = sb("tc", [P, N])
        hn = sb("hn", [P, N])
        sq = sb("sq", [P, QB, C, D])
        stats = sb("rstats", [P, QB * C, 6])
        work3 = sb("rwork3", [P, 3, QB * C])
        mean = sb("rmean", [P, QB * C])
        rstd = sb("rrstd", [P, QB * C])
        names = ("w_in", "g_in", "ones_done", "set_mm", "set_free", "set_hi", "own", "gbias_done", "wg_hi", "wg_done", "rb_done",
                 "xh_done", "xl_done", "ring_mm", "ring_free", "conv_hi", "relu_done", "h1l_done",
                 "hq_done", "xs_done", "x_hi", "hs_done", "c_own", "c_own2", "c_done", "tanh_done", "h_done",
                 "stat_done", "norm_own", "rstd_done", "x2_done")
        S = {n: sem("r_" + n) for n in names}
        gate_mm = [sem(f"gate_mm_{n}") for n in "ifgo"]
        gate_act = [sem(f"gate_act_{n}") for n in "ifgo"]

        steps = [(1, 0, u_) for u_ in range(QB)]
        for p_ in range(2, MAX_SKIP + 1):
            steps += [(p_, t, s) for t in range(p_) for s in (0, 1)]
        NS = len(steps)
        FILL = [2, 2, 2, 2, 2, 3, 1, 5, 3, 3, 1, 0, 1, 3, 3, 2, 0, 0, 1, 1, 1, 0]
        REST = 1
        NF = sum(t > 0 for _, t, _ in steps)

        def view(p_, t, s, source=None):
            if p_ == 1:
                return (Hq if source is None else source)[:, s, :], N
            nw = N // p_
            return Hq[:, 2 * s:2 * s + 2, t:t + (nw - 1) * p_ + 1:p_], 2 * nw

        def like(ap, p_, n):
            return ap[..., 0:n] if p_ == 1 else ap[..., 0:n].rearrange("p (b w) -> p b w", b=2)

        def gates_of(t):
            return (G, I, O) if t == 0 else (G, I, F, O)

        def uses(k, gate):
            return sum(gate in gates_of(t) for _, t, _ in steps[:k])

        def y(layer, b):
            return [(f"Y{layer}", b, c) for c in range(C)]

        def w(layer, b):
            return [(f"W{layer}", b, None)]

        def relu_then(b, pieces):
            return pieces[:2] + [("relu", b, None)] + pieces[2:] + [("low", b, None)]

        conv = y(0, 0) + y(0, 1) + w(0, 0) + relu_then(0, y(0, 2) + w(0, 1)) + relu_then(1, y(0, 3) + w(0, 2)) \
            + relu_then(2, y(1, 0) + w(0, 3)) + relu_then(3, y(1, 1) + w(1, 0)) + y(1, 2) + w(1, 1) + y(1, 3) \
            + w(1, 2) + w(1, 3)

        def is_tile(kind, c):
            return kind[0] in "YWR" and c in (None, C - 1)

        def has_cost(item):
            return item[0][0] in "YW"

        def tiles_in(items):
            return sum(is_tile(kind, c) for kind, _, c in items)

        split_at = [i for i, item in enumerate(conv) if has_cost(item)][-REST]
        body, rest = conv[:split_at], conv[split_at:]
        CONV, BODY, RESID = tiles_in(conv), tiles_in(body), QB
        tile_order = [(kind, b) for kind, b, c in conv if is_tile(kind, c)]
        y_order = [(kind, b) for kind, b in tile_order if kind[0] == "Y"]

        def schedule(g, with_next, with_last):
            fill = [(*item, g) for item in rest] + ([(*item, g + 1) for item in body] if with_next else [])
            at = 0
            for k in range(NS):
                if with_last and k in (0, 1):
                    yield from [("R", b, None, g - 1) for b in ((0, 1) if k == 0 else (2, 3))]
                if with_last and k in (3, 6):
                    yield ("stats" if k == 3 else "norm", 0, None, g - 1)
                now = []
                pieces = 0
                while at < (len(fill) if k else len(rest)) and (pieces < FILL[k] or k == NS - 1 or not has_cost(fill[at])):
                    pieces += has_cost(fill[at])
                    now.append(fill[at])
                    at += 1
                yield ("X", k, None, g)
                if steps[k][1] > 0:
                    yield from now
                yield ("L", k, None, g)
                if steps[k][1] == 0:
                    yield from now

        def alone():
            return [(*item, 0) for item in body]

        def residual():
            return [("R", b, None, NQ - 1) for b in range(QB)]

        HS = sum(t < p_ - 1 for p_, t, _ in steps)

        def hs_before(k):
            return sum(t < p_ - 1 for p_, t, _ in steps[:k])

        def ring_base(g):
            if g is None:
                return 0
            if isinstance(g, int) and g in (0, NQ):
                return BODY if g == 0 else (CONV + RESID) * g - RESID
            return BODY - RESID + (CONV + RESID) * g

        def numbered(items, g):
            base = ring_base(g)
            n = base if isinstance(base, int) else BODY
            for kind, b, c, q in items:
                yield kind, b, c, q, base, 4 + n % 4
                if is_tile(kind, c):
                    n, base = n + 1, base + 1

        def y_tile(kind, b, g):
            return ring_base(g) - (BODY - tile_order.index(("Y" + kind[1], b)))

        block = ctx.enter_context(nc.Block())

        @block.sync
        def _(sp):
            sp.dma_start(Hq[:, :, :].rearrange("p k (g h) -> p k g h", g=4),
                         d["L1_gnn_Wih"].rearrange("k (g p) h -> p k g h", p=P)).then_inc(S["w_in"], 16)
            sp.dma_start(Hin[:, 0:MAX_SKIP - 1, :].rearrange("p k (g h) -> p k g h", g=4),
                         d["L1_gnn_Whh"][1:MAX_SKIP].rearrange("k (g p) h -> p k g h", p=P))\
                .then_inc(S["w_in"], 16)
            for i in (0, 1):
                sp.dma_start(Wg[i][:, :], d[f"L1_gnn_Wg{i}"]).then_inc(S["g_in"], 16)
            sp.dma_start(bg0[:, :], d["L1_gnn_bg0"].rearrange("(o h) -> o h", o=1).broadcast_to([P, D]))\
                .then_inc(S["g_in"], 16)
            sp.dma_start(bg1[:, :], d["L1_gnn_bg1"].rearrange("(h o) -> h o", o=1)).then_inc(S["g_in"], 16)
            sp.dma_start(bi[:, :, :], d["L1_gnn_bih"].rearrange("k (g p) -> p k g", p=P)).then_inc(S["g_in"], 16)
            sp.dma_start(bh[:, :, :], d["L1_gnn_bhh"].rearrange("k (g p) -> p k g", p=P)).then_inc(S["g_in"], 16)

        set_tiles = [("A", j) for j in range(C)] + [("WI", k) for k in range(MAX_SKIP)] \
            + [("WH", k) for k in range(MAX_SKIP - 1)] + [("rs", 0)]

        def set_target(kind, j, part):
            return {"A": AT[part], "WI": WI[part], "WH": WH[part]}[kind][:, j]

        def bank_like(n, kind):
            o = sh.psum[:, n % 8, :]
            return o if kind == "A" else o.rearrange("p (g h) -> p g h", g=4)

        @block.tensor
        def _(pe):
            for n, (kind, j) in enumerate(set_tiles):
                if n >= 8:
                    pe.wait_ge(S["set_free"], n - 7)
                if n == C:
                    pe.wait_ge(S["w_in"], 32)
                o = sh.psum[:, n % 8, :]
                if kind == "rs":
                    pe.wait_ge(S["ones_done"], 1)
                    ins = pe.matmul(o, ones[:, :], diag[:, :, :], start=True, stop=True)
                for c in range(4 if kind != "rs" else 0):
                    src = {"A": sh.A[:, c, j * P:(j + 1) * P],
                           "WI": Hq[:, j, c * P:(c + 1) * P], "WH": Hin[:, min(j, MAX_SKIP - 2), c * P:(c + 1) * P]}[kind]
                    ins = pe.transpose(o[:, c * P:(c + 1) * P], src, sh.ident[:, :])
                ins.then_inc(S["set_mm"], 1)
            pe.wait_ge(S["set_free"], len(set_tiles))
            pe.wait_ge(S["wg_done"], 1)

            def ring_item(kind, b, c, q, n, bk, y_at):
                o = sh.psum[:, bk, :]
                if kind == "R":
                    pe.wait_ge(S["h_done"], NS * q + NS - 1 + b // 2)
                if c in (None, 0):
                    wait(pe, S["ring_free"], n - 3)
                if kind[0] == "Y":
                    if kind == "Y0" and b == 0:
                        pe.wait_ge(S["xl_done"], C * q + c + 1)
                    if kind == "Y1" and c == 0:
                        pe.wait_ge(S["h1l_done"], QB * q + b + 1)
                    hi, lo = (Xh, Xl) if kind == "Y0" else (h1h, h1l)
                    ins = product(pe, o, (hi[:, c, b, :], lo[:, c, b, :]), (ATh[:, c, :], ATl[:, c, :]),
                                  start=(c == 0), stop=(c == C - 1))
                elif kind[0] == "W":
                    pe.wait_ge(S["ring_free"], y_at + 1)
                    if kind == "W0":
                        for j in range(C):
                            cols = slice(j * P, (j + 1) * P)
                            ins = product(pe, o[:, cols], (ych[:, b % 2, cols], ycl[:, b % 2, cols]),
                                          (Wgs[0][0][:, :], Wgs[0][1][:, :]))
                    else:
                        ins = product(pe, o, (Wgs[1][0][:, :], Wgs[1][1][:, :]), (ych[:, b % 2, :], ycl[:, b % 2, :]))
                else:
                    for j in range(C):
                        ins = pe.transpose(o[:, j * P:(j + 1) * P], Hq[:, b, j * P:(j + 1) * P], sh.ident[:, :])
                if is_tile(kind, c):
                    ins.then_inc(S["ring_mm"], 1)

            def from_input(k, g):
                p_, t, s = steps[k]
                n = view(p_, t, s)[1]
                pe.wait_ge(S["xs_done"], NS * g + k + 1)
                for gate in gates_of(t):
                    per = NF if gate == F else NS
                    wait(pe, gate_act[gate], per * g + uses(k, gate))
                    ins = product(pe, sh.psum[:, gate, 0:n], (WI[0][:, p_ - 1, gate, :], WI[1][:, p_ - 1, gate, :]),
                                  (xh[:, s % 2, 0:n], xl[:, s % 2, 0:n]), stop=(t == 0))
                    if t == 0:
                        ins.then_inc(gate_mm[gate], 1)

            def from_state(k, g):
                p_, t, s = steps[k]
                if t == 0:
                    return
                n = view(p_, t, s)[1]
                pe.wait_ge(S["hs_done"], HS * g + hs_before(k - 2) + 1)
                for gate in gates_of(t):
                    product(pe, sh.psum[:, gate, 0:n], (WH[0][:, p_ - 2, gate, :], WH[1][:, p_ - 2, gate, :]),
                            (hh[:, s % 2, 0:n], hl[:, s % 2, 0:n]), start=False).then_inc(gate_mm[gate], 1)

            def run(items, g):
                y_at = {}
                for kind, b, c, q, n, bk in numbered(items, g):
                    if kind == "X":
                        from_input(b, g)
                    elif kind == "L":
                        from_state(b, g)
                    elif kind[0] in "YWR":
                        if kind[0] == "Y":
                            y_at[kind, b] = n
                        of = None if kind[0] != "W" else \
                            y_at["Y" + kind[1], b] if ("Y" + kind[1], b) in y_at else y_tile(kind, b, g)
                        ring_item(kind, b, c, q, n, bk, of)

            run(alone(), None)
            run(schedule(0, True, False), 0)
            with pe.Fori(1, NQ - 1) as g:
                run(schedule(g, True, True), g)
            run(schedule(NQ - 1, False, True), NQ - 1)
            run(residual(), NQ)

        @block.scalar
        def _(act):
            for i in (0, 1):
                if i == 0:
                    act.wait_ge(S["g_in"], 96)
                act.activation(Wgs[i][0][:, :], Wg[i][:, :], ACT.Copy).then_inc(S["wg_hi"], 1)
            for n, (kind, j) in enumerate(set_tiles[:-1]):
                act.wait_ge(S["set_mm"], n + 1)
                act.activation(set_target(kind, j, 0), bank_like(n, kind), ACT.Copy).then_inc(S["set_hi"], 1)
            act.wait_ge(S["gbias_done"], 1)

            def split_x(q, c):
                act.activation(Xh[:, c, :, :], sh.X[:, c, bass.ds(QB * q, QB), :], ACT.Copy)\
                    .then_inc(S["xh_done"], 1)

            def just_made(k):
                return steps[k][0] == 1 and ("W1", k, None) in rest

            def split_h(k, g):
                p_, t, s = steps[k]
                hv, n = view(p_, t, s, Hin)
                if p_ == 1:
                    act.wait_ge(S["hq_done"], QB * g + s + 1)
                elif t == 0:
                    last = max(i for i in range(k) if steps[i][0] == p_ - 1
                               and (steps[i][2] == s if p_ > 2 else steps[i][2] // 2 == s))
                    act.wait_ge(S["h_done"], NS * g + last + 1)
                wait(act, gate_mm[O], NS * g + k - 1)
                act.activation(like(xh[:, s % 2, :], p_, n), hv, ACT.Copy).then_inc(S["x_hi"], 1)

            def lstm(k, g, with_next):
                p_, t, s = steps[k]
                n = view(p_, t, s)[1]
                late = k < NS - 1 and steps[k + 1][1] == 0 and steps[k + 1][0] > 1
                if k < NS - 1 and not late and not just_made(k + 1):
                    split_h(k + 1, g)
                elif k == NS - 1 and with_next:
                    split_h(0, g + 1)
                for gate in gates_of(t):
                    if late and gate == gates_of(t)[2]:
                        split_h(k + 1, g)
                    per = NF if gate == F else NS
                    act.wait_ge(gate_mm[gate], per * g + uses(k, gate) + 1)
                    wait(act, S["h_done" if gate == O else "c_done"], NS * g + k)
                    act.activation(gates[:, gate, 0:n], sh.psum[:, gate, 0:n],
                                   ACT.Tanh if gate == G else ACT.Sigmoid,
                                   bias=gbias[:, p_ - 1, gate:gate + 1]).then_inc(gate_act[gate], 1)
                act.wait_ge(S["c_done"], NS * g + k + 1)
                act.activation(tc[:, 0:n], cell[:, s % 2, 0:n], ACT.Tanh).then_inc(S["tanh_done"], 1)

            def run(items, g, with_next):
                u_at = {}
                for kind, b, c, q, n, bk in numbered(items, g):
                    if kind == "X" and just_made(b):
                        split_h(b, g)
                    elif kind == "L":
                        lstm(b, g, with_next)
                        if with_next and b < 2:
                            split_x(g + 1, 2 * b)
                            split_x(g + 1, 2 * b + 1)
                    elif kind[0] == "Y" and is_tile(kind, c):
                        act.wait_ge(S["ring_mm"], n + 1)
                        act.activation(ych[:, b % 2, :], sh.psum[:, bk, :], ACT.Copy).then_inc(S["conv_hi"], 1)
                    elif kind == "W0":
                        u_at[b] = n
                    elif kind == "relu":
                        act.wait_ge(S["ring_free"], u_at[b] + 1)
                        act.activation(h1h[:, :, b, :], u[:, b % 2, :, :], ACT.Relu).then_inc(S["relu_done"], 1)

            for c in range(C):
                split_x(0, c)
            run(alone(), None, True)
            split_h(0, 0)
            run(schedule(0, True, False), 0, True)
            with act.Fori(1, NQ - 1) as g:
                run(schedule(g, True, True), g, True)
            run(schedule(NQ - 1, False, True), NQ - 1, False)

        @block.vector
        def _(dve):
            for c in range(C):
                ins = dve.reduce_sum(rs[:, c:c + 1], sh.A[:, c, :], AX.X)
            ins.then_inc(S["own"], 1)
            dve.memset(ones[:, :], 1.0)
            dve.wait_ge(S["own"], 1)
            for c in range(C):
                ins = dve.tensor_scalar(diag[:, c, :], sh.ident[:, :], rs[:, c:c + 1], None, ALU.mult)
            ins.then_inc(S["ones_done"], 1)
            dve.wait_ge(S["g_in"], 96)
            dve.tensor_tensor(gbias[:, :, :], bi[:, :, :], bh[:, :, :], ALU.add).then_inc(S["gbias_done"], 1)
            for c in range(C):
                ins = dve.tensor_scalar(RB0[:, c, :], bg0[:, :], rs[:, c:c + 1], None, ALU.mult)
            ins.then_inc(S["rb_done"], 1)
            for i in (0, 1):
                dve.wait_ge(S["wg_hi"], i + 1)
                ins = low_part(dve, Wgs[i][1][:, :], Wg[i][:, :], Wgs[i][0][:, :])
            ins.then_inc(S["wg_done"], 1)
            for n, (kind, j) in enumerate(set_tiles[:-1]):
                dve.wait_ge(S["set_hi"], n + 1)
                low_part(dve, set_target(kind, j, 1), bank_like(n, kind), set_target(kind, j, 0))\
                    .then_inc(S["set_free"], 1)
            dve.wait_ge(S["set_mm"], len(set_tiles))
            dve.tensor_scalar(RB1[:, :], sh.psum[:, (len(set_tiles) - 1) % 8, :], bg1[:, 0:1], None, ALU.mult)\
                .then_inc(S["set_free"], 1)
            dve.wait_ge(S["rb_done"], 1)
            dve.wait_ge(S["set_free"], len(set_tiles))

            def lstm(k, g):
                p_, t, s = steps[k]
                hv, n = view(p_, t, s)
                c_ = cell[:, s % 2, 0:n]

                def gate_is_there(gate):
                    per = NF if gate == F else NS
                    dve.wait_ge(gate_act[gate], per * g + uses(k, gate) + 1)

                gate_is_there(I)
                if t == 0:
                    dve.tensor_tensor(c_, gates[:, I, 0:n], gates[:, G, 0:n], ALU.mult).then_inc(S["c_done"], 1)
                else:
                    dve.tensor_tensor(gates[:, I, 0:n], gates[:, I, 0:n], gates[:, G, 0:n], ALU.mult)
                    gate_is_there(F)
                    dve.tensor_tensor(gates[:, F, 0:n], gates[:, F, 0:n], c_, ALU.mult).then_inc(S["c_own"], 1)
                    dve.wait_ge(S["c_own"], NF * g + uses(k, F) + 1)
                    dve.tensor_tensor(c_, gates[:, F, 0:n], gates[:, I, 0:n], ALU.add).then_inc(S["c_done"], 1)
                dve.wait_ge(S["tanh_done"], NS * g + k + 1)
                if t == p_ - 1:
                    dve.tensor_tensor(hv, like(gates[:, O, :], p_, n), like(tc, p_, n), ALU.mult)\
                        .then_inc(S["h_done"], 1)
                else:
                    dve.tensor_tensor(hn[:, 0:n], gates[:, O, 0:n], tc[:, 0:n], ALU.mult).then_inc(S["h_done"], 1)
                    dve.wait_ge(S["h_done"], NS * g + k + 1)
                    dve.tensor_copy(hh[:, s % 2, 0:n], hn[:, 0:n]).then_inc(S["c_own2"], 1)
                    dve.wait_ge(S["c_own2"], HS * g + hs_before(k) + 1)
                    low_part(dve, hl[:, s % 2, 0:n], hn[:, 0:n], hh[:, s % 2, 0:n]).then_inc(S["hs_done"], 1)

            def run(items, g):
                for kind, b, c, q, n, bk in numbered(items, g):
                    o = sh.psum[:, bk, :]
                    if kind == "L":
                        lstm(b, g)
                    elif kind == "stats":
                        take_stats(q)
                    elif kind == "norm":
                        normalise(q)
                    elif kind[0] == "Y" and is_tile(kind, c):
                        dve.wait_ge(S["conv_hi"], 2 * QB * q + y_order.index((kind, b)) + 1)
                        low_part(dve, ycl[:, b % 2, :], o, ych[:, b % 2, :]).then_inc(S["ring_free"], 1)
                    elif kind == "W0":
                        dve.wait_ge(S["ring_mm"], n + 1)
                        wait(dve, S["h1l_done"], QB * q + b - 1)
                        dve.tensor_tensor(u[:, b % 2, :, :], o.rearrange("p (c d) -> p c d", c=C), RB0[:, :, :],
                                          ALU.add).then_inc(S["ring_free"], 1)
                    elif kind == "low":
                        dve.wait_ge(S["relu_done"], QB * q + b + 1)
                        dve.scalar_tensor_tensor(h1l[:, :, b, :], u[:, b % 2, :, :], 0.0,
                                                 h1h[:, :, b, :].bitcast(F32), ALU.max, ALU.subtract)\
                            .then_inc(S["h1l_done"], 1)
                    elif kind == "W1":
                        dve.wait_ge(S["ring_mm"], n + 1)
                        dve.tensor_tensor(Hin[:, b, :], o, RB1[:, :], ALU.add).then_inc(S["ring_free"], 1)
                        dve.wait_ge(S["ring_free"], n + 1)
                        dve.tensor_scalar(Hin[:, b, :], Hin[:, b, :], 0.0, None, ALU.max).then_inc(S["hq_done"], 1)
                    elif kind == "R":
                        dve.wait_ge(S["ring_mm"], n + 1)
                        dve.tensor_tensor(sq[:, b, :, :], o.rearrange("p (c d) -> p c d", c=C),
                                          sh.X[:, :, bass.ds(QB * q + b, 1), :].rearrange("p c o d -> p c (o d)"),
                                          ALU.add).then_inc(S["ring_free"], 1)

            def take_stats(g):
                dve.wait_ge(S["ring_free"], ring_base(g + 1) + RESID)
                for b in range(QB):
                    ins = norm_stats(dve, stats[:, b * C:(b + 1) * C, :], sq[:, b, :, :])
                ins.then_inc(S["stat_done"], 1)

            def normalise(g):
                dve.wait_ge(S["rstd_done"], g + 1)
                for b in range(QB):
                    for c in range(C):
                        k = b * C + c
                        ins = dve.tensor_scalar(sh.X[:, c, bass.ds(QB * g + b, 1), :], sq[:, b, c:c + 1, :],
                                                mean[:, k:k + 1], rstd[:, k:k + 1], ALU.subtract, ALU.mult)
                ins.then_inc(S["x2_done"], 1)

            run(alone(), None)
            run(schedule(0, True, False), 0)
            with dve.Fori(1, NQ - 1) as g:
                run(schedule(g, True, True), g)
            run(schedule(NQ - 1, False, True), NQ - 1)
            run(residual(), NQ)
            take_stats(NQ - 1)
            normalise(NQ - 1)

        @block.gpsimd
        def _(pool):
            def split_x(q, c):
                pool.wait_ge(S["xh_done"], C * q + c + 1)
                low_part(pool, Xl[:, c, :, :], sh.X[:, c, bass.ds(QB * q, QB), :], Xh[:, c, :, :])\
                    .then_inc(S["xl_done"], 1)

            def lstm(k, g):
                p_, t, s = steps[k]
                hv, n = view(p_, t, s, Hin)
                pool.wait_ge(S["x_hi"], NS * g + k + 1)
                low_part(pool, like(xl[:, s % 2, :], p_, n), hv, like(xh[:, s % 2, :], p_, n))\
                    .then_inc(S["xs_done"], 1)

            def norm(g):
                pool.wait_ge(S["stat_done"], g + 1)
                norm_scales(pool, sh, QB * C, stats, work3, mean[:, :], rstd[:, :], S["norm_own"],
                            NORM_LINKS * g).then_inc(S["rstd_done"], 1)

            def quad(g, with_next, with_last):
                for k in range(1, NS + 1):
                    if k < NS:
                        lstm(k, g)
                    elif with_next:
                        lstm(0, g + 1)
                    if with_next and k <= 2:
                        split_x(g + 1, 2 * k - 2)
                        split_x(g + 1, 2 * k - 1)
                    if with_last and k == 5:
                        norm(g - 1)

            for c in range(C):
                split_x(0, c)
            lstm(0, 0)
            quad(0, True, False)
            with pool.Fori(1, NQ - 1) as g:
                quad(g, True, True)
            quad(NQ - 1, False, True)
            norm(NQ - 1)


def phase_batchnorm(nc, sh, d):
    C, D, N, NB = sh.C, sh.D, sh.N, sh.NB
    NP, NQ = NB // 2, NB // QB
    J = d["L2_gnn_W1"].shape[0] // P
    with ExitStack() as ctx:
        sb, sem = allocators(nc, ctx)
        H1 = sb("H1", [P, J, NB, N])
        O2 = sb("O2", [P, NB, N])
        AhT = (sb("AhTh", [P, C, N], F32R), sb("AhTl", [P, C, N], F32R))
        HI = sb("HI", [P, QB * J, N], F32R)
        LO = sb("LO", [P, QB * J, N], F32R)
        tmp = sb("tmp", [P, 4, N])
        wn = sb("wn", [P, 4, P])
        WT = (sb("WTh", [P, 4, P], F32R), sb("WTl", [P, 4, P], F32R))
        ones = sb("bones", [P, P])
        rsum = sb("brs", [P, C])
        dsum = sb("bds", [P, C])
        deg = sb("deg", [P, C])
        dinv = sb("dinv", [P, C])
        dblock = sb("dblock", [P, C, P])
        drow = sb("drow", [P, N])
        par1 = sb("par1", [P, 3, J])
        par2 = sb("par2", [P, 3, 1])
        st1 = sb("st1", [P, J, NB, 6])
        st2 = sb("st2", [P, 1, NB, 6])
        bmv = sb("bmv", [P, J + 1, 2])
        bsc = sb("bsc", [P, J + 1])
        bsh = sb("bsh", [P, J + 1])
        norm = sh.norm
        names = ("w_in", "p_in", "ones_done", "set_mm", "set_free", "set_hi", "own", "deg_done", "dinv_done", "ah_done",
                 "ah_hi", "ah_lo", "xh_done", "xl_done", "y_mm", "y_hi", "y_lo", "w_mm", "w_out", "st_done",
                 "bmv_done", "bve", "brstd", "bn_done", "u_done", "t_hi", "t_lo", "o_mm", "o_out", "ost_done",
                 "z_done", "z_mm", "z_add", "stat_done", "norm_own", "rstd_done", "x_done")
        S = {n: sem("b_" + n) for n in names}
        block = ctx.enter_context(nc.Block())

        def xb(b):
            return sh.X[:, :, bass.ds(b, 1), :].rearrange("p c o d -> p c (o d)")

        def by_chunk(ap):
            return ap.rearrange("p (c d) -> p c d", c=C)

        @block.sync
        def _(sp):
            sp.dma_start(wn[:, 0:J, :], d["L2_gnn_W1"].rearrange("(j p) d -> p j d", p=P)).then_inc(S["w_in"], 16)
            sp.dma_start(wn[:, J:2 * J, :], d["L2_gnn_W2"].rearrange("o (j h) -> o j h", j=J))\
                .then_inc(S["w_in"], 16)
            for k, name in enumerate(("b", "g", "be")):
                sp.dma_start(par1[:, k, :], d[f"L2_gnn_{name}1"].rearrange("(j p) -> p j", p=P))\
                    .then_inc(S["p_in"], 16)
                sp.dma_start(par2[:, k, :], d[f"L2_gnn_{name}2"].rearrange("(p o) -> p o", o=1))\
                    .then_inc(S["p_in"], 16)

        @block.tensor
        def _(pe):
            pe.wait_ge(S["ones_done"], 1)
            for c2 in range(C):
                for c in range(C):
                    ins = pe.matmul(sh.psum[:, 0, c2:c2 + 1], sh.A[:, c, c2 * P:(c2 + 1) * P], ones[:, 0:1],
                                    start=(c == 0), stop=(c == C - 1))
            ins.then_inc(S["set_mm"], 1)
            pe.wait_ge(S["w_in"], 32)
            for k in range(2 * J):
                ins = pe.transpose(sh.psum[:, 1, k * P:(k + 1) * P], wn[:, k, :], sh.ident[:, :])
            ins.then_inc(S["set_mm"], 1)
            for j in range(C):
                for c in range(C):
                    ins = pe.transpose(sh.psum[:, 3 + j, c * P:(c + 1) * P], sh.A[:, c, j * P:(j + 1) * P],
                                       sh.ident[:, :])
            ins.then_inc(S["set_mm"], 1)
            pe.wait_ge(S["deg_done"], 2)
            pe.matmul(sh.psum[:, 2, :], ones[:, :], dblock[:, :, :], start=True, stop=True)\
                .then_inc(S["set_mm"], 1)
            pe.wait_ge(S["ah_lo"], C)
            pe.wait_ge(S["set_free"], 2)

            def first(i, last):
                for s in (0, 1):
                    pe.wait_ge(S["xl_done"], 2 * i + s + 1)
                    for c in range(C):
                        cols = slice(c * D, (c + 1) * D)
                        ins = product(pe, sh.psum[:, s, :], (HI[:, s, cols], LO[:, s, cols]),
                                      (AhT[0][:, c, :], AhT[1][:, c, :]), start=(c == 0), stop=(c == C - 1))
                    ins.then_inc(S["y_mm"], 1)
                wait(pe, S["w_out"], 4 * i)
                for s in (0, 1):
                    pe.wait_ge(S["y_lo"], 2 * i + s + 1)
                    for j in range(J):
                        product(pe, sh.psum[:, 2 + 2 * s + j, :], (WT[0][:, j, :], WT[1][:, j, :]),
                                (HI[:, 2 + s, :], LO[:, 2 + s, :])).then_inc(S["w_mm"], 1)

            def second(i, last):
                for b in range(QB):
                    n = QB * i + b
                    pe.wait_ge(S["t_lo"], J * (n + 1))
                    wait(pe, S["o_out"], n - QB + 1)
                    for j in range(J):
                        ins = product(pe, sh.psum[:, 4 + b, :], (WT[0][:, J + j, :], WT[1][:, J + j, :]),
                                      (HI[:, J * b + j, :], LO[:, J * b + j, :]), start=(j == 0),
                                      stop=(j == J - 1))
                    ins.then_inc(S["o_mm"], 1)

            def third(i, last):
                for b in range(QB):
                    n = QB * i + b
                    pe.wait_ge(S["z_done"], n + 1)
                    wait(pe, S["z_add"], n - QB + 1)
                    for c in range(C):
                        cols = slice(c * P, (c + 1) * P)
                        ins = pe.transpose(sh.psum[:, b, cols], tmp[:, b, cols], sh.ident[:, :])
                    ins.then_inc(S["z_mm"], 1)

            peeled(pe, NP, first)
            peeled(pe, NQ, second)
            peeled(pe, NQ, third)

        @block.scalar
        def _(act):
            act.wait_ge(S["set_mm"], 2)
            act.activation(WT[0][:, :, :], sh.psum[:, 1, :].rearrange("p (k h) -> p k h", h=P), ACT.Copy)\
                .then_inc(S["set_hi"], 1)
            for j in range(C):
                act.wait_ge(S["ah_done"], j + 1)
                act.activation(AhT[0][:, j, :], tmp[:, j, :], ACT.Copy).then_inc(S["ah_hi"], 1)

            def split_x(b, s):
                act.activation(by_chunk(HI[:, s, :]), xb(b), ACT.Copy).then_inc(S["xh_done"], 1)

            def first(i, last):
                for s in (0, 1):
                    act.wait_ge(S["y_mm"], 2 * i + s + 1)
                    act.activation(HI[:, 2 + s, :], sh.psum[:, s, :], ACT.Copy).then_inc(S["y_hi"], 1)
                    if not last:
                        split_x(2 * i + 2 + s, s)
                for s in (0, 1):
                    for j in range(J):
                        act.wait_ge(S["w_mm"], 4 * i + 2 * s + j + 1)
                        act.activation(H1[:, j, bass.ds(2 * i + s, 1), :], sh.psum[:, 2 + 2 * s + j, :],
                                       ACT.Identity, bias=par1[:, 0, j:j + 1]).then_inc(S["w_out"], 1)

            def second_out(n, b):
                act.wait_ge(S["o_mm"], n + 1)
                act.activation(O2[:, bass.ds(n, 1), :], sh.psum[:, 4 + b, :], ACT.Identity,
                               bias=par2[:, 0, 0:1]).then_inc(S["o_out"], 1)

            def second(i, last):
                for b in range(QB):
                    n = QB * i + b
                    wait(act, S["o_mm"], n - QB + 1)
                    for j in range(J):
                        act.activation(HI[:, J * b + j, :], H1[:, j, bass.ds(n, 1), :], ACT.Relu,
                                       bias=bsh[:, j:j + 1], scale=bsc[:, j:j + 1]).then_inc(S["t_hi"], 1)
                    if not isinstance(i, int) or n >= 2:
                        second_out(n - 2, (b - 2) % QB)

            def z(n, b):
                wait(act, S["z_mm"], n - QB + 1)
                act.activation(tmp[:, b, :], O2[:, bass.ds(n, 1), :], ACT.Identity,
                               bias=bsh[:, J:J + 1], scale=bsc[:, J:J + 1]).then_inc(S["z_done"], 1)

            def third(i, last):
                for b in range(QB):
                    if not last:
                        z(QB * (i + 1) + b, b)
                    if not isinstance(i, int) or i > 0:
                        if b == 0:
                            act.wait_ge(S["rstd_done"], i)
                        norm.apply(act, QB * (i - 1) + b, b).then_inc(S["x_done"], 1)

            for s in (0, 1):
                split_x(s, s)
            act.wait_ge(S["p_in"], 96)
            peeled(act, NP, first)
            act.wait_ge(S["bn_done"], 1)
            peeled(act, NQ, second)
            for n in (NB - 2, NB - 1):
                second_out(n, n % QB)
            act.wait_ge(S["bn_done"], 2)
            for b in range(QB):
                z(b, b)
            peeled(act, NQ, third)
            act.wait_ge(S["rstd_done"], NQ)
            for b in range(QB):
                norm.apply(act, NB - QB + b, b).then_inc(S["x_done"], 1)

        @block.vector
        def _(dve):
            chain = [0]

            def link(ins):
                chain[0] += 1
                ins.then_inc(S["own"], 1)
                dve.wait_ge(S["own"], chain[0])

            dve.memset(ones[:, :], 1.0).then_inc(S["ones_done"], 1)
            for c in range(C):
                dve.reduce_sum(rsum[:, c:c + 1], sh.A[:, c, :], AX.X)
            for c in range(C):
                ins = dve.tensor_tensor(dblock[:, c, :], sh.A[:, c, c * P:(c + 1) * P], sh.ident[:, :], ALU.mult)
            link(ins)
            link(dve.reduce_sum(dsum[:, :], dblock[:, :, :], AX.X))
            link(dve.scalar_tensor_tensor(rsum[:, :], rsum[:, :], 1.0, dsum[:, :], ALU.add, ALU.subtract))
            dve.wait_ge(S["set_mm"], 1)
            dve.tensor_tensor(deg[:, :], sh.psum[:, 0, 0:C], rsum[:, :], ALU.add).then_inc(S["deg_done"], 1)
            dve.wait_ge(S["dinv_done"], 1)
            for c in range(C):
                ins = dve.tensor_scalar(dblock[:, c, :], sh.ident[:, :], dinv[:, c:c + 1], None, ALU.mult)
            ins.then_inc(S["deg_done"], 1)
            dve.wait_ge(S["set_hi"], 1)
            low_part(dve, WT[1][:, :, :], sh.psum[:, 1, :].rearrange("p (k h) -> p k h", h=P), WT[0][:, :, :])\
                .then_inc(S["set_free"], 1)
            dve.wait_ge(S["set_mm"], 4)
            dve.tensor_copy(drow[:, :], sh.psum[:, 2, :]).then_inc(S["set_free"], 1)
            dve.wait_ge(S["set_free"], 2)
            dve.wait_ge(S["deg_done"], 2)
            for j in range(C):
                link(dve.tensor_scalar(tmp[:, j, :], sh.psum[:, 3 + j, :], dinv[:, j:j + 1], None, ALU.mult))
                own = tmp[:, j, j * P:(j + 1) * P]
                link(dve.tensor_tensor(own, own, dblock[:, j, :], ALU.add))
                dve.tensor_tensor(tmp[:, j, :], tmp[:, j, :], drow[:, :], ALU.mult).then_inc(S["ah_done"], 1)
            for j in range(C):
                dve.wait_ge(S["ah_hi"], j + 1)
                low_part(dve, AhT[1][:, j, :], tmp[:, j, :], AhT[0][:, j, :]).then_inc(S["ah_lo"], 1)

            def first(i, last):
                for s in (0, 1):
                    dve.wait_ge(S["y_hi"], 2 * i + s + 1)
                    low_part(dve, LO[:, 2 + s, :], sh.psum[:, s, :], HI[:, 2 + s, :]).then_inc(S["y_lo"], 1)
                for s in (0, 1):
                    for j in range(J):
                        dve.wait_ge(S["w_out"], 4 * i + 2 * s + j + 1)
                        dve.bn_stats(st1[:, j, bass.ds(2 * i + s, 1), :], H1[:, j, bass.ds(2 * i + s, 1), :])\
                            .then_inc(S["st_done"], 1)

            def batch_norm(js, k):
                st, par = (st1, par1) if k == 0 else (st2, par2)
                for j in js:
                    ins = dve.bn_aggr(bmv[:, j, :], st[:, j - js[0], :, :].rearrange("p b s -> p (b s)"))
                ins.then_inc(S["bmv_done"], 1)
                dve.wait_ge(S["brstd"], k + 1)
                cols = slice(js[0], js[-1] + 1)
                link(dve.tensor_tensor(bsc[:, cols], bsc[:, cols], par[:, 1, :], ALU.mult))
                link(dve.tensor_tensor(bsh[:, cols], bmv[:, cols, 0], bsc[:, cols], ALU.mult))
                dve.tensor_tensor(bsh[:, cols], par[:, 2, :], bsh[:, cols], ALU.subtract)\
                    .then_inc(S["bn_done"], 1)
                dve.wait_ge(S["bn_done"], k + 1)

            def second_stats(n):
                dve.wait_ge(S["o_out"], n + 1)
                dve.bn_stats(st2[:, 0, bass.ds(n, 1), :], O2[:, bass.ds(n, 1), :]).then_inc(S["ost_done"], 1)

            def second(i, last):
                for b in range(QB):
                    n = QB * i + b
                    wait(dve, S["t_lo"], J * (n - 1))
                    for j in range(J):
                        dve.tensor_scalar(tmp[:, J * (b % 2) + j, :], H1[:, j, bass.ds(n, 1), :], bsc[:, j:j + 1],
                                          bsh[:, j:j + 1], ALU.mult, ALU.add).then_inc(S["u_done"], 1)
                    for j in range(J):
                        dve.wait_ge(S["u_done"], J * n + j + 1)
                        dve.wait_ge(S["t_hi"], J * n + j + 1)
                        dve.scalar_tensor_tensor(LO[:, J * b + j, :], tmp[:, J * (b % 2) + j, :], 0.0,
                                                 HI[:, J * b + j, :].bitcast(F32), ALU.max, ALU.subtract)\
                            .then_inc(S["t_lo"], 1)
                    if not isinstance(i, int) or n >= 3:
                        second_stats(n - 3)

            def third_stats(n):
                dve.wait_ge(S["z_add"], n + 1)
                norm.take_stats(dve, n).then_inc(S["stat_done"], 1)

            def third(i, last):
                for b in range(QB):
                    n = QB * i + b
                    dve.wait_ge(S["z_mm"], n + 1)
                    dve.tensor_tensor(xb(n), by_chunk(sh.psum[:, b, :]), xb(n), ALU.add).then_inc(S["z_add"], 1)
                    if not isinstance(i, int) or n >= 1:
                        third_stats(n - 1)

            peeled(dve, NP, first)
            dve.wait_ge(S["st_done"], 2 * J * NP)
            batch_norm(list(range(J)), 0)
            peeled(dve, NQ, second)
            for n in range(NB - 3, NB):
                second_stats(n)
            dve.wait_ge(S["ost_done"], NB)
            batch_norm([J], 1)
            peeled(dve, NQ, third)
            third_stats(NB - 1)

        @block.gpsimd
        def _(pool):
            pool.wait_ge(S["deg_done"], 1)
            pool.tensor_tensor(dinv[:, :], deg[:, :], sh.const[:, sh.ROOT, 0:C], ALU.pow).then_inc(S["dinv_done"], 1)

            def split_x(b, s, n):
                pool.wait_ge(S["xh_done"], n)
                low_part(pool, by_chunk(LO[:, s, :]), xb(b), by_chunk(HI[:, s, :])).then_inc(S["xl_done"], 1)

            for s in (0, 1):
                split_x(s, s, s + 1)
            with pool.Fori(0, NP - 1) as i:
                for s in (0, 1):
                    split_x(2 * i + 2 + s, s, 2 * i + s + 3)

            def batch_norm(cols, k):
                pool.wait_ge(S["bmv_done"], k + 1)
                n = cols.stop - cols.start
                pool.tensor_tensor(bsc[:, cols], bmv[:, cols, 1], sh.const[:, sh.EPS, 0:n], ALU.add).then_inc(S["bve"], 1)
                pool.wait_ge(S["bve"], k + 1)
                pool.tensor_tensor(bsc[:, cols], bsc[:, cols], sh.const[:, sh.ROOT, 0:n], ALU.pow).then_inc(S["brstd"], 1)

            batch_norm(slice(0, J), 0)
            batch_norm(slice(J, J + 1), 1)

            def quad_norm(g, last):
                pool.wait_ge(S["stat_done"], QB * (g + 1))
                wait(pool, S["x_done"], QB * g)
                norm.scales(pool, g, S["norm_own"], SHIFT_LINKS * g).then_inc(S["rstd_done"], 1)

            peeled(pool, NQ, quad_norm)


def phase_attention(nc, sh, d, out):
    C, D, N, NB = sh.C, sh.D, sh.N, sh.NB
    NE = d["L3_gnn_src"].shape[0]
    K = NE // P
    NH, DH = d["L3_gnn_a"].shape
    NQ, NP = NB // QB, NB // 2
    R = QB * NH
    with ExitStack() as ctx:
        sb, sem = allocators(nc, ctx)
        ir = sb("ir", [P, 2, NE], I32)
        icol = sb("icol", [P, 2, K], I32)
        irf = sb("irf", [P, 2, NE])
        icf = sb("icf", [P, 2, K])
        iota = sb("iota", [P, N], I32)
        iotac = sb("iotac", [P, C], I32)
        iof = sb("iof", [P, N])
        ioc = sb("ioc", [P, C])
        keyr = sb("keyr", [P, NE])
        keyc = sb("keyc", [P, K])
        less = sb("less", [P, K, NE])
        pos = sb("pos", [P, K])
        perm = sb("perm", [P, K, NE])
        idxb = sb("idxb", [P, 2, K, P])
        ss = sb("ss", [P, 2, NE])
        sc = sb("sc", [P, K])
        Gs = sb("Gs", [P, C, NE])
        GZ = sb("GZ", [P, C, 2, NE], F32R)
        GsT = sb("GsT", [P, K, N], F32R)
        ones = sb("aones", [P, P])
        sel = sb("sel", [P, C, NE])
        lg = sb("lg", [R, NE])
        tiny = sb("tiny", [P, 1])
        ne = sb("ne", [R, NE])
        pf = sb("pf", [R, QB, NE])
        pr = sb("pr", [R, QB, NE])
        kf = sb("kf", [R, QB, NE])
        wn = sb("awn", [P, 3, P])
        WT = (sb("aWTh", [P, 3, P], F32R), sb("aWTl", [P, 3, P], F32R))
        acol = sb("acol", [P, 1])
        wide = sb("wide", [P, 2 * R - NH])
        XH = sb("aXH", [P, 2, N], F32R)
        XL = sb("aXL", [P, 2, N], F32R)
        ZH = sb("ZH", [P, QB, N], F32R)
        ZL = sb("ZL", [P, QB, N], F32R)
        uq = sb("uq", [P, 2, NE])
        lr = sb("lr", [P, 2, NE])
        V = sb("aV", [P, NB, K, D])
        sco = sb("sco", [R, QB, NE])
        s1 = sb("s1", [R, QB, NE])
        s2 = sb("s2", [R, QB, NE])
        aT = sb("aT", [P, K, NB, NH])
        va = sb("va", [P, QB, K, D])
        vah = sb("vah", [P, QB, K, D], F32R)
        val = sb("val", [P, QB, K, D], F32R)
        norm = sh.norm
        names = ("i_in", "w_in", "iota_done", "own", "perm_done", "set_mm", "ss_done", "g_done", "sel_done", "lg_done",
                 "w_hi", "w_lo", "wide0", "wide_done", "xh_done", "xl_done", "z_mm", "z_hi", "z_lo", "uv_mm", "uv_out",
                 "lr_done", "sc_mm", "sc_done", "sd_done", "ex_done", "soft", "at_mm", "at_done", "va_done",
                 "va_hi", "va_lo", "y_mm", "y_hi", "y_lo", "o_mm", "o_add", "stat_done", "norm_own",
                 "rstd_done", "x_done", "stored")
        S = {n: sem("a_" + n) for n in names}
        block = ctx.enter_context(nc.Block())

        def xb(b):
            return sh.X[:, :, bass.ds(b, 1), :].rearrange("p c o d -> p c (o d)")

        def by_chunk(ap):
            return ap.rearrange("p (c d) -> p c d", c=C)

        @block.sync
        def _(sp):
            for k, name in enumerate(("src", "dst")):
                sp.dma_start(ir[:, k, :], d[f"L3_gnn_{name}"].rearrange("(o e) -> o e", o=1)
                             .broadcast_to([P, NE])).then_inc(S["i_in"], 16)
                sp.dma_start(icol[:, k, :], d[f"L3_gnn_{name}"].rearrange("(k p) -> p k", p=P))\
                    .then_inc(S["i_in"], 16)
            for k, name in enumerate(("W_lin", "W_val", "W_out")):
                sp.dma_start(wn[:, k, :], d[f"L3_gnn_{name}"]).then_inc(S["w_in"], 16)
            sp.dma_start(acol[:, :], d["L3_gnn_a"].rearrange("h (e o) -> (h e) o", o=1)).then_inc(S["w_in"], 16)
            ov = out.rearrange("b (c p) d -> p c b d", p=P)
            with sp.Fori(0, NP) as i:
                sp.wait_ge(S["x_done"], 2 * (i + 1))
                for c in range(C):
                    sp.dma_start(ov[:, c, bass.ds(2 * i, 2), :], sh.X[:, c, bass.ds(2 * i, 2), :])\
                        .then_inc(S["stored"], 16)
            sp.wait_ge(S["stored"], 16 * C * NP)

        @block.gpsimd
        def _(pool):
            pool.iota(iota[:, :], pattern=[[1, N]], base=0, channel_multiplier=0).then_inc(S["iota_done"], 1)
            pool.iota(iotac[:, :], pattern=[[P, C]], base=0, channel_multiplier=1).then_inc(S["iota_done"], 1)
            pool.memset(wide[:, :], 0.0).then_inc(S["wide0"], 1)
            pool.memset(tiny[:, :], 1e-8).then_inc(S["wide0"], 1)

            def split_x(b, s, n):
                pool.wait_ge(S["xh_done"], n)
                low_part(pool, by_chunk(XL[:, s, :]), xb(b), by_chunk(XH[:, s, :])).then_inc(S["xl_done"], 1)

            for s in (0, 1):
                split_x(s, s, s + 1)
            with pool.Fori(0, NP - 1) as i:
                for s in (0, 1):
                    split_x(2 * i + 2 + s, s, 2 * i + s + 3)

            def quad_norm(g, last):
                pool.wait_ge(S["stat_done"], QB * (g + 1))
                wait(pool, S["x_done"], QB * g)
                norm.scales(pool, g, S["norm_own"], SHIFT_LINKS * g).then_inc(S["rstd_done"], 1)

            peeled(pool, NQ, quad_norm)

        @block.scalar
        def _(act):
            act.wait_ge(S["set_mm"], 1)
            act.activation(WT[0][:, :, :], sh.psum[:, 0, 0:3 * P].rearrange("p (k h) -> p k h", h=P), ACT.Copy)\
                .then_inc(S["w_hi"], 1)
            act.wait_ge(S["set_mm"], 4)
            act.wait_ge(S["wide0"], 2)
            act.activation(lg[:, :], sh.psum[0:R, 4, 0:NE], ACT.Ln, bias=tiny[0:R, 0:1]).then_inc(S["lg_done"], 1)

            def split_x(b, s):
                act.activation(by_chunk(XH[:, s, :]), xb(b), ACT.Copy).then_inc(S["xh_done"], 1)

            def gather(g, h, last):
                for s in (0, 1):
                    n = QB * g + 2 * h + s
                    act.wait_ge(S["z_mm"], n + 1)
                    act.activation(ZH[:, s, :], sh.psum[:, s, :], ACT.Copy).then_inc(S["z_hi"], 1)
                    if not last:
                        split_x(n + 2, s)
                for s in (0, 1):
                    n = QB * g + 2 * h + s
                    act.wait_ge(S["uv_mm"], n + 1)
                    wait(act, S["lr_done"], QB * g + 2 * h)
                    act.activation(uq[:, s, :], sh.psum[:, 2 + s, 0:NE], ACT.Copy).then_inc(S["uv_out"], 1)
                    act.activation(V[:, bass.ds(n, 1), :, :],
                                   sh.psum[:, 2 + s, NE:2 * NE].rearrange("p (k d) -> p k d", k=K), ACT.Copy)\
                        .then_inc(S["uv_out"], 1)

            for s in (0, 1):
                split_x(s, s)

            def gather_quad(g, last):
                gather(g, 0, False)
                gather(g, 1, last)

            peeled(act, NQ, gather_quad)
            act.wait_ge(S["sd_done"], 1)
            act.activation(s2[:, :, :], s1[:, :, :], ACT.Exp).then_inc(S["ex_done"], 1)

            def scattered_high(n, b):
                act.wait_ge(S["y_mm"], n + 1)
                act.activation(ZH[:, b, :], sh.psum[:, b, :], ACT.Copy).then_inc(S["y_hi"], 1)

            def attend(i, last):
                for b in range(QB):
                    n = QB * i + b
                    act.wait_ge(S["va_done"], n + 1)
                    wait(act, S["y_mm"], n - QB + 1)
                    act.activation(vah[:, b, :, :], va[:, b, :, :], ACT.Copy).then_inc(S["va_hi"], 1)
                    if not isinstance(i, int) or n >= 1:
                        scattered_high(n - 1, (b - 1) % QB)
                if not isinstance(i, int) or i > 0:
                    act.wait_ge(S["rstd_done"], i)
                    for b in range(QB):
                        norm.apply(act, QB * (i - 1) + b, b).then_inc(S["x_done"], 1)

            peeled(act, NQ, attend)
            scattered_high(NB - 1, QB - 1)
            act.wait_ge(S["rstd_done"], NQ)
            for b in range(QB):
                norm.apply(act, NB - QB + b, b).then_inc(S["x_done"], 1)

        @block.vector
        def _(dve):
            chain = [0]

            def link(ins):
                chain[0] += 1
                ins.then_inc(S["own"], 1)
                dve.wait_ge(S["own"], chain[0])

            dve.wait_ge(S["iota_done"], 2)
            dve.wait_ge(S["i_in"], 64)
            dve.memset(ones[:, :], 1.0)
            dve.tensor_copy(iof[:, :], iota[:, :])
            dve.tensor_copy(ioc[:, :], iotac[:, :])
            dve.tensor_copy(icf[:, :, :], icol[:, :, :])
            link(dve.tensor_copy(irf[:, :, :], ir[:, :, :]))
            dve.scalar_tensor_tensor(keyr[:, :], irf[:, 0, :], float(NE), iof[:, 0:NE], ALU.mult, ALU.add)
            link(dve.scalar_tensor_tensor(keyc[:, :], icf[:, 0, :], float(NE), ioc[:, 0:K], ALU.mult, ALU.add))
            for k in range(K):
                ins = dve.tensor_scalar(less[:, k, :], keyr[:, :], keyc[:, k:k + 1], None, ALU.is_lt)
            link(ins)
            link(dve.reduce_sum(pos[:, :], less[:, :, :], AX.X))
            for k in range(K):
                dve.tensor_scalar(perm[:, k, :], iof[:, 0:NE], pos[:, k:k + 1], None, ALU.is_equal)
                for j in (0, 1):
                    ins = dve.tensor_scalar(idxb[:, j, k, :], ones[:, :], icf[:, j, k:k + 1], None, ALU.mult)
            ins.then_inc(S["perm_done"], 1)
            dve.wait_ge(S["w_hi"], 1)
            low_part(dve, WT[1][:, :, :], sh.psum[:, 0, 0:3 * P].rearrange("p (k h) -> p k h", h=P), WT[0][:, :, :])\
                .then_inc(S["w_lo"], 1)
            dve.wait_ge(S["wide0"], 2)
            dve.wait_ge(S["w_in"], 64)
            for h in range(NH):
                rows = slice(h * DH, (h + 1) * DH)
                ins = dve.tensor_copy(wide[rows, R - NH + h:R - NH + h + 1], acol[rows, 0:1])
            ins.then_inc(S["wide_done"], 1)
            dve.wait_ge(S["set_mm"], 2)
            dve.tensor_copy(sc[:, :], sh.psum[:, 2, 0:K])
            link(dve.tensor_copy(ss[:, :, :], sh.psum[:, 1, :].rearrange("p (j e) -> p j e", j=2)))
            for c in range(C):
                dve.tensor_scalar(Gs[:, c, :], ss[:, 0, :], ioc[:, c:c + 1], None, ALU.is_equal)
                ins = dve.tensor_scalar(GZ[:, c, 1, :], ss[:, 1, :], ioc[:, c:c + 1], None, ALU.is_equal)
            link(ins)
            dve.tensor_tensor(GZ[:, :, 0, :], Gs[:, :, :], GZ[:, :, 1, :].bitcast(F32), ALU.add)
            for k in range(K):
                ins = dve.tensor_scalar(GsT[:, k, :], iof[:, :], sc[:, k:k + 1], None, ALU.is_equal)
            ins.then_inc(S["g_done"], 1)
            dve.wait_ge(S["set_mm"], 3)
            dve.tensor_tensor(sel[:, :, :], sh.psum[:, 5:7, :].rearrange("p t (c e) -> p (t c) e", e=NE),
                              GZ[:, :, 1, :].bitcast(F32), ALU.mult).then_inc(S["sel_done"], 1)
            link(dve.tensor_tensor(ne[:, 1:NE], ss[0:R, 0, 1:NE], ss[0:R, 0, 0:NE - 1], ALU.not_equal))
            for q in range(QB):
                dve.tensor_scalar(pf[:, q, 1:NE], ne[:, 1:NE], LOWEST, None, ALU.mult)
                dve.tensor_scalar(kf[:, q, 1:NE], ne[:, 1:NE], -1.0, 1.0, ALU.mult, ALU.add)
                dve.tensor_scalar(pr[:, q, 0:NE - 1], ne[:, 1:NE], LOWEST, None, ALU.mult)
            dve.memset(pf[:, :, 0:1], LOWEST)
            dve.memset(kf[:, :, 0:1], 0.0)
            dve.memset(pr[:, :, NE - 1:NE], LOWEST)

            def gather(g, h, last):
                for s in (0, 1):
                    n = QB * g + 2 * h + s
                    dve.wait_ge(S["z_hi"], n + 1)
                    low_part(dve, ZL[:, s, :], sh.psum[:, s, :], ZH[:, s, :]).then_inc(S["z_lo"], 1)
                for s in (0, 1):
                    n = QB * g + 2 * h + s
                    dve.wait_ge(S["uv_out"], 2 * n + 1)
                    dve.scalar_tensor_tensor(lr[:, s, :], uq[:, s, :], 0.2, uq[:, s, :], ALU.mult, ALU.max)\
                        .then_inc(S["lr_done"], 1)

            def scores(g):
                dve.wait_ge(S["sc_mm"], QB * g + QB)
                dve.tensor_tensor(sco[:, bass.ds(g, 1), :].rearrange("p o e -> p (o e)"), sh.psum[0:R, 4, 0:NE],
                                  lg[:, :], ALU.add).then_inc(S["sc_done"], 1)

            dve.wait_ge(S["lg_done"], 1)

            def gather_quad(g, last):
                for h in (0, 1):
                    wait(dve, S["sc_mm"], QB * g + 2 * h)
                    gather(g, h, False)
                scores(g)

            peeled(dve, NQ, gather_quad)

            def flat(t):
                return t[:, :, :].rearrange("p q e -> p (q e)")

            soft = [0]

            def then(ins):
                soft[0] += 1
                ins.then_inc(S["soft"], 1)
                dve.wait_ge(S["soft"], soft[0])

            dve.wait_ge(S["sc_done"], NQ)
            then(dve.tensor_tensor_scan(flat(s1), flat(pf), flat(sco), LOWEST, ALU.add, ALU.max))
            then(dve.tensor_tensor_scan(flat(s2)[:, ::-1], flat(pr)[:, ::-1], flat(s1)[:, ::-1], LOWEST,
                                        ALU.add, ALU.max))
            dve.tensor_tensor(flat(s1), flat(sco), flat(s2), ALU.subtract).then_inc(S["sd_done"], 1)
            dve.wait_ge(S["ex_done"], 1)
            then(dve.tensor_tensor_scan(flat(s1), flat(kf), flat(s2), 0.0, ALU.mult, ALU.add))
            then(dve.tensor_tensor_scan(flat(sco)[:, ::-1], flat(pr)[:, ::-1], flat(s1)[:, ::-1], 0.0,
                                        ALU.add, ALU.max))
            then(dve.reciprocal(flat(s1), flat(sco)))
            dve.tensor_tensor(flat(sco), flat(s2), flat(s1), ALU.mult).then_inc(S["soft"], 1)
            dve.wait_ge(S["at_mm"], 1)
            dve.tensor_copy(aT[:, :, :, :].rearrange("p k (q b) h -> p k q (b h)", q=NQ),
                            sh.psum[:, 5, 0:NQ * K * R].rearrange("p (k q r) -> p k q r", k=K, q=NQ))\
                .then_inc(S["at_done"], 1)
            dve.wait_ge(S["at_done"], 1)

            def weigh(n, b):
                for k in range(K):
                    ins = dve.tensor_tensor(
                        va[:, b, k, :].rearrange("p (h e) -> p h e", h=NH),
                        V[:, bass.ds(n, 1), k, :].rearrange("p o (h e) -> p (o h) e", h=NH),
                        aT[:, k, bass.ds(n, 1), :].rearrange("p o h -> p (o h)").unsqueeze(2)
                        .broadcast_to([P, NH, DH]), ALU.mult)
                ins.then_inc(S["va_done"], 1)

            def weighted_low(n, b):
                dve.wait_ge(S["va_hi"], n + 1)
                low_part(dve, val[:, b, :, :], va[:, b, :, :], vah[:, b, :, :]).then_inc(S["va_lo"], 1)

            def scattered_low(n, b):
                dve.wait_ge(S["y_hi"], n + 1)
                low_part(dve, ZL[:, b, :], sh.psum[:, b, :], ZH[:, b, :]).then_inc(S["y_lo"], 1)

            def residual(n, b):
                dve.wait_ge(S["o_mm"], n + 1)
                dve.tensor_tensor(xb(n), by_chunk(sh.psum[:, 4 + b, :]), xb(n), ALU.add).then_inc(S["o_add"], 1)

            def out_stats(n):
                dve.wait_ge(S["o_add"], n + 1)
                norm.take_stats(dve, n).then_inc(S["stat_done"], 1)

            def attend(i, last):
                for b in range(QB):
                    n = QB * i + b
                    first = isinstance(i, int) and i == 0
                    if not last or b < QB - 1:
                        wait(dve, S["va_lo"], n - QB + 2)
                        weigh(n + 1, (b + 1) % QB)
                    if not first or b >= 1:
                        scattered_low(n - 1, (b - 1) % QB)
                    weighted_low(n, b)
                    if not first or b >= 2:
                        residual(n - 2, (b - 2) % QB)
                        out_stats(n - 2)

            weigh(0, 0)
            peeled(dve, NQ, attend)
            scattered_low(NB - 1, QB - 1)
            for n in (NB - 2, NB - 1):
                residual(n, n % QB)
                out_stats(n)

        @block.tensor
        def _(pe):
            pe.wait_ge(S["w_in"], 64)
            for k in range(3):
                ins = pe.transpose(sh.psum[:, 0, k * P:(k + 1) * P], wn[:, k, :], sh.ident[:, :])
            ins.then_inc(S["set_mm"], 1)
            pe.wait_ge(S["perm_done"], 1)
            for j in (0, 1):
                for k in range(K):
                    pe.matmul(sh.psum[:, 1, j * NE:(j + 1) * NE], idxb[:, j, k, :], perm[:, k, :], start=(k == 0),
                              stop=(k == K - 1))
            for q in range(K):
                for k in range(K):
                    ins = pe.matmul(sh.psum[:, 2, q:q + 1], perm[:, k, q * P:(q + 1) * P], icf[:, 0, k:k + 1],
                                    start=(k == 0), stop=(k == K - 1))
            ins.then_inc(S["set_mm"], 1)
            pe.wait_ge(S["g_done"], 1)
            for m in range(C):
                for c in range(C):
                    ins = pe.matmul(sh.psum[:, 5 + m // 2, (m % 2) * NE:(m % 2 + 1) * NE],
                                    sh.A[:, c, m * P:(m + 1) * P], Gs[:, c, :], start=(c == 0), stop=(c == C - 1))
            ins.then_inc(S["set_mm"], 1)
            pe.wait_ge(S["sel_done"], 1)
            for c in range(C):
                ins = pe.matmul(sh.psum[0:R, 4, 0:NE], ones[:, 0:R], sel[:, c, :], start=(c == 0),
                                stop=(c == C - 1))
            ins.then_inc(S["set_mm"], 1)
            pe.wait_ge(S["w_lo"], 1)
            pe.wait_ge(S["wide_done"], 1)
            pe.wait_ge(S["lg_done"], 1)

            def gather_quad(g, last):
                for h in (0, 1):
                    n = QB * g + 2 * h
                    for s in (0, 1):
                        pe.wait_ge(S["xl_done"], n + s + 1)
                        for c in range(C):
                            cols = slice(c * D, (c + 1) * D)
                            for part in (XH, XL):
                                ins = pe.matmul(sh.psum[:, s, :], part[:, s, cols], GZ[:, c, :, :],
                                                start=(c == 0 and part is XH), stop=(c == C - 1 and part is XL))
                        ins.then_inc(S["z_mm"], 1)
                    wait(pe, S["uv_out"], 2 * n)
                    for s in (0, 1):
                        pe.wait_ge(S["z_lo"], n + s + 1)
                        product(pe, sh.psum[:, 2 + s, 0:NE], (WT[0][:, 0, :], WT[1][:, 0, :]),
                                (ZH[:, s, 0:NE], ZL[:, s, 0:NE]))
                        for k in range(K):
                            cols = slice(NE + k * P, NE + (k + 1) * P)
                            ins = product(pe, sh.psum[:, 2 + s, cols], (ZH[:, s, cols], ZL[:, s, cols]),
                                          (WT[0][:, 1, :], WT[1][:, 1, :]))
                        ins.then_inc(S["uv_mm"], 1)
                    if h == 0:
                        wait(pe, S["sc_done"], g)
                    for s in (0, 1):
                        pe.wait_ge(S["lr_done"], n + s + 1)
                        b = 2 * h + s
                        pe.matmul(sh.psum[0:R, 4, 0:NE], wide[:, R - NH - NH * b:2 * R - NH - NH * b], lr[:, s, :],
                                  start=(b == 0), stop=(b == QB - 1)).then_inc(S["sc_mm"], 1)

            peeled(pe, NQ, gather_quad)
            pe.wait_ge(S["soft"], 6)
            for k in range(K):
                for q in range(NQ):
                    at = (k * NQ + q) * R
                    ins = pe.transpose(sh.psum[:, 5, at:at + R], sco[:, q, k * P:(k + 1) * P],
                                       sh.ident[0:R, 0:R])
            ins.then_inc(S["at_mm"], 1)

            def project(n, b):
                pe.wait_ge(S["y_lo"], n + 1)
                wait(pe, S["o_add"], n - QB + 1)
                for c in range(C):
                    cols = slice(c * P, (c + 1) * P)
                    ins = product(pe, sh.psum[:, 4 + b, cols], (ZH[:, b, cols], ZL[:, b, cols]),
                                  (WT[0][:, 2, :], WT[1][:, 2, :]))
                ins.then_inc(S["o_mm"], 1)

            def attend(i, last):
                for b in range(QB):
                    n = QB * i + b
                    pe.wait_ge(S["va_lo"], n + 1)
                    wait(pe, S["y_lo"], n - QB + 1)
                    for k in range(K):
                        for part in (vah, val):
                            ins = pe.matmul(sh.psum[:, b, :], part[:, b, k, :], GsT[:, k, :],
                                            start=(k == 0 and part is vah), stop=(k == K - 1 and part is val))
                    ins.then_inc(S["y_mm"], 1)
                    if not isinstance(i, int) or n >= 1:
                        project(n - 1, (b - 1) % QB)

            peeled(pe, NQ, attend)
            project(NB - 1, QB - 1)


def diffusion_gnn_stack(nc, out, **d):
    sh = Shared()
    sh.NB, sh.N, sh.D = d["x"].shape
    sh.C = sh.N // P
    assert sh.D == P and sh.NB % QB == 0 and sh.N == 512
    with ExitStack() as ctx:
        ctx.enter_context(nc.allow_non_contiguous_dma(reason="a few hundred elements of columns"))
        sb, _ = allocators(nc, ctx)
        sh.X = sb("X", [P, sh.C, sh.NB, sh.D])
        sh.ident = sb("ident", [P, P])
        sh.HALF, sh.PER_D, sh.QUARTER, sh.EPS, sh.ROOT, sh.MINUS = range(6)
        sh.const_values = (0.5, 1.0 / sh.D, 0.25, EPS, -0.5, -1.0)
        sh.const = sb("const", [P, len(sh.const_values), sh.C * QB])
        sh.psum = ctx.enter_context(nc.psum_tensor("psum", [P, 8, 512], F32))
        sh.norm = NormBuffers(sb, sh)
        sh.A = sb("A", [P, sh.C, sh.N])
        with ExitStack() as early:
            esb, _ = allocators(nc, early)
            sh.bias0 = esb("bias0", [P, sh.C, sh.D])
            sh.LT = [(esb(f"LT{r}h", [P, sh.C, sh.N], F32R), esb(f"LT{r}l", [P, sh.C, sh.N], F32R))
                     for r in range(BABY)]
            sh.E = (esb("Eh", [P, BABY, NCO // BABY, sh.D], F32R), esb("El", [P, BABY, NCO // BABY, sh.D], F32R))
            phase_operators(nc, sh, d)
            phase_diffusion(nc, sh, d)

        phase_recurrent(nc, sh, d)
        phase_batchnorm(nc, sh, d)
        phase_attention(nc, sh, d, out)


OUTPUT_SHAPE = (16, 512, 128)


def kernel(**inputs):
    import numpy as np
    import concourse.bacc as bacc
    from concourse.bass_utils import run_bass_kernel_spmd

    nc = bacc.Bacc("TRN2", target_bir_lowering=False, num_devices=1)
    arrays, tensors = {}, {}
    for name, value in inputs.items():
        a = np.ascontiguousarray(value)
        arrays[f"in_{name}"] = a
        tensors[name] = nc.dram_tensor(f"in_{name}", a.shape, mybir.dt.from_np(a.dtype), kind="ExternalInput").ap()
    out = nc.dram_tensor("out", OUTPUT_SHAPE, F32, kind="ExternalOutput").ap()
    diffusion_gnn_stack(nc, out, **tensors)
    results = run_bass_kernel_spmd(nc, [arrays], core_ids=[0])
    return results.results[0]["out"]
```

```python
import math
from contextlib import ExitStack

import concourse.bass as bass
from concourse import mybir

ALU = mybir.AluOpType
ACT = mybir.ActivationFunctionType
AX = mybir.AxisListType
F32 = mybir.dt.float32
F32R = mybir.dt.float32r
I32 = mybir.dt.int32

P = 128
EPS = 1e-5
N_STEPS = 8
DT = 1.0 / N_STEPS
BABY = 3
NCO = N_STEPS + 1
MAX_SKIP = 4
QB = 4
LOWEST = -3.0e38


def binom(n, k):
    return float(math.comb(n, k))


class Shared:
    pass


def wait(eng, sem, value):
    if not isinstance(value, int) or value > 0:
        eng.wait_ge(sem, value)


def peeled(eng, n, step):
    step(0, n == 1)
    if n > 2:
        with eng.Fori(1, n - 1) as i:
            step(i, False)
    if n > 1:
        step(n - 1, True)


def peeled_two(eng, n, step):
    step(0, False)
    step(1, False)
    with eng.Fori(2, n - 1) as i:
        step(i, False)
    step(n - 1, True)


def product(pe, out, lhs, rhs, start=True, stop=True):
    pe.matmul(out, lhs[0], rhs[0], start=start, stop=False)
    pe.matmul(out, lhs[0], rhs[1], start=False, stop=False)
    return pe.matmul(out, lhs[1], rhs[0], start=False, stop=stop)


def low_part(eng, out, full, high):
    return eng.tensor_tensor(out, full, high.bitcast(F32), ALU.subtract)


def allocators(nc, ctx):
    def sb(name, shape, dt=F32):
        return ctx.enter_context(nc.sbuf_tensor(name, shape, dt))

    def sem(name):
        return ctx.enter_context(nc.semaphore(name))

    return sb, sem


def phase_operators(nc, sh, d):
    C, D, N = sh.C, sh.D, sh.N
    with ExitStack() as ctx:
        sb, sem = allocators(nc, ctx)
        w_nat = sb("w_nat", [P, D])
        wT = sb("wT", [P, D])
        wTd = sb("wTd", [P, D])
        fcw = sb("fcw", [P, D])
        dcol = sb("dcol", [P, 1])
        dclip = sb("dclip", [P, 1])
        bcol = sb("bcol", [P, 1])
        alpha = sb("alpha", [P, C])
        gate = sb("gate", [P, C])
        kappa = sb("kappa", [P, C])
        ldiag = sb("ldiag", [P, C])
        L = sb("L", [P, C, N])
        Lh = sb("Lh", [P, C, N], F32R)
        Ll = sb("Ll", [P, C, N], F32R)
        RP = sb("RP", [P, NCO, D])
        Ef = sb("Ef", [P, NCO, D])
        NI = NCO // BABY
        bsel = sb("bsel", [P, NCO, BABY])
        V = sb("V", [BABY, NI, D])
        U = sb("U", [P, C, BABY])
        Uh = sb("Uh", [P, C, BABY], F32R)
        Ul = sb("Ul", [P, C, BABY], F32R)
        UT = sb("UT", [BABY, N])
        b01 = sb("b01", [P, NI - 1, N])
        bt = sb("bt", [P, 2, N])
        bth = sb("bth", [P, 2, C, D], F32R)
        btl = sb("btl", [P, 2, C, D], F32R)
        NE = sh.NE
        K = NE // P
        R = sh.R
        ir = sb("ir", [P, 2, NE], I32)
        icol = sb("icol", [P, 2, K], I32)
        irf = sb("irf", [P, 2, NE])
        icf = sb("icf", [P, 2, K])
        iota = sb("iota", [P, NE], I32)
        iotac = sb("iotac", [P, C], I32)
        iof = sb("iof", [P, NE])
        keyr = sb("keyr", [P, NE])
        keyc = sb("keyc", [P, K])
        less = sb("less", [P, K, NE])
        pos = sb("pos", [P, K])
        perm = sb("perm", [P, K, NE])
        idxb = sb("idxb", [P, 2, K, P])
        Gs = sb("Gs", [P, C, NE])
        Gd = sb("Gd", [P, C, NE])
        sel = sb("sel", [P, C, NE])
        ones = sb("ones", [P, P])
        tiny = sb("tiny", [P, 1])
        rsum = sb("rsum", [P, C])
        dsum = sb("dsum", [P, C])
        deg = sb("deg", [P, C])
        dblock = sb("dblock", [P, C, P])
        names = ("w_in", "fc_in", "a_in", "small_in", "x_in", "idn", "memsets", "pe_tile", "dve_tile",
                 "hi_done", "gate_done", "l_done", "lh_done", "ll_done", "own", "bsel_done", "eh_done", "e_done",
                 "u_done", "xh_done", "i_in", "iota_done", "perm_done", "g_done", "deg_done",
                 "dinv_done", "diag_done", "sel_done")
        S = {n: sem(n) for n in names}

        order = ["wT", "R", *(f"LT{j}" for j in range(C)), "R2", "UT", "L2T0", "R34", "L2T1", "R58", "L2T2", "FR03",
                 "L2T3", "FR47", "FR8V", "L3T0", "B2", "L3T1", "B01T0", "B01T1", "L3T2", "L3T3", "SMALL", "T", "PERM", "T'",
                 "ROWS0", "ROWS1", "S", "DROW", "S'", "LG"]
        at = {n: i for i, n in enumerate(order)}
        his = [n for n in order if n[:2] in ("LT", "L2", "L3", "B2", "T'")]

        def bank(name):
            return sh.psum[:, at[name] % 8, :]

        def by_node(name):
            return bank(name).rearrange("p (c d) -> p c d", d=D)

        def node_power(name):
            return (0 if name[1] == "T" else int(name[1]) - 1), int(name[-1])

        ALL_SET = 4 + len(sh.const_values) + 2

        block = ctx.enter_context(nc.Block())

        @block.sync
        def _(sp):
            sp.dma_start(w_nat[:, :], d["L0_gnn_w"]).then_inc(S["w_in"], 16)
            sp.dma_start(sh.A[:, :, :], d["adj"].rearrange("(c p) m -> p c m", p=P)).then_inc(S["a_in"], 16)
            for k, name in enumerate(("src", "dst")):
                sp.dma_start(ir[:, k, :], d[f"L3_gnn_{name}"].rearrange("(o e) -> o e", o=1)
                             .broadcast_to([P, NE])).then_inc(S["i_in"], 16)
                sp.dma_start(icol[:, k, :], d[f"L3_gnn_{name}"].rearrange("(k p) -> p k", p=P))\
                    .then_inc(S["i_in"], 16)
            xv = d["x"].rearrange("b (c p) d -> p c b d", p=P)
            for q in range(sh.NB // QB):
                for c in range(C):
                    sp.dma_start(sh.X[:, c, q * QB:(q + 1) * QB, :], xv[:, c, q * QB:(q + 1) * QB, :])\
                        .then_inc(S["x_in"], 16)
            sp.wait_ge(S["x_in"], 16 * C * (sh.NB // QB))

        @block.gpsimd
        def _(pool):
            pool.memset(sh.ident[:, :], 0.0).then_inc(S["memsets"], 1)
            pool.memset(bsel[:, :, :], 0.0).then_inc(S["memsets"], 1)
            pool.memset(U[:, :, 0:1], 0.0).then_inc(S["memsets"], 1)
            pool.memset(U[:, :, 1:2], 1.0).then_inc(S["memsets"], 1)
            pool.wait_ge(S["memsets"], 1)
            pool.affine_select(out=sh.ident[:, :], in_=sh.ident[:, :], compare_op=ALU.not_equal, fill=1.0,
                               base=0, pattern=[[-1, P]], channel_multiplier=1).then_inc(S["idn"], 1)
            for k, value in enumerate(sh.const_values):
                pool.memset(sh.const[:, k, :], value).then_inc(S["memsets"], 1)
            pool.memset(tiny[:, :], 1e-8).then_inc(S["memsets"], 1)
            pool.memset(ones[:, :], 1.0).then_inc(S["memsets"], 1)
            pool.iota(iota[:, :], pattern=[[1, NE]], base=0, channel_multiplier=0).then_inc(S["iota_done"], 1)
            pool.iota(iotac[:, :], pattern=[[P, C]], base=0, channel_multiplier=1).then_inc(S["iota_done"], 1)
            pool.wait_ge(S["memsets"], ALL_SET)
            pool.wait_ge(S["deg_done"], 1)
            pool.tensor_tensor(sh.dinv[:, :], deg[:, :], sh.const[:, sh.ROOT, 0:C], ALU.pow)\
                .then_inc(S["dinv_done"], 1)
            for c in range(C):
                pool.wait_ge(S["xh_done"], c + 1)
                low_part(pool, sh.Xl[:, c, :, :], sh.X[:, c, 0:QB, :], sh.Xh[:, c, :, :])

        @block.scalar
        def _(act):
            act.dma_start(alpha[:, :], d["L0_gnn_alpha_train"].rearrange("(c p) -> p c", p=P))\
                .then_inc(S["small_in"], 16)
            act.dma_start(dcol[:, :], d["L0_gnn_d"].rearrange("(p o) -> p o", o=1)).then_inc(S["small_in"], 16)
            act.dma_start(bcol[:, :], d["L0_gnn_fc_in_b"].rearrange("(p o) -> p o", o=1))\
                .then_inc(S["small_in"], 16)
            act.dma_start(fcw[:, :], d["L0_gnn_fc_in_w"]).then_inc(S["fc_in"], 16)
            act.wait_ge(S["small_in"], 48)
            act.activation(gate[:, :], alpha[:, :], ACT.Sigmoid).then_inc(S["gate_done"], 1)
            for c in range(C):
                act.wait_ge(S["l_done"], c + 1)
                act.activation(Lh[:, c, :], L[:, c, :], ACT.Copy).then_inc(S["lh_done"], 1)
            for name in his:
                if name == "T'":
                    act.wait_ge(S["x_in"], 16 * C * (sh.NB // QB))
                    for c in range(C):
                        act.activation(sh.Xh[:, c, :, :], sh.X[:, c, 0:QB, :], ACT.Copy).then_inc(S["xh_done"], 1)
                act.wait_ge(S["pe_tile"], at[name] + 1)
                if name in ("B2", "T'"):
                    act.activation(bth[:, int(name != "B2"), :, :], by_node(name), ACT.Copy)\
                        .then_inc(S["hi_done"], 1)
                    continue
                r, j = node_power(name)
                act.activation(sh.LT[r][0][:, j, :], bank(name), ACT.Copy).then_inc(S["hi_done"], 1)
                if name == f"L2T{C - 1}":
                    act.wait_ge(S["e_done"], 1)
                    act.activation(sh.E[0][:, :, :, :], Ef[:, :, :].rearrange("p (i r) d -> p r i d", r=BABY),
                                   ACT.Copy).then_inc(S["eh_done"], 1)
            act.wait_ge(S["pe_tile"], at["LG"] + 1)
            act.wait_ge(S["memsets"], ALL_SET)
            act.activation(sh.lg[:, :], bank("LG")[0:R, 0:NE], ACT.Ln, bias=tiny[0:R, 0:1])

        @block.vector
        def _(dve):
            chain = [0]

            def link(ins):
                chain[0] += 1
                ins.then_inc(S["own"], 1)
                dve.wait_ge(S["own"], chain[0])

            def tile(name):
                dve.wait_ge(S["pe_tile"], at[name] + 1)

            dve.wait_ge(S["gate_done"], 1)
            link(dve.tensor_scalar(kappa[:, :], gate[:, :], 0.5 * DT, None, ALU.mult))
            dve.tensor_scalar(dclip[:, :], dcol[:, :], 0.0, 1.0, ALU.max, ALU.min)
            link(dve.tensor_scalar(ldiag[:, :], kappa[:, :], -1.0, 1.0 - DT, ALU.mult, ALU.add))
            tile("wT")
            link(dve.tensor_copy(wT[:, :], bank("wT")[:, 0:D]))
            dve.tensor_scalar(wTd[:, :], wT[:, :], dclip[:, 0:1], DT, ALU.mult, ALU.mult)\
                .then_inc(S["dve_tile"], 1)
            dve.wait_ge(S["a_in"], 16)
            dve.wait_ge(S["idn"], 1)
            for c in range(C):
                link(dve.tensor_scalar(L[:, c, :], sh.A[:, c, :], kappa[:, c:c + 1], None, ALU.mult))
                own = L[:, c, c * P:(c + 1) * P]
                dve.scalar_tensor_tensor(own, sh.ident[:, :], ldiag[:, c:c + 1], own, ALU.mult, ALU.add)\
                    .then_inc(S["l_done"], 1)
            for c in range(C):
                dve.wait_ge(S["lh_done"], c + 1)
                low_part(dve, Ll[:, c, :], L[:, c, :], Lh[:, c, :]).then_inc(S["ll_done"], 1)
            tile("R")
            dve.tensor_copy(RP[:, 0, :], sh.ident[:, :])
            dve.tensor_copy(RP[:, 1, :], bank("R")[:, 0:D]).then_inc(S["dve_tile"], 1)

            def split(name):
                dve.wait_ge(S["hi_done"], his.index(name) + 1)
                r, j = node_power(name)
                low_part(dve, sh.LT[r][1][:, j, :], bank(name), sh.LT[r][0][:, j, :]).then_inc(S["dve_tile"], 1)

            def copy(name, out, src):
                tile(name)
                dve.tensor_copy(out, src).then_inc(S["dve_tile"], 1)

            for c in range(C):
                ins = dve.reduce_sum(U[:, c, 2:3], L[:, c, :], AX.X)
            dve.wait_ge(S["memsets"], 4)
            link(ins)
            link(dve.tensor_copy(Uh[:, :, :], U[:, :, :]))
            low_part(dve, Ul[:, :, :], U[:, :, :], Uh[:, :, :]).then_inc(S["u_done"], 1)
            for j in range(C):
                split(f"LT{j}")
            copy("R2", RP[:, 2, :], bank("R2")[:, 0:D])
            tile("UT")
            link(dve.tensor_copy(UT[:, :], bank("UT")[0:BABY, :]))
            dve.memset(UT[0:1, :], 1.0).then_inc(S["dve_tile"], 1)
            split("L2T0")
            copy("R34", RP[:, 3:5, :], bank("R34")[:, 0:2 * D].rearrange("p (k d) -> p k d", d=D))
            for j in range(NCO):
                ins = dve.tensor_scalar(bsel[:, j, j % BABY:j % BABY + 1], bcol[:, 0:1], binom(N_STEPS, j), None,
                                        ALU.mult)
            ins.then_inc(S["bsel_done"], 1)
            split("L2T1")
            copy("R58", RP[:, 5:9, :], bank("R58").rearrange("p (k d) -> p k d", d=D))
            dve.wait_ge(S["iota_done"], 2)
            dve.wait_ge(S["i_in"], 64)
            dve.wait_ge(S["memsets"], ALL_SET)
            dve.tensor_copy(iof[:, :], iota[:, :])
            dve.tensor_copy(sh.ioc[:, :], iotac[:, :])
            dve.tensor_copy(icf[:, :, :], icol[:, :, :])
            link(dve.tensor_copy(irf[:, :, :], ir[:, :, :]))
            dve.scalar_tensor_tensor(keyr[:, :], irf[:, 0, :], float(NE), iof[:, :], ALU.mult, ALU.add)
            link(dve.scalar_tensor_tensor(keyc[:, :], icf[:, 0, :], float(NE), sh.ioc[:, 0:K], ALU.mult, ALU.add))
            for k in range(K):
                ins = dve.tensor_scalar(less[:, k, :], keyr[:, :], keyc[:, k:k + 1], None, ALU.is_lt)
            link(ins)
            link(dve.reduce_sum(pos[:, :], less[:, :, :], AX.X))
            for k in range(K):
                dve.tensor_scalar(perm[:, k, :], iof[:, :], pos[:, k:k + 1], None, ALU.is_equal)
                for j in (0, 1):
                    ins = dve.tensor_scalar(idxb[:, j, k, :], ones[:, :], icf[:, j, k:k + 1], None, ALU.mult)
            ins.then_inc(S["perm_done"], 1)
            split("L2T2")

            def start_e(name, k0, n):
                tile(name)
                for k in range(n):
                    j = N_STEPS - k0 - k
                    ins = dve.tensor_scalar(Ef[:, j, :], bank(name)[:, k * D:(k + 1) * D], binom(N_STEPS, j),
                                            None, ALU.mult)
                return ins

            start_e("FR03", 0, 4).then_inc(S["dve_tile"], 1)
            split("L2T3")
            for c in range(C):
                dve.reduce_sum(sh.rs[:, c:c + 1], sh.A[:, c, :], AX.X)
            for c in range(C):
                ins = dve.tensor_tensor(dblock[:, c, :], sh.A[:, c, c * P:(c + 1) * P], sh.ident[:, :], ALU.mult)
            link(ins)
            link(dve.reduce_sum(dsum[:, :], dblock[:, :, :], AX.X))
            link(dve.scalar_tensor_tensor(rsum[:, :], sh.rs[:, :], 1.0, dsum[:, :], ALU.add, ALU.subtract))
            start_e("FR47", 4, 4).then_inc(S["dve_tile"], 1)
            start_e("FR8V", 8, 1)
            dve.tensor_copy(V[:, :, :], bank("FR8V")[0:BABY, D:(NI + 1) * D].rearrange("p (i d) -> p i d", d=D))\
                .then_inc(S["dve_tile"], 1)
            dve.wait_ge(S["dve_tile"], at["FR8V"] + 1)
            for i in range(N_STEPS):
                for j in range(N_STEPS - i):
                    ins = dve.scalar_tensor_tensor(Ef[:, j, :], RP[:, i, :], DT * binom(i + j, j), Ef[:, j, :],
                                                   ALU.mult, ALU.add)
                if i < N_STEPS - 1:
                    link(ins)
            ins.then_inc(S["e_done"], 1)

            def low_bias(name, k):
                dve.wait_ge(S["hi_done"], his.index(name) + 1)
                low_part(dve, btl[:, k, :, :], by_node(name), bth[:, k, :, :]).then_inc(S["dve_tile"], 1)

            split("L3T0")
            dve.wait_ge(S["eh_done"], 1)
            low_part(dve, sh.E[1][:, :, :, :], Ef[:, :, :].rearrange("p (i r) d -> p r i d", r=BABY),
                     sh.E[0][:, :, :, :])
            low_bias("B2", 0)
            split("L3T1")
            for i in (0, 1):
                copy(f"B01T{i}", b01[:, i, :], bank(f"B01T{i}"))
            split("L3T2")
            split("L3T3")
            tile("SMALL")
            dve.tensor_tensor(deg[:, :], bank("SMALL")[:, 0:C], rsum[:, :], ALU.add).then_inc(S["deg_done"], 1)
            dve.tensor_copy(sh.sc[:, :], bank("SMALL")[:, C:C + K]).then_inc(S["dve_tile"], 1)
            tile("T")
            dve.tensor_tensor(bt[:, 0, :], bank("T"), b01[:, 1, :], ALU.add).then_inc(S["dve_tile"], 1)
            tile("PERM")
            dve.tensor_copy(sh.ss[:, :, :], bank("PERM").rearrange("p (j e) -> p j e", j=2)).then_inc(S["dve_tile"], 1)
            low_bias("T'", 1)
            dve.wait_ge(S["dve_tile"], at["T'"] + 1)
            for c in range(C):
                ins = dve.tensor_scalar(Gs[:, c, :], sh.ss[:, 0, :], sh.ioc[:, c:c + 1], None, ALU.is_equal)
            ins.then_inc(S["g_done"], 1)
            for c in range(C):
                dve.tensor_scalar(Gd[:, c, :], sh.ss[:, 1, :], sh.ioc[:, c:c + 1], None, ALU.is_equal)
            dve.wait_ge(S["dinv_done"], 1)
            for c in range(C):
                ins = dve.tensor_scalar(dblock[:, c, :], sh.ident[:, :], sh.dinv[:, c:c + 1], None, ALU.mult)
            ins.then_inc(S["diag_done"], 1)
            dve.wait_ge(S["diag_done"], 1)
            for i in (0, 1):
                tile(f"ROWS{i}")
                ins = dve.tensor_tensor(sel[:, 2 * i:2 * i + 2, :],
                                        bank(f"ROWS{i}").rearrange("p (c e) -> p c e", e=NE),
                                        Gd[:, 2 * i:2 * i + 2, :], ALU.mult)
                if i == 0:
                    ins.then_inc(S["dve_tile"], 1)
            ins.then_inc(S["dve_tile"], 1)
            tile("S")
            dve.tensor_tensor(bt[:, 1, :], bank("S"), b01[:, 0, :], ALU.add).then_inc(S["dve_tile"], 1)
            copy("DROW", sh.drow[:, :], bank("DROW"))
            copy("S'", sh.bias0[:, :, :], by_node("S'"))

        @block.tensor
        def _(pe):
            def begin(name, needs=()):
                upto = max([at[name] - 7] + [at[n] + 1 for n in needs])
                if upto > 0:
                    pe.wait_ge(S["dve_tile"], upto)

            def done(ins):
                ins.then_inc(S["pe_tile"], 1)

            pe.wait_ge(S["w_in"], 16)
            pe.wait_ge(S["idn"], 1)
            done(pe.transpose(bank("wT")[:, 0:D], w_nat[:, :], sh.ident[:, :]))
            begin("R", ["wT"])
            done(pe.matmul(bank("R")[:, 0:D], wTd[:, :], wT[:, :], start=True, stop=True))
            pe.wait_ge(S["l_done"], C)
            for j in range(C):
                for c in range(C):
                    ins = pe.transpose(bank(f"LT{j}")[:, c * P:(c + 1) * P], L[:, c, j * P:(j + 1) * P],
                                       sh.ident[:, :])
                done(ins)
            def r_power(name, k, n):
                done(pe.matmul(bank(name)[:, 0:n * D], RP[:, k, :], RP[:, 1:n + 1, :], start=True, stop=True))

            def l_power(r, j, needs):
                begin(f"L{r}T{j}", [needs])
                for k in range(C):
                    rows = slice(j * P, (j + 1) * P)
                    ins = product(pe, bank(f"L{r}T{j}"), (Lh[:, k, rows], Ll[:, k, rows]),
                                  (sh.LT[r - 2][0][:, k, :], sh.LT[r - 2][1][:, k, :]),
                                  start=(k == 0), stop=(k == C - 1))
                done(ins)

            def bias_horner(name, k, needs):
                begin(name, needs)
                for c in range(C):
                    ins = product(pe, bank(name), (bth[:, k, c, :], btl[:, k, c, :]),
                                  (sh.LT[2][0][:, c, :], sh.LT[2][1][:, c, :]), start=(c == 0), stop=(c == C - 1))
                done(ins)

            def turned(name, k):
                begin(name + "'", [name])
                for c in range(C):
                    cols = slice(c * P, (c + 1) * P)
                    ins = pe.transpose(bank(name + "'")[:, cols], bt[:, k, cols], sh.ident[:, :])
                done(ins)

            begin("R2", ["R"])
            r_power("R2", 1, 1)
            begin("UT", [f"LT{C - 1}"])
            pe.wait_ge(S["u_done"], 1)
            for k in range(C):
                ins = product(pe, bank("UT")[0:BABY, :], (Uh[:, k, :], Ul[:, k, :]),
                              (sh.LT[0][0][:, k, :], sh.LT[0][1][:, k, :]), start=(k == 0), stop=(k == C - 1))
            done(ins)
            pe.wait_ge(S["ll_done"], C)
            l_power(2, 0, f"LT{C - 1}")
            begin("R34", ["R2"])
            r_power("R34", 2, 2)
            l_power(2, 1, f"LT{C - 1}")
            begin("R58", ["R34"])
            r_power("R58", 4, 4)
            l_power(2, 2, f"LT{C - 1}")
            begin("FR03", ["R58"])
            pe.wait_ge(S["fc_in"], 16)
            done(pe.matmul(bank("FR03"), fcw[:, :], RP[:, 0:4, :], start=True, stop=True))
            l_power(2, 3, f"LT{C - 1}")
            begin("FR47")
            done(pe.matmul(bank("FR47"), fcw[:, :], RP[:, 4:8, :], start=True, stop=True))
            begin("FR8V")
            pe.matmul(bank("FR8V")[:, 0:D], fcw[:, :], RP[:, 8, :], start=True, stop=True)
            pe.wait_ge(S["bsel_done"], 1)
            for j in range(NCO):
                i, r = divmod(j, BABY)
                ins = pe.matmul(bank("FR8V")[0:BABY, (i + 1) * D:(i + 2) * D], bsel[:, j, :], RP[:, N_STEPS - j, :],
                                start=(r == 0), stop=(r == BABY - 1))
            done(ins)
            l_power(3, 0, f"L2T{C - 1}")
            begin("B2", ["FR8V"])
            for c in range(C):
                ins = pe.matmul(bank("B2")[:, c * D:(c + 1) * D], UT[:, c * P:(c + 1) * P], V[:, NI - 1, :],
                                start=True, stop=True)
            done(ins)
            l_power(3, 1, f"L2T{C - 1}")
            for i in (0, 1):
                begin(f"B01T{i}")
                done(pe.matmul(bank(f"B01T{i}"), V[:, i, :], UT[:, :], start=True, stop=True))
            l_power(3, 2, f"L2T{C - 1}")
            l_power(3, 3, f"L2T{C - 1}")
            begin("SMALL")
            pe.wait_ge(S["memsets"], ALL_SET)
            for c2 in range(C):
                for c in range(C):
                    pe.matmul(bank("SMALL")[:, c2:c2 + 1], sh.A[:, c, c2 * P:(c2 + 1) * P], ones[:, 0:1],
                              start=(c == 0), stop=(c == C - 1))
            pe.wait_ge(S["perm_done"], 1)
            for q in range(K):
                for k in range(K):
                    ins = pe.matmul(bank("SMALL")[:, C + q:C + q + 1], perm[:, k, q * P:(q + 1) * P],
                                    icf[:, 0, k:k + 1], start=(k == 0), stop=(k == K - 1))
            done(ins)
            bias_horner("T", 0, [f"L3T{C - 1}", "B2"])
            begin("PERM")
            for j in (0, 1):
                for k in range(K):
                    ins = pe.matmul(bank("PERM")[:, j * NE:(j + 1) * NE], idxb[:, j, k, :], perm[:, k, :],
                                    start=(k == 0), stop=(k == K - 1))
            done(ins)
            turned("T", 0)
            for i in (0, 1):
                begin(f"ROWS{i}")
                pe.wait_ge(S["g_done"], 1)
                for m in (2 * i, 2 * i + 1):
                    for c in range(C):
                        ins = pe.matmul(bank(f"ROWS{i}")[:, (m % 2) * NE:(m % 2 + 1) * NE],
                                        sh.A[:, c, m * P:(m + 1) * P], Gs[:, c, :], start=(c == 0), stop=(c == C - 1))
                done(ins)
            bias_horner("S", 1, ["T'"])
            begin("DROW")
            pe.wait_ge(S["diag_done"], 1)
            done(pe.matmul(bank("DROW"), ones[:, :], dblock[:, :, :], start=True, stop=True))
            turned("S", 1)
            begin("LG", ["ROWS1"])
            for c in range(C):
                ins = pe.matmul(bank("LG")[0:R, 0:NE], ones[:, 0:R], sel[:, c, :], start=(c == 0),
                                stop=(c == C - 1))
            done(ins)


SHIFT_LINKS = 6


def norm_scales(pool, sh, n, stats, work, mean, rstd, own, before, shift, free=None):
    a, b, c = (work[:, k, 0:n] for k in range(3))

    def const(k):
        return sh.const[:, k, 0:n]

    def link(k, ins):
        ins.then_inc(own, 1)
        pool.wait_ge(own, before + k)

    pool.tensor_tensor(a, stats[:, :, 1], stats[:, :, 4], ALU.add)
    pool.tensor_tensor(b, stats[:, :, 1], stats[:, :, 4], ALU.subtract)
    link(1, pool.tensor_tensor(c, stats[:, :, 2], stats[:, :, 5], ALU.add))
    pool.tensor_tensor(mean, a, const(sh.HALF), ALU.mult)
    pool.tensor_tensor(c, c, const(sh.PER_D), ALU.mult)
    link(2, pool.tensor_tensor(b, b, b, ALU.mult))
    link(3, pool.tensor_tensor(b, b, const(sh.QUARTER), ALU.mult))
    link(4, pool.tensor_tensor(b, b, c, ALU.add))
    link(5, pool.tensor_tensor(b, b, const(sh.EPS), ALU.add))
    if free is None:
        free = lambda: None
    pool.tensor_tensor(mean, mean, const(sh.MINUS), ALU.mult)
    link(6, pool.tensor_tensor(a, b, const(sh.ROOT), ALU.pow))
    free()
    pool.tensor_tensor(rstd, a, const(sh.ONE), ALU.mult)
    return pool.tensor_tensor(shift, mean, a, ALU.mult)


class NormBuffers:

    def __init__(self, sb, sem, sh):
        self.sh = sh
        self.rows = QB * sh.C
        self.stats = sb("nstats", [P, sh.NB * sh.C, 6])
        self.work = sb("nwork", [P, 3, self.rows])
        self.mean = sb("nmean", [P, self.rows])
        self.scale = sb("nscale", [P, self.rows])
        self.shift = sb("nshift", [P, self.rows])
        self.own = sem("norm_own")
        self.ready = sem("norm_ready")

    def row_stats(self, dve, n, c):
        return dve.bn_stats(self.stats[:, bass.ds(self.sh.C * n + c, 1), :], self.sh.X[:, c, bass.ds(n, 1), :])

    def take_stats(self, dve, n):
        for c in range(self.sh.C):
            ins = self.row_stats(dve, n, c)
        return ins

    def scales(self, pool, g, own, before, free=None):
        return norm_scales(pool, self.sh, self.rows, self.stats[:, bass.ds(self.rows * g, self.rows), :],
                           self.work, self.mean[:, :], self.scale[:, :], own, before, self.shift[:, :], free)

    def apply_on_dve(self, dve, n, b, chunks=None, other=None):
        scale, shift = other or (self.scale, self.shift)
        C = self.sh.C
        for c in range(C) if chunks is None else chunks:
            k = b * C + c
            row = self.sh.X[:, c, bass.ds(n, 1), :]
            ins = dve.tensor_scalar(row, row, scale[:, k:k + 1], shift[:, k:k + 1], ALU.mult, ALU.add)
        return ins


    def finish_scales(self, pool, earlier):
        self.scales(pool, self.sh.NB // QB - 1, self.own, SHIFT_LINKS * earlier).then_inc(self.ready, 1)

    def finish(self, act, earlier, done, batches=range(QB)):
        act.wait_ge(self.ready, earlier + 1)
        for b in batches:
            self.apply(act, self.sh.NB - QB + b, b).then_inc(done, 1)

    def apply(self, act, n, b, chunks=None, other=None):
        scale, shift = other or (self.scale, self.shift)
        C = self.sh.C
        for c in range(C) if chunks is None else chunks:
            k = b * C + c
            row = self.sh.X[:, c, bass.ds(n, 1), :]
            ins = act.activation(row, row, ACT.Identity, bias=shift[:, k:k + 1], scale=scale[:, k:k + 1])
        return ins


def phase_diffusion(nc, sh, d):
    C, D, N = sh.C, sh.D, sh.N
    NQ = sh.NB // QB
    with ExitStack() as ctx:
        sb, sem = allocators(nc, ctx)
        Xh, Xl = sh.Xh, sh.Xl
        norm = sh.norm
        yh = sb("yh", [P, 2, BABY, N], F32R)
        yl = sb("yl", [P, 2, BABY, N], F32R)
        B2h = sb("B2h", [P, C, QB, D], F32R)
        B2l = sb("B2l", [P, C, QB, D], F32R)
        B01 = sb("B01", [P, C, QB, 2, D])
        tq = sb("tq", [P, C, QB, D])
        th = sb("th", [P, C, QB, D], F32R)
        tl = sb("tl", [P, C, QB, D], F32R)
        names = ("pe_tile", "dve_tile", "hi_done", "xh_done", "xl_done", "xb_done", "th_done", "tl_done",
                 "sum2", "stat_done", "norm_own", "rstd_done", "x1_done")
        S = {n: sem("d_" + n) for n in names}

        work = [("B", 0), ("Y", 2), ("B", 1), ("Y", 3), ("B", 2), ("B", 3), ("Y+", 0), ("T", 0), ("Y+", 1),
                ("S", 0)]
        TILES = 4 * len(work)
        HEAD = 8
        HIS = {"Y": 3, "Y+": 3, "B": 4, "T": 0, "S": 0}
        HI_QUAD = sum(HIS[k] for k, _ in work)
        HI_HEAD = 6

        def steps(g, last):
            hi = 0
            for i, (kind, b) in enumerate(work):
                if not (last and kind == "Y+"):
                    skipped = sum(k == "Y+" for k, _ in work[:i]) if last else 0
                    yield kind, b, HEAD + g * TILES + 4 * (i - skipped), 4 * (i - skipped) % 8, \
                        HI_HEAD + g * HI_QUAD + hi
                    hi += HIS[kind]

        block = ctx.enter_context(nc.Block())

        def ready(eng, n, k):
            eng.wait_ge(S["pe_tile"], n + k + 1)

        @block.tensor
        def _(pe):
            def free(n, k, first=False):
                if not first:
                    pe.wait_ge(S["dve_tile"], n + k - 7)

            def Y(b, n, bk, first=False):
                for k in range(4):
                    free(n, k, first)
                    o = sh.psum[:, bk + k, :]
                    if k < 2:
                        src = (Xh, Xl)[k]
                        for c in range(C):
                            ins = pe.transpose(o[:, c * P:(c + 1) * P], src[:, c, b, :].bitcast(F32),
                                               sh.ident[:, :])
                    else:
                        for c in range(C):
                            ins = product(pe, o, (Xh[:, c, b, :], Xl[:, c, b, :]),
                                          (sh.LT[k - 2][0][:, c, :], sh.LT[k - 2][1][:, c, :]),
                                          start=(c == 0), stop=(c == C - 1))
                    ins.then_inc(S["pe_tile"], 1)

            def B(b, n, bk, y_end):
                pe.wait_ge(S["dve_tile"], y_end)
                for c in range(C):
                    free(n, c)
                    cols = slice(c * P, (c + 1) * P)
                    for r in range(BABY):
                        ins = product(pe, sh.psum[:, bk + c, 0:BABY * D],
                                      (yh[:, b % 2, r, cols], yl[:, b % 2, r, cols]),
                                      (sh.E[0][:, r, :, :], sh.E[1][:, r, :, :]),
                                      start=(r == 0), stop=(r == BABY - 1))
                    ins.then_inc(S["pe_tile"], 1)

            def horner(n, bk, hi, lo):
                for c2 in range(C):
                    free(n, c2)
                    cols = slice(c2 * P, (c2 + 1) * P)
                    for c in range(C):
                        ins = product(pe, sh.psum[:, bk + c2, :],
                                      (sh.LT[2][0][:, c, cols], sh.LT[2][1][:, c, cols]),
                                      (hi[:, c, :, :], lo[:, c, :, :]), start=(c == 0), stop=(c == C - 1))
                    ins.then_inc(S["pe_tile"], 1)

            def quad(g, last):
                start = HEAD + g * TILES
                y_end = {0: start - 4, 1: start}
                for kind, b, n, bk, _ in steps(g, last):
                    if kind in ("Y", "Y+"):
                        if kind == "Y+" and b == 0:
                            pe.wait_ge(S["xl_done"], C * (g + 1))
                        Y(b, n, bk)
                        y_end[b] = n + 4
                    elif kind == "B":
                        B(b, n, bk, y_end[b])
                        b_end = n + 4
                    elif kind == "T":
                        pe.wait_ge(S["dve_tile"], b_end)
                        horner(n, bk, B2h, B2l)
                    else:
                        pe.wait_ge(S["tl_done"], C * (g + 1))
                        horner(n, bk, th, tl)

            Y(0, 0, 0, first=True)
            Y(1, 4, 4, first=True)
            with pe.Fori(0, NQ - 1) as g:
                quad(g, False)
            quad(NQ - 1, True)

        @block.scalar
        def _(act):
            def split_x(g):
                for c in range(C):
                    act.activation(Xh[:, c, :, :], sh.X[:, c, bass.ds(QB * g, QB), :], ACT.Copy)\
                        .then_inc(S["xh_done"], 1)

            def Y(b, n, bk):
                for k, r in ((0, 0), (2, 1), (3, 2)):
                    ready(act, n, k)
                    act.activation(yh[:, b % 2, r, :], sh.psum[:, bk + k, :], ACT.Copy)\
                        .then_inc(S["hi_done"], 1)

            def quad(g, last):
                for kind, b, n, bk, _ in steps(g, last):
                    if kind in ("Y", "Y+"):
                        Y(b, n, bk)
                        if kind == "Y" and b == QB - 1:
                            if not last:
                                split_x(g + 1)
                            if not isinstance(g, int) or g > 0:
                                act.wait_ge(S["rstd_done"], g)
                                for n_ in range(QB):
                                    norm.apply(act, QB * (g - 1) + n_, n_).then_inc(S["x1_done"], 1)
                    elif kind == "B":
                        if b == 0:
                            act.wait_ge(S["dve_tile"], n)
                        for c in range(C):
                            ready(act, n, c)
                            act.activation(B2h[:, c, b, :], sh.psum[:, bk + c, 2 * D:3 * D], ACT.Copy)
                            act.activation(B01[:, c, b, :, :],
                                           sh.psum[:, bk + c, 0:2 * D].rearrange("p (i d) -> p i d", d=D),
                                           ACT.Copy).then_inc(S["hi_done"], 1)
                    elif kind == "T":
                        for c in range(C):
                            act.wait_ge(S["dve_tile"], n + c + 1)
                            act.activation(th[:, c, :, :], tq[:, c, :, :], ACT.Copy).then_inc(S["th_done"], 1)

            Y(0, 0, 0)
            Y(1, 4, 4)
            peeled(act, NQ, quad)

        @block.vector
        def _(dve):
            def Y(b, n, bk, hi):
                dve.wait_ge(S["hi_done"], hi + 1)
                ready(dve, n, 1)
                dve.tensor_copy(yl[:, b % 2, 0, :], sh.psum[:, bk + 1, :]).then_inc(S["dve_tile"], 2)
                for k in (2, 3):
                    dve.wait_ge(S["hi_done"], hi + k)
                    low_part(dve, yl[:, b % 2, k - 1, :], sh.psum[:, bk + k, :], yh[:, b % 2, k - 1, :])\
                        .then_inc(S["dve_tile"], 1)

            def quad(g, last):
                for kind, b, n, bk, hi in steps(g, last):
                    if kind in ("Y", "Y+"):
                        Y(b, n, bk, hi)
                    elif kind == "B":
                        for c in range(C):
                            dve.wait_ge(S["hi_done"], hi + c + 1)
                            low_part(dve, B2l[:, c, b, :], sh.psum[:, bk + c, 2 * D:3 * D], B2h[:, c, b, :])\
                                .then_inc(S["dve_tile"], 1)
                    elif kind == "T":
                        for c in range(C):
                            ready(dve, n, c)
                            dve.tensor_tensor(tq[:, c, :, :],
                                              sh.psum[:, bk + c, :].rearrange("p (b d) -> p b d", d=D),
                                              B01[:, c, :, 1, :], ALU.add).then_inc(S["dve_tile"], 1)
                    else:
                        for c in range(C):
                            ready(dve, n, c)
                            dve.tensor_tensor(tq[:, c, :, :],
                                              sh.psum[:, bk + c, :].rearrange("p (b d) -> p b d", d=D),
                                              B01[:, c, :, 0, :], ALU.add).then_inc(S["dve_tile"], 1)
                            if c == 0:
                                dve.wait_ge(S["xb_done"], C * (g + 1))
                            dve.wait_ge(S["dve_tile"], n + c + 1)
                            xq = sh.X[:, c, bass.ds(QB * g, QB), :]
                            dve.tensor_tensor(xq, tq[:, c, :, :], xq, ALU.add).then_inc(S["sum2"], 1)
                            dve.wait_ge(S["sum2"], C * g + c + 1)
                            for b in range(QB):
                                ins = norm.row_stats(dve, QB * g + b, c)
                            ins.then_inc(S["stat_done"], 1)

            Y(0, 0, 0, 0)
            Y(1, 4, 4, 3)
            peeled(dve, NQ, quad)

        @block.gpsimd
        def _(pool):
            def split_x(g):
                for c in range(C):
                    pool.wait_ge(S["xh_done"], C * (g - 1) + c + 1)
                    low_part(pool, Xl[:, c, :, :], sh.X[:, c, bass.ds(QB * g, QB), :], Xh[:, c, :, :])\
                        .then_inc(S["xl_done"], 1)

            def quad(g, last):
                wait(pool, S["xl_done"], C * g)
                for c in range(C):
                    xq = sh.X[:, c, bass.ds(QB * g, QB), :]
                    pool.tensor_tensor(xq, xq, sh.bias0[:, c:c + 1, :].broadcast_to([P, QB, D]), ALU.add)\
                        .then_inc(S["xb_done"], 1)
                if not last:
                    split_x(g + 1)
                for c in range(C):
                    pool.wait_ge(S["th_done"], C * g + c + 1)
                    low_part(pool, tl[:, c, :, :], tq[:, c, :, :], th[:, c, :, :]).then_inc(S["tl_done"], 1)
                if not last:
                    pool.wait_ge(S["stat_done"], C * (g + 1))
                    wait(pool, S["x1_done"], QB * g)
                    norm.scales(pool, g, S["norm_own"], SHIFT_LINKS * g).then_inc(S["rstd_done"], 1)

            peeled(pool, NQ, quad)


def phase_recurrent(nc, sh, d):
    C, D, N = sh.C, sh.D, sh.N
    NQ = sh.NB // QB
    I, F, G, O = range(4)
    with ExitStack() as ctx:
        sb, sem = allocators(nc, ctx)
        AT = (sb("ATh", [P, C, N], F32R), sb("ATl", [P, C, N], F32R))
        ATh, ATl = AT
        Wg = [sb(f"Wg{i}", [P, D]) for i in (0, 1)]
        Wgs = [(sb(f"Wg{i}h", [P, D], F32R), sb(f"Wg{i}l", [P, D], F32R)) for i in (0, 1)]
        bg0 = sb("bg0", [P, D])
        bg1 = sb("bg1", [P, 1])
        WI = (sb("WIh", [P, MAX_SKIP, 4, D], F32R), sb("WIl", [P, MAX_SKIP, 4, D], F32R))
        WH = (sb("WHh", [P, MAX_SKIP - 1, 4, D], F32R), sb("WHl", [P, MAX_SKIP - 1, 4, D], F32R))
        bi = sb("bi", [P, MAX_SKIP, 4])
        bh = sb("bh", [P, MAX_SKIP, 4])
        gbias = sb("gbias", [P, MAX_SKIP, 4])
        ones = sb("rones", [P, P])
        rs = sh.rs
        diag = sb("diag", [P, C, P])
        RB0 = sb("RB0", [P, C, D])
        RB1 = sb("RB1", [P, N])
        Xh = sb("rXh", [P, C, QB, D], F32R)
        Xl = sb("rXl", [P, C, QB, D], F32R)
        ych = sb("ych", [P, 2, N], F32R)
        ycl = sb("ycl", [P, 2, N], F32R)
        u = sb("u", [P, 2, C, D])
        h1h = sb("h1h", [P, C, QB, D], F32R)
        h1l = sb("h1l", [P, C, QB, D], F32R)
        Hin = sb("Hin", [P, QB, N])
        Hq = sb("Hq", [P, QB, N])
        xh = sb("xh", [P, 2, N], F32R)
        xl = sb("xl", [P, 2, N], F32R)
        hh = sb("hh", [P, 2, N], F32R)
        hl = sb("hl", [P, 2, N], F32R)
        cell = sb("cell", [P, 2, N])
        gates = sb("gates", [P, 4, N])
        tc = sb("tc", [P, N])
        hn = sb("hn", [P, N])
        whh = sb("whh", [P, MAX_SKIP - 1, N])
        norm = sh.norm
        names = ("w_in", "g_in", "b_in", "ones_done", "set_mm", "set_free", "set_hi", "gbias_done", "wg_hi", "wg_done", "rb_done",
                 "xh_done", "xl_done", "ring_mm", "ring_free", "conv_hi", "relu_done", "h1l_done",
                 "hq_done", "xs_done", "x_hi", "hs_done", "c_own", "c_own2", "c_done", "tanh_done", "h_done",
                 "stat_done", "norm_own", "rstd_done", "x2_done")
        S = {n: sem("r_" + n) for n in names}
        gate_mm = [sem(f"gate_mm_{n}") for n in "ifgo"]
        gate_act = [sem(f"gate_act_{n}") for n in "ifgo"]

        steps = [(1, 0, u_) for u_ in range(QB)]
        for p_ in range(2, MAX_SKIP + 1):
            steps += [(p_, t, s) for t in range(p_) for s in (0, 1)]
        NS = len(steps)
        FILL = [1, 2, 3, 1, 2, 4, 1, 5, 3, 3, 1, 0, 1, 4, 3, 2, 0, 0, 0, 1, 1, 0]
        REST = 1
        NF = sum(t > 0 for _, t, _ in steps)

        def view(p_, t, s, source=None):
            if p_ == 1:
                return (Hq if source is None else source)[:, s, :], N
            nw = N // p_
            return Hq[:, 2 * s:2 * s + 2, t:t + (nw - 1) * p_ + 1:p_], 2 * nw

        def like(ap, p_, n):
            return ap[..., 0:n] if p_ == 1 else ap[..., 0:n].rearrange("p (b w) -> p b w", b=2)

        def gates_of(t):
            return (G, I, O) if t == 0 else (G, I, F, O)

        def uses(k, gate):
            return sum(gate in gates_of(t) for _, t, _ in steps[:k])

        def y(layer, b):
            return [(f"Y{layer}", b, c) for c in range(C)]

        def w(layer, b):
            return [(f"W{layer}", b, None)]

        def relu_then(b, pieces):
            return pieces[:2] + [("relu", b, None)] + pieces[2:] + [("low", b, None)]

        conv = y(0, 0) + y(0, 1) + w(0, 0) + relu_then(0, y(0, 2) + w(0, 1)) + relu_then(1, y(0, 3) + w(0, 2)) \
            + relu_then(2, y(1, 0) + w(0, 3)) + relu_then(3, y(1, 1) + w(1, 0)) + y(1, 2) + w(1, 1) + y(1, 3) \
            + w(1, 2) + w(1, 3)

        def is_tile(kind, c):
            return kind[0] in "YWR" and c in (None, C - 1)

        def has_cost(item):
            return item[0][0] in "YW"

        def tiles_in(items):
            return sum(is_tile(kind, c) for kind, _, c in items)

        split_at = [i for i, item in enumerate(conv) if has_cost(item)][-REST]
        body, rest = conv[:split_at], conv[split_at:]
        CONV, BODY, RESID = tiles_in(conv), tiles_in(body), QB
        tile_order = [(kind, b) for kind, b, c in conv if is_tile(kind, c)]
        y_order = [(kind, b) for kind, b in tile_order if kind[0] == "Y"]

        def schedule(g, with_next, with_last):
            fill = [(*item, g) for item in rest] + ([(*item, g + 1) for item in body] if with_next else [])
            at = 0
            for k in range(NS):
                if with_last and k in (0, 1):
                    yield from [("R", b, None, g - 1) for b in ((0, 1) if k == 0 else (2, 3))]
                if with_last and k in (3, 6):
                    yield ("stats" if k == 3 else "norm", 0, None, g - 1)
                now = []
                pieces = 0
                while at < (len(fill) if k else len(rest)) and (pieces < FILL[k] or k == NS - 1 or not has_cost(fill[at])):
                    pieces += has_cost(fill[at])
                    now.append(fill[at])
                    at += 1
                yield ("X", k, None, g)
                if steps[k][1] > 0:
                    yield from now
                yield ("L", k, None, g)
                if steps[k][1] == 0:
                    yield from now

        set_tiles = [("A", j) for j in range(C)] + [("rs", 0)] + [("WI", k) for k in range(MAX_SKIP)] \
            + [("WH", k) for k in range(MAX_SKIP - 1)]
        EARLY = C + 1

        def alone():
            later = iter(range(EARLY, len(set_tiles)))
            for i, item in enumerate(body):
                yield (*item, 0)
                if item[0] in ("W0", "W1"):
                    yield ("set", next(later), None, 0)

        def residual():
            return [("R", b, None, NQ - 1) for b in range(QB)]

        HS = sum(t < p_ - 1 for p_, t, _ in steps)

        def hs_before(k):
            return sum(t < p_ - 1 for p_, t, _ in steps[:k])

        def ring_base(g):
            if g is None:
                return 0
            if isinstance(g, int) and g in (0, NQ):
                return BODY if g == 0 else (CONV + RESID) * g - RESID
            return BODY - RESID + (CONV + RESID) * g

        def numbered(items, g):
            base = ring_base(g)
            n = base if isinstance(base, int) else BODY
            for kind, b, c, q in items:
                yield kind, b, c, q, base, 4 + n % 4
                if is_tile(kind, c):
                    n, base = n + 1, base + 1

        def y_tile(kind, b, g):
            return ring_base(g) - (BODY - tile_order.index(("Y" + kind[1], b)))

        block = ctx.enter_context(nc.Block())

        @block.sync
        def _(sp):
            for i in (0, 1):
                sp.dma_start(Wg[i][:, :], d[f"L1_gnn_Wg{i}"]).then_inc(S["g_in"], 16)
            sp.dma_start(bg0[:, :], d["L1_gnn_bg0"].rearrange("(o h) -> o h", o=1).broadcast_to([P, D]))\
                .then_inc(S["g_in"], 16)
            sp.dma_start(bg1[:, :], d["L1_gnn_bg1"].rearrange("(h o) -> h o", o=1)).then_inc(S["g_in"], 16)
            sp.dma_start(Hq[:, :, :].rearrange("p k (g h) -> p k g h", g=4),
                         d["L1_gnn_Wih"].rearrange("k (g p) h -> p k g h", p=P)).then_inc(S["w_in"], 16)
            sp.dma_start(whh[:, :, :].rearrange("p k (g h) -> p k g h", g=4),
                         d["L1_gnn_Whh"][1:MAX_SKIP].rearrange("k (g p) h -> p k g h", p=P))\
                .then_inc(S["w_in"], 16)
            sp.dma_start(bi[:, :, :], d["L1_gnn_bih"].rearrange("k (g p) -> p k g", p=P)).then_inc(S["b_in"], 16)
            sp.dma_start(bh[:, :, :], d["L1_gnn_bhh"].rearrange("k (g p) -> p k g", p=P)).then_inc(S["b_in"], 16)

        def set_target(kind, j, part):
            return {"A": AT[part], "WI": WI[part], "WH": WH[part]}[kind][:, j]

        def bank_like(n, kind):
            o = sh.psum[:, n % 4, :]
            return o if kind == "A" else o.rearrange("p (g h) -> p g h", g=4)

        @block.tensor
        def _(pe):
            def set_up(first, end):
                for n in range(first, end):
                    kind, j = set_tiles[n]
                    if n >= 4:
                        pe.wait_ge(S["set_free"], n - 3)
                    if kind == "rs":
                        pe.wait_ge(S["ones_done"], 1)
                        pe.matmul(sh.psum[:, n % 4, :], ones[:, :], diag[:, :, :], start=True, stop=True)\
                            .then_inc(S["set_mm"], 1)
                        continue
                    for c in range(C):
                        src = {"A": sh.A[:, c, j * P:(j + 1) * P], "WI": Hq[:, j, c * P:(c + 1) * P],
                               "WH": whh[:, min(j, MAX_SKIP - 2), c * P:(c + 1) * P]}[kind]
                        ins = pe.transpose(sh.psum[:, n % 4, c * P:(c + 1) * P], src, sh.ident[:, :])
                    ins.then_inc(S["set_mm"], 1)

            set_up(0, EARLY)
            pe.wait_ge(S["set_free"], EARLY)
            pe.wait_ge(S["wg_done"], 1)

            def ring_item(kind, b, c, q, n, bk, y_at):
                o = sh.psum[:, bk, :]
                if kind == "R":
                    pe.wait_ge(S["h_done"], NS * q + NS - 1 + b // 2)
                if c in (None, 0):
                    wait(pe, S["ring_free"], n - 3)
                if kind[0] == "Y":
                    if kind == "Y0" and b == 0:
                        pe.wait_ge(S["xl_done"], C * q + c + 1)
                    if kind == "Y1" and c == 0:
                        pe.wait_ge(S["h1l_done"], QB * q + b + 1)
                    hi, lo = (Xh, Xl) if kind == "Y0" else (h1h, h1l)
                    ins = product(pe, o, (hi[:, c, b, :], lo[:, c, b, :]), (ATh[:, c, :], ATl[:, c, :]),
                                  start=(c == 0), stop=(c == C - 1))
                elif kind[0] == "W":
                    pe.wait_ge(S["ring_free"], y_at + 1)
                    if kind == "W0":
                        for j in range(C):
                            cols = slice(j * P, (j + 1) * P)
                            ins = product(pe, o[:, cols], (ych[:, b % 2, cols], ycl[:, b % 2, cols]),
                                          (Wgs[0][0][:, :], Wgs[0][1][:, :]))
                    else:
                        ins = product(pe, o, (Wgs[1][0][:, :], Wgs[1][1][:, :]), (ych[:, b % 2, :], ycl[:, b % 2, :]))
                else:
                    for j in range(C):
                        ins = pe.transpose(o[:, j * P:(j + 1) * P], Hq[:, b, j * P:(j + 1) * P], sh.ident[:, :])
                if is_tile(kind, c):
                    ins.then_inc(S["ring_mm"], 1)

            def from_input(k, g):
                p_, t, s = steps[k]
                n = view(p_, t, s)[1]
                pe.wait_ge(S["xs_done"], NS * g + k + 1)
                for gate in gates_of(t):
                    per = NF if gate == F else NS
                    wait(pe, gate_act[gate], per * g + uses(k, gate))
                    ins = product(pe, sh.psum[:, gate, 0:n], (WI[0][:, p_ - 1, gate, :], WI[1][:, p_ - 1, gate, :]),
                                  (xh[:, s % 2, 0:n], xl[:, s % 2, 0:n]), stop=(t == 0))
                    if t == 0:
                        ins.then_inc(gate_mm[gate], 1)

            def from_state(k, g):
                p_, t, s = steps[k]
                if t == 0:
                    return
                n = view(p_, t, s)[1]
                pe.wait_ge(S["hs_done"], HS * g + hs_before(k - 2) + 1)
                for gate in gates_of(t):
                    product(pe, sh.psum[:, gate, 0:n], (WH[0][:, p_ - 2, gate, :], WH[1][:, p_ - 2, gate, :]),
                            (hh[:, s % 2, 0:n], hl[:, s % 2, 0:n]), start=False).then_inc(gate_mm[gate], 1)

            def run(items, g):
                y_at = {}
                for kind, b, c, q, n, bk in numbered(items, g):
                    if kind == "X":
                        from_input(b, g)
                    elif kind == "set":
                        if b == EARLY:
                            pe.wait_ge(S["w_in"], 32)
                        set_up(b, b + 1)
                    elif kind == "L":
                        from_state(b, g)
                    elif kind[0] in "YWR":
                        if kind[0] == "Y":
                            y_at[kind, b] = n
                        of = None if kind[0] != "W" else \
                            y_at["Y" + kind[1], b] if ("Y" + kind[1], b) in y_at else y_tile(kind, b, g)
                        ring_item(kind, b, c, q, n, bk, of)

            run(alone(), None)
            pe.wait_ge(S["set_free"], len(set_tiles))
            run(schedule(0, True, False), 0)
            with pe.Fori(1, NQ - 1) as g:
                run(schedule(g, True, True), g)
            run(schedule(NQ - 1, False, True), NQ - 1)
            run(residual(), NQ)

        @block.scalar
        def _(act):
            def set_up(first, end):
                for n in range(first, end):
                    kind, j = set_tiles[n]
                    if kind != "rs":
                        act.wait_ge(S["set_mm"], n + 1)
                        act.activation(set_target(kind, j, 0), bank_like(n, kind), ACT.Copy)\
                            .then_inc(S["set_hi"], 1)

            def split_x(q, c):
                act.activation(Xh[:, c, :, :], sh.X[:, c, bass.ds(QB * q, QB), :], ACT.Copy)\
                    .then_inc(S["xh_done"], 1)

            def just_made(k):
                return steps[k][0] == 1 and ("W1", k, None) in rest

            def split_h(k, g):
                p_, t, s = steps[k]
                hv, n = view(p_, t, s, Hin)
                if p_ == 1:
                    act.wait_ge(S["hq_done"], QB * g + s + 1)
                elif t == 0:
                    last = max(i for i in range(k) if steps[i][0] == p_ - 1
                               and (steps[i][2] == s if p_ > 2 else steps[i][2] // 2 == s))
                    act.wait_ge(S["h_done"], NS * g + last + 1)
                wait(act, gate_mm[O], NS * g + k - 1)
                act.activation(like(xh[:, s % 2, :], p_, n), hv, ACT.Copy).then_inc(S["x_hi"], 1)

            def lstm(k, g, with_next):
                p_, t, s = steps[k]
                n = view(p_, t, s)[1]
                late = k < NS - 1 and steps[k + 1][1] == 0 and steps[k + 1][0] > 1
                if k < NS - 1 and not late and not just_made(k + 1):
                    split_h(k + 1, g)
                elif k == NS - 1 and with_next:
                    split_h(0, g + 1)
                for gate in gates_of(t):
                    if late and gate == gates_of(t)[2]:
                        split_h(k + 1, g)
                    per = NF if gate == F else NS
                    act.wait_ge(gate_mm[gate], per * g + uses(k, gate) + 1)
                    wait(act, S["h_done" if gate == O else "c_done"], NS * g + k)
                    act.activation(gates[:, gate, 0:n], sh.psum[:, gate, 0:n],
                                   ACT.Tanh if gate == G else ACT.Sigmoid,
                                   bias=gbias[:, p_ - 1, gate:gate + 1]).then_inc(gate_act[gate], 1)
                act.wait_ge(S["c_done"], NS * g + k + 1)
                act.activation(tc[:, 0:n], cell[:, s % 2, 0:n], ACT.Tanh).then_inc(S["tanh_done"], 1)

            def run(items, g, with_next):
                u_at = {}
                for kind, b, c, q, n, bk in numbered(items, g):
                    if kind == "X" and just_made(b):
                        split_h(b, g)
                    elif kind == "set":
                        set_up(b, b + 1)
                    elif kind == "L":
                        lstm(b, g, with_next)
                        if with_next and b < 2:
                            split_x(g + 1, 2 * b)
                            split_x(g + 1, 2 * b + 1)
                    elif kind[0] == "Y" and is_tile(kind, c):
                        act.wait_ge(S["ring_mm"], n + 1)
                        act.activation(ych[:, b % 2, :], sh.psum[:, bk, :], ACT.Copy).then_inc(S["conv_hi"], 1)
                        if g is None and (kind, b) in y_order[QB - 1:2 * QB - 1]:
                            norm.finish(act, 0, S["x2_done"], [y_order.index((kind, b)) - QB + 1])
                    elif kind == "W1" and g is None and b == 1:
                        split_h(0, 0)
                    elif kind == "W0":
                        u_at[b] = n
                    elif kind == "relu":
                        act.wait_ge(S["ring_free"], u_at[b] + 1)
                        act.activation(h1h[:, :, b, :], u[:, b % 2, :, :], ACT.Relu).then_inc(S["relu_done"], 1)

            for c in range(C):
                split_x(0, c)
            act.wait_ge(S["g_in"], 64)
            for i in (0, 1):
                act.activation(Wgs[i][0][:, :], Wg[i][:, :], ACT.Copy).then_inc(S["wg_hi"], 1)
            set_up(0, EARLY)
            run(alone(), None, True)
            act.wait_ge(S["gbias_done"], 1)
            run(schedule(0, True, False), 0, True)
            with act.Fori(1, NQ - 1) as g:
                run(schedule(g, True, True), g, True)
            run(schedule(NQ - 1, False, True), NQ - 1, False)

        @block.vector
        def _(dve):
            dve.memset(ones[:, :], 1.0)
            for c in range(C):
                ins = dve.tensor_scalar(diag[:, c, :], sh.ident[:, :], rs[:, c:c + 1], None, ALU.mult)
            ins.then_inc(S["ones_done"], 1)
            dve.wait_ge(S["g_in"], 64)
            for c in range(C):
                ins = dve.tensor_scalar(RB0[:, c, :], bg0[:, :], rs[:, c:c + 1], None, ALU.mult)
            ins.then_inc(S["rb_done"], 1)
            for i in (0, 1):
                dve.wait_ge(S["wg_hi"], i + 1)
                ins = low_part(dve, Wgs[i][1][:, :], Wg[i][:, :], Wgs[i][0][:, :])
            ins.then_inc(S["wg_done"], 1)

            def set_up(first, end):
                for n in range(first, end):
                    kind, j = set_tiles[n]
                    if kind == "rs":
                        dve.wait_ge(S["set_mm"], n + 1)
                        dve.tensor_scalar(RB1[:, :], bank_like(n, "A"), bg1[:, 0:1], None, ALU.mult)\
                            .then_inc(S["set_free"], 1)
                    else:
                        dve.wait_ge(S["set_hi"], n + 1 - (n > C))
                        low_part(dve, set_target(kind, j, 1), bank_like(n, kind), set_target(kind, j, 0))\
                            .then_inc(S["set_free"], 1)

            set_up(0, EARLY)
            dve.wait_ge(S["rb_done"], 1)
            dve.wait_ge(S["set_free"], EARLY)

            def lstm(k, g):
                p_, t, s = steps[k]
                hv, n = view(p_, t, s)
                c_ = cell[:, s % 2, 0:n]

                def gate_is_there(gate):
                    per = NF if gate == F else NS
                    dve.wait_ge(gate_act[gate], per * g + uses(k, gate) + 1)

                gate_is_there(I)
                if t == 0:
                    dve.tensor_tensor(c_, gates[:, I, 0:n], gates[:, G, 0:n], ALU.mult).then_inc(S["c_done"], 1)
                else:
                    dve.tensor_tensor(gates[:, I, 0:n], gates[:, I, 0:n], gates[:, G, 0:n], ALU.mult)
                    gate_is_there(F)
                    dve.tensor_tensor(gates[:, F, 0:n], gates[:, F, 0:n], c_, ALU.mult).then_inc(S["c_own"], 1)
                    dve.wait_ge(S["c_own"], NF * g + uses(k, F) + 1)
                    dve.tensor_tensor(c_, gates[:, F, 0:n], gates[:, I, 0:n], ALU.add).then_inc(S["c_done"], 1)
                dve.wait_ge(S["tanh_done"], NS * g + k + 1)
                if t == p_ - 1:
                    dve.tensor_tensor(hv, like(gates[:, O, :], p_, n), like(tc, p_, n), ALU.mult)\
                        .then_inc(S["h_done"], 1)
                else:
                    dve.tensor_tensor(hn[:, 0:n], gates[:, O, 0:n], tc[:, 0:n], ALU.mult).then_inc(S["h_done"], 1)
                    dve.wait_ge(S["h_done"], NS * g + k + 1)
                    dve.tensor_copy(hh[:, s % 2, 0:n], hn[:, 0:n]).then_inc(S["c_own2"], 1)
                    dve.wait_ge(S["c_own2"], HS * g + hs_before(k) + 1)
                    low_part(dve, hl[:, s % 2, 0:n], hn[:, 0:n], hh[:, s % 2, 0:n]).then_inc(S["hs_done"], 1)

            def run(items, g):
                for kind, b, c, q, n, bk in numbered(items, g):
                    o = sh.psum[:, bk, :]
                    if kind == "L":
                        lstm(b, g)
                    elif kind == "set":
                        set_up(b, b + 1)
                    elif kind == "stats":
                        take_stats(q)
                    elif kind == "norm":
                        normalise(q)
                    elif kind[0] == "Y" and is_tile(kind, c):
                        dve.wait_ge(S["conv_hi"], 2 * QB * q + y_order.index((kind, b)) + 1)
                        low_part(dve, ycl[:, b % 2, :], o, ych[:, b % 2, :]).then_inc(S["ring_free"], 1)
                    elif kind == "W0":
                        dve.wait_ge(S["ring_mm"], n + 1)
                        wait(dve, S["h1l_done"], QB * q + b - 1)
                        dve.tensor_tensor(u[:, b % 2, :, :], o.rearrange("p (c d) -> p c d", c=C), RB0[:, :, :],
                                          ALU.add).then_inc(S["ring_free"], 1)
                    elif kind == "low":
                        dve.wait_ge(S["relu_done"], QB * q + b + 1)
                        dve.scalar_tensor_tensor(h1l[:, :, b, :], u[:, b % 2, :, :], 0.0,
                                                 h1h[:, :, b, :].bitcast(F32), ALU.max, ALU.subtract)\
                            .then_inc(S["h1l_done"], 1)
                    elif kind == "W1":
                        dve.wait_ge(S["ring_mm"], n + 1)
                        dve.tensor_tensor(Hin[:, b, :], o, RB1[:, :], ALU.add).then_inc(S["ring_free"], 1)
                        dve.wait_ge(S["ring_free"], n + 1)
                        dve.tensor_scalar(Hin[:, b, :], Hin[:, b, :], 0.0, None, ALU.max).then_inc(S["hq_done"], 1)
                    elif kind == "R":
                        dve.wait_ge(S["ring_mm"], n + 1)
                        xb = sh.X[:, :, bass.ds(QB * q + b, 1), :].rearrange("p c o d -> p c (o d)")
                        dve.tensor_tensor(xb, o.rearrange("p (c d) -> p c d", c=C), xb, ALU.add)\
                            .then_inc(S["ring_free"], 1)

            def take_stats(g):
                dve.wait_ge(S["ring_free"], ring_base(g + 1) + RESID)
                for b in range(QB):
                    ins = norm.take_stats(dve, QB * g + b)
                ins.then_inc(S["stat_done"], 1)

            def normalise(g):
                dve.wait_ge(S["rstd_done"], g + 1)
                for b in range(QB):
                    ins = norm.apply_on_dve(dve, QB * g + b, b)
                ins.then_inc(S["x2_done"], QB)

            run(alone(), None)
            dve.wait_ge(S["b_in"], 32)
            dve.tensor_tensor(gbias[:, :, :], bi[:, :, :], bh[:, :, :], ALU.add).then_inc(S["gbias_done"], 1)
            run(schedule(0, True, False), 0)
            with dve.Fori(1, NQ - 1) as g:
                run(schedule(g, True, True), g)
            run(schedule(NQ - 1, False, True), NQ - 1)
            run(residual(), NQ)

        @block.gpsimd
        def _(pool):
            def split_x(q, c):
                pool.wait_ge(S["xh_done"], C * q + c + 1)
                low_part(pool, Xl[:, c, :, :], sh.X[:, c, bass.ds(QB * q, QB), :], Xh[:, c, :, :])\
                    .then_inc(S["xl_done"], 1)

            def lstm(k, g):
                p_, t, s = steps[k]
                hv, n = view(p_, t, s, Hin)
                pool.wait_ge(S["x_hi"], NS * g + k + 1)
                low_part(pool, like(xl[:, s % 2, :], p_, n), hv, like(xh[:, s % 2, :], p_, n))\
                    .then_inc(S["xs_done"], 1)

            def make_scales(g):
                pool.wait_ge(S["stat_done"], g + 1)
                pool.wait_ge(S["x2_done"], QB * (g + 1))
                norm.scales(pool, g, S["norm_own"], SHIFT_LINKS * g).then_inc(S["rstd_done"], 1)

            def quad(g, with_next, with_last):
                for k in range(1, NS + 1):
                    if k < NS:
                        lstm(k, g)
                    elif with_next:
                        lstm(0, g + 1)
                    if with_next and k <= 2:
                        split_x(g + 1, 2 * k - 2)
                        split_x(g + 1, 2 * k - 1)
                    if with_last and k == 5:
                        make_scales(g - 1)

            for c in range(C):
                split_x(0, c)
            norm.finish_scales(pool, 0)
            lstm(0, 0)
            quad(0, True, False)
            with pool.Fori(1, NQ - 1) as g:
                quad(g, True, True)
            quad(NQ - 1, False, True)


def phase_batchnorm(nc, sh, d):
    C, D, N, NB = sh.C, sh.D, sh.N, sh.NB
    NP, NQ = NB // 2, NB // QB
    J = d["L2_gnn_W1"].shape[0] // P
    with ExitStack() as ctx:
        sb, sem = allocators(nc, ctx)
        H1 = sb("H1", [P, J, NB, N])
        O2 = sb("O2", [P, NB, N])
        AhT = (sb("AhTh", [P, C, N], F32R), sb("AhTl", [P, C, N], F32R))
        HI = sb("HI", [P, 4, N], F32R)
        LO = sb("LO", [P, 4, N], F32R)
        parts = tuple([t[:, k, :] for t in (early, late) for k in range(4)]
                      for early, late in ((HI, AhT[0]), (LO, AhT[1])))
        K = sh.NE // P
        iota = sb("biota", [P, N], I32)
        aw = O2[:, 0, 0:3 * P].rearrange("p (k h) -> p k h", k=3)
        wn = O2[:, 1, :].rearrange("p (k h) -> p k h", h=P)
        own = O2[:, 2, :].rearrange("p (k h) -> p k h", h=P)
        Gs = O2[:, 3:5, :].rearrange("p t (c e) -> p (t c) e", e=sh.NE)
        assert C >= QB >= 2 * J
        tmp = sh.A
        WT = (sb("WTh", [P, 4, P], F32R), sb("WTl", [P, 4, P], F32R))
        par1 = sb("par1", [P, 3, J])
        par2 = sb("par2", [P, 3, 1])
        st1 = sb("st1", [P, J, NB, 6])
        st2 = sb("st2", [P, 1, NB, 6])
        bmv = sb("bmv", [P, J + 1, 2])
        bsc = sb("bsc", [P, J + 1])
        bsh = sb("bsh", [P, J + 1])
        norm = sh.norm
        names = ("aw_in", "iota_done", "t_lo1", "w_in", "p_in", "set_mm", "set_free", "set_hi", "own", "rest_done", "ah_done",
                 "ah_hi", "ah_lo", "xh_done", "xl_done", "y_mm", "y_hi", "y_lo", "w_mm", "w_out", "st_done",
                 "bmv_done", "bve", "brstd", "bn_done", "u_done", "t_hi", "t_lo", "o_mm", "o_out", "ost_done",
                 "z_done", "z_mm", "z_add", "stat_done", "norm_own", "rstd_done", "x_done", "xd_done")
        S = {n: sem("b_" + n) for n in names}
        block = ctx.enter_context(nc.Block())

        def xb(b):
            return sh.X[:, :, bass.ds(b, 1), :].rearrange("p c o d -> p c (o d)")

        def by_chunk(ap):
            return ap.rearrange("p (c d) -> p c d", c=C)

        @block.sync
        def _(sp):
            sp.dma_start(wn[:, 0:J, :], d["L2_gnn_W1"].rearrange("(j p) d -> p j d", p=P)).then_inc(S["w_in"], 16)
            sp.dma_start(wn[:, J:2 * J, :], d["L2_gnn_W2"].rearrange("o (j h) -> o j h", j=J))\
                .then_inc(S["w_in"], 16)
            for k, name in enumerate(("W_lin", "W_val", "W_out")):
                sp.dma_start(aw[:, k, :], d[f"L3_gnn_{name}"]).then_inc(S["aw_in"], 16)
            for k, name in enumerate(("b", "g", "be")):
                sp.dma_start(par1[:, k, :], d[f"L2_gnn_{name}1"].rearrange("(j p) -> p j", p=P))\
                    .then_inc(S["p_in"], 16)
                sp.dma_start(par2[:, k, :], d[f"L2_gnn_{name}2"].rearrange("(p o) -> p o", o=1))\
                    .then_inc(S["p_in"], 16)

        @block.tensor
        def _(pe):
            for j in range(C):
                for c in range(C):
                    ins = pe.transpose(sh.psum[:, 4 + j, c * P:(c + 1) * P], sh.A[:, c, j * P:(j + 1) * P],
                                       sh.ident[:, :])
                ins.then_inc(S["set_mm"], 1)
            pe.wait_ge(S["w_in"], 32)
            for k in range(2 * J):
                ins = pe.transpose(sh.psum[:, 3, k * P:(k + 1) * P], wn[:, k, :], sh.ident[:, :])
            ins.then_inc(S["set_mm"], 1)
            pe.wait_ge(S["aw_in"], 48)
            for k in range(3):
                ins = pe.transpose(sh.psum[:, 2, k * P:(k + 1) * P], aw[:, k, :], sh.ident[:, :])
            ins.then_inc(S["set_mm"], 1)

            def first(i, last):
                for s in (0, 1):
                    pe.wait_ge(S["xl_done"], 2 * i + s + 1)
                    for c in range(C):
                        cols = slice(c * D, (c + 1) * D)
                        if isinstance(i, int) and 2 * i + s == 0:
                            pe.wait_ge(S["ah_lo"], c + 1)
                        ins = product(pe, sh.psum[:, s, :], (HI[:, s, cols], LO[:, s, cols]),
                                      (AhT[0][:, c, :], AhT[1][:, c, :]), start=(c == 0), stop=(c == C - 1))
                    ins.then_inc(S["y_mm"], 1)
                if isinstance(i, int) and i == 0:
                    pe.wait_ge(S["set_free"], 2)
                wait(pe, S["w_out"], 4 * i)
                for s in (0, 1):
                    pe.wait_ge(S["y_lo"], 2 * i + s + 1)
                    for j in range(J):
                        product(pe, sh.psum[:, 2 + 2 * s + j, :], (WT[0][:, j, :], WT[1][:, j, :]),
                                (HI[:, 2 + s, :], LO[:, 2 + s, :])).then_inc(S["w_mm"], 1)

            def second(i, last):
                for b in range(QB):
                    n = QB * i + b
                    pe.wait_ge(S["t_lo"], n + 1)
                    pe.wait_ge(S["t_lo1"], n + 1)
                    wait(pe, S["o_out"], n - QB + 1)
                    for j in range(J):
                        ins = product(pe, sh.psum[:, 4 + b, :], (WT[0][:, J + j, :], WT[1][:, J + j, :]),
                                      (parts[0][J * b + j], parts[1][J * b + j]), start=(j == 0),
                                      stop=(j == J - 1))
                    ins.then_inc(S["o_mm"], 1)

            def third(i, last):
                for b in range(QB):
                    n = QB * i + b
                    pe.wait_ge(S["z_done"], n + 1)
                    wait(pe, S["z_add"], n - QB + 1)
                    for c in range(C):
                        cols = slice(c * P, (c + 1) * P)
                        ins = pe.transpose(sh.psum[:, b, cols], tmp[:, b, cols], sh.ident[:, :])
                    ins.then_inc(S["z_mm"], 1)

            peeled(pe, NP, first)
            peeled(pe, NQ, second)
            peeled(pe, NQ, third)

        @block.scalar
        def _(act):
            for s in (0, 1):
                act.activation(by_chunk(HI[:, s, :]), xb(s), ACT.Copy).then_inc(S["xh_done"], 1)
            for j in range(C):
                act.wait_ge(S["ah_done"], j + 1)
                act.activation(AhT[0][:, j, :], tmp[:, j, :], ACT.Copy).then_inc(S["ah_hi"], 1)
            act.wait_ge(S["set_mm"], C + 1)
            act.activation(WT[0][:, :, :], sh.psum[:, 3, :].rearrange("p (k h) -> p k h", h=P), ACT.Copy)\
                .then_inc(S["set_hi"], 1)
            act.wait_ge(S["set_mm"], C + 2)
            act.activation(sh.aWT[0][:, :, :], sh.psum[:, 2, 0:3 * P].rearrange("p (k h) -> p k h", h=P), ACT.Copy)\
                .then_inc(S["set_hi"], 1)

            def split_x(b, s):
                act.activation(by_chunk(HI[:, s, :]), xb(b), ACT.Copy).then_inc(S["xh_done"], 1)

            def first(i, last):
                for s in (0, 1):
                    act.wait_ge(S["y_mm"], 2 * i + s + 1)
                    act.activation(HI[:, 2 + s, :], sh.psum[:, s, :], ACT.Copy).then_inc(S["y_hi"], 1)
                    if not last:
                        split_x(2 * i + 2 + s, s)
                if isinstance(i, int) and i == 0:
                    norm.finish(act, 1, S["x_done"], range(2))
                for s in (0, 1):
                    for j in range(J):
                        act.wait_ge(S["w_mm"], 4 * i + 2 * s + j + 1)
                        act.activation(H1[:, j, bass.ds(2 * i + s, 1), :], sh.psum[:, 2 + 2 * s + j, :],
                                       ACT.Identity, bias=par1[:, 0, j:j + 1]).then_inc(S["w_out"], 1)
                if isinstance(i, int) and i == 0:
                    norm.finish(act, 1, S["x_done"], range(2, QB))

            def second_out(n, b):
                act.wait_ge(S["o_mm"], n + 1)
                act.activation(O2[:, bass.ds(n, 1), :], sh.psum[:, 4 + b, :], ACT.Identity,
                               bias=par2[:, 0, 0:1]).then_inc(S["o_out"], 1)

            def second(i, last):
                for b in range(QB):
                    n = QB * i + b
                    wait(act, S["t_lo"], n - 1)
                    wait(act, S["t_lo1"], n - 1)
                    for j in range(J):
                        act.activation(tmp[:, J * (b % 2) + j, :], H1[:, j, bass.ds(n, 1), :], ACT.Relu,
                                       bias=bsh[:, j:j + 1], scale=bsc[:, j:j + 1]).then_inc(S["u_done"], 1)
                    if not isinstance(i, int) or n >= 2:
                        second_out(n - 2, (b - 2) % QB)

            def z(n, b):
                wait(act, S["z_mm"], n - QB + 1)
                act.activation(tmp[:, b, :], O2[:, bass.ds(n, 1), :], ACT.Identity,
                               bias=bsh[:, J:J + 1], scale=bsc[:, J:J + 1]).then_inc(S["z_done"], 1)

            def third(i, last):
                for b in range(QB):
                    if not last:
                        z(QB * (i + 1) + b, b)
                    if not isinstance(i, int) or i > 0:
                        if b == 0:
                            act.wait_ge(S["rstd_done"], i)
                        norm.apply(act, QB * (i - 1) + b, b, range(C - 1)).then_inc(S["x_done"], 1)

            act.wait_ge(S["p_in"], 96)
            peeled(act, NP, first)
            act.wait_ge(S["bn_done"], 1)
            peeled(act, NQ, second)
            for n in (NB - 2, NB - 1):
                second_out(n, n % QB)
            act.wait_ge(S["bn_done"], 2)
            for b in range(QB):
                z(b, b)
            peeled(act, NQ, third)

        @block.vector
        def _(dve):
            chain = [0]

            def link(ins):
                chain[0] += 1
                ins.then_inc(S["own"], 1)
                dve.wait_ge(S["own"], chain[0])

            for j in range(C):
                ins = dve.scalar_tensor_tensor(own[:, j, :], sh.ident[:, :], sh.dinv[:, j:j + 1],
                                               sh.drow[:, j * P:(j + 1) * P], ALU.mult, ALU.mult)
            for j in range(C):
                dve.wait_ge(S["set_mm"], C)
                link(dve.scalar_tensor_tensor(tmp[:, j, :], sh.psum[:, 4 + j, :], sh.dinv[:, j:j + 1],
                                              sh.drow[:, :], ALU.mult, ALU.mult))
                diagonal = tmp[:, j, j * P:(j + 1) * P]
                dve.tensor_tensor(diagonal, diagonal, own[:, j, :], ALU.add).then_inc(S["ah_done"], 1)
                if j > 0:
                    dve.wait_ge(S["ah_hi"], j)
                    low_part(dve, AhT[1][:, j - 1, :], tmp[:, j - 1, :], AhT[0][:, j - 1, :]).then_inc(S["ah_lo"], 1)
            dve.wait_ge(S["ah_hi"], C)
            low_part(dve, AhT[1][:, C - 1, :], tmp[:, C - 1, :], AhT[0][:, C - 1, :]).then_inc(S["ah_lo"], 1)
            dve.wait_ge(S["set_hi"], 1)
            low_part(dve, WT[1][:, :, :], sh.psum[:, 3, :].rearrange("p (k h) -> p k h", h=P), WT[0][:, :, :])\
                .then_inc(S["set_free"], 1)
            dve.wait_ge(S["set_hi"], 2)
            low_part(dve, sh.aWT[1][:, :, :], sh.psum[:, 2, 0:3 * P].rearrange("p (k h) -> p k h", h=P),
                     sh.aWT[0][:, :, :]).then_inc(S["set_free"], 1)
            for n in range(NB - QB, NB):
                ins = norm.take_stats(dve, n)
            ins.then_inc(S["rest_done"], 1)
            for c in range(C):
                dve.tensor_scalar(Gs[:, c, :], sh.ss[:, 0, :], sh.ioc[:, c:c + 1], None, ALU.is_equal)
                ins = dve.tensor_scalar(sh.GZ[:, c, 1, :], sh.ss[:, 1, :], sh.ioc[:, c:c + 1], None, ALU.is_equal)
            link(ins)
            dve.tensor_tensor(sh.GZ[:, :, 0, :], Gs[:, :, :], sh.GZ[:, :, 1, :].bitcast(F32), ALU.add)
            dve.wait_ge(S["iota_done"], 1)
            for k in range(K):
                dve.tensor_scalar(sh.GsT[:, k, :], iota[:, :], sh.sc[:, k:k + 1], None, ALU.is_equal)

            def first(i, last):
                for s in (0, 1):
                    dve.wait_ge(S["y_hi"], 2 * i + s + 1)
                    low_part(dve, LO[:, 2 + s, :], sh.psum[:, s, :], HI[:, 2 + s, :]).then_inc(S["y_lo"], 1)
                for s in (0, 1):
                    for j in range(J):
                        dve.wait_ge(S["w_out"], 4 * i + 2 * s + j + 1)
                        dve.bn_stats(st1[:, j, bass.ds(2 * i + s, 1), :], H1[:, j, bass.ds(2 * i + s, 1), :])\
                            .then_inc(S["st_done"], 1)

            def batch_norm(js, k):
                st, par = (st1, par1) if k == 0 else (st2, par2)
                for j in js:
                    ins = dve.bn_aggr(bmv[:, j, :], st[:, j - js[0], :, :].rearrange("p b s -> p (b s)"))
                ins.then_inc(S["bmv_done"], 1)
                dve.wait_ge(S["brstd"], k + 1)
                cols = slice(js[0], js[-1] + 1)
                link(dve.tensor_tensor(bsc[:, cols], bsc[:, cols], par[:, 1, :], ALU.mult))
                link(dve.tensor_tensor(bsh[:, cols], bmv[:, cols, 0], bsc[:, cols], ALU.mult))
                dve.tensor_tensor(bsh[:, cols], par[:, 2, :], bsh[:, cols], ALU.subtract)\
                    .then_inc(S["bn_done"], 1)
                dve.wait_ge(S["bn_done"], k + 1)

            def second_stats(n):
                dve.wait_ge(S["o_out"], n + 1)
                dve.bn_stats(st2[:, 0, bass.ds(n, 1), :], O2[:, bass.ds(n, 1), :]).then_inc(S["ost_done"], 1)

            def second(i, last):
                for b in range(QB):
                    n = QB * i + b
                    wait(dve, S["o_mm"], n - QB + 1)
                    for j in range(J):
                        dve.wait_ge(S["u_done"], J * n + j + 1)
                        dve.tensor_copy(parts[0][J * b + j], tmp[:, J * (b % 2) + j, :]).then_inc(S["t_hi"], 1)
                    dve.wait_ge(S["t_hi"], J * n + 1)
                    low_part(dve, parts[1][J * b], tmp[:, J * (b % 2), :], parts[0][J * b]).then_inc(S["t_lo"], 1)
                    if not isinstance(i, int) or n >= 3:
                        second_stats(n - 3)

            def third_stats(n):
                dve.wait_ge(S["z_add"], n + 1)
                norm.take_stats(dve, n).then_inc(S["stat_done"], 1)

            def third(i, last):
                for b in range(QB):
                    n = QB * i + b
                    dve.wait_ge(S["z_mm"], n + 1)
                    dve.tensor_tensor(xb(n), by_chunk(sh.psum[:, b, :]), xb(n), ALU.add).then_inc(S["z_add"], 1)
                    if not isinstance(i, int) or n >= 1:
                        third_stats(n - 1)
                if not isinstance(i, int) or i > 0:
                    dve.wait_ge(S["rstd_done"], i)
                    for b in range(QB):
                        ins = norm.apply_on_dve(dve, QB * (i - 1) + b, b, range(C - 1, C))
                    ins.then_inc(S["xd_done"], 1)

            peeled(dve, NP, first)
            dve.wait_ge(S["st_done"], 2 * J * NP)
            batch_norm(list(range(J)), 0)
            peeled(dve, NQ, second)
            for n in range(NB - 3, NB):
                second_stats(n)
            dve.wait_ge(S["ost_done"], NB)
            batch_norm([J], 1)
            peeled(dve, NQ, third)
            third_stats(NB - 1)

        @block.gpsimd
        def _(pool):
            pool.iota(iota[:, :], pattern=[[1, N]], base=0, channel_multiplier=0).then_inc(S["iota_done"], 1)
            def split_x(b, s, n):
                pool.wait_ge(S["xh_done"], n)
                low_part(pool, by_chunk(LO[:, s, :]), xb(b), by_chunk(HI[:, s, :])).then_inc(S["xl_done"], 1)

            for n in range(2):
                split_x(n, n % 2, n + 1)
            pool.wait_ge(S["rest_done"], 1)
            norm.finish_scales(pool, 1)
            pool.wait_ge(norm.ready, 2)
            with pool.Fori(0, NP - 1) as i:
                for s in (0, 1):
                    split_x(2 * i + 2 + s, s, 2 * i + s + 3)

            def batch_norm(cols, k):
                pool.wait_ge(S["bmv_done"], k + 1)
                n = cols.stop - cols.start
                pool.tensor_tensor(bsc[:, cols], bmv[:, cols, 1], sh.const[:, sh.EPS, 0:n], ALU.add).then_inc(S["bve"], 1)
                pool.wait_ge(S["bve"], k + 1)
                pool.tensor_tensor(bsc[:, cols], bsc[:, cols], sh.const[:, sh.ROOT, 0:n], ALU.pow).then_inc(S["brstd"], 1)

            batch_norm(slice(0, J), 0)

            def second(i, last):
                for b in range(QB):
                    n = QB * i + b
                    for j in range(1, J):
                        pool.wait_ge(S["t_hi"], J * n + j + 1)
                        ins = low_part(pool, parts[1][J * b + j], tmp[:, J * (b % 2) + j, :], parts[0][J * b + j])
                    ins.then_inc(S["t_lo1"], 1)

            peeled(pool, NQ, second)
            batch_norm(slice(J, J + 1), 1)

            def quad_norm(g, last):
                def free():
                    pool.wait_ge(S["x_done"], QB * (g + 1))
                    wait(pool, S["xd_done"], g)

                pool.wait_ge(S["stat_done"], QB * (g + 1))
                wait(pool, S["rstd_done"], g)
                norm.scales(pool, g, S["norm_own"], SHIFT_LINKS * g, free).then_inc(S["rstd_done"], 1)

            peeled(pool, NQ - 1, quad_norm)


def phase_attention(nc, sh, d, out):
    C, D, N, NB = sh.C, sh.D, sh.N, sh.NB
    NE = d["L3_gnn_src"].shape[0]
    K = NE // P
    NH, DH = d["L3_gnn_a"].shape
    NQ, NP = NB // QB, NB // 2
    R = QB * NH
    with ExitStack() as ctx:
        sb, sem = allocators(nc, ctx)
        ss, lg = sh.ss, sh.lg
        GZ, GsT, WT = sh.GZ, sh.GsT, sh.aWT
        ne = sb("ne", [R, NE])
        pf = sb("pf", [R, QB, NE])
        pr = sb("pr", [R, QB, NE])
        kf = sb("kf", [R, QB, NE])
        acol = sb("acol", [P, 1])
        wide = sb("wide", [P, 2 * R - NH])
        XH = sb("aXH", [P, 2, N], F32R)
        XL = sb("aXL", [P, 2, N], F32R)
        ZH = sb("ZH", [P, QB, N], F32R)
        ZL = sb("ZL", [P, QB, N], F32R)
        uq = sb("uq", [P, 2, NE])
        lr = sb("lr", [P, 2, NE])
        V = sb("aV", [P, NB, K, D])
        sco = sb("sco", [R, QB, NE])
        s1 = sb("s1", [R, QB, NE])
        s2 = sb("s2", [R, QB, NE])
        inverse = sb("inverse", [P, NQ * K * R])
        aT = sb("aT", [P, K, NB, NH])
        va = sb("va", [P, QB, K, D])
        vah = sb("vah", [P, QB, K, D], F32R)
        val = sb("val", [P, QB, K, D], F32R)
        last_mean = sb("last_mean", [P, QB * C])
        last_norm = (sb("last_scale", [P, QB * C]), sb("last_shift", [P, QB * C]))
        norm = sh.norm
        names = ("w_in", "own", "wide0", "wide_done", "xh_done", "xl_done", "z_mm", "z_hi", "z_lo", "uv_mm", "uv_out",
                 "lr_done", "sc_mm", "sc_done", "sd_done", "ex_done", "soft", "at_mm", "at_done", "va_done",
                 "va_hi", "va_lo", "y_mm", "y_hi", "y_lo", "o_mm", "o_add", "stat_done", "norm_own",
                 "rstd_done", "x_done", "xd_done", "stored")
        S = {n: sem("a_" + n) for n in names}
        QUADS = (slice(0, NQ - 1), slice(NQ - 1, NQ))
        block = ctx.enter_context(nc.Block())

        def xb(b):
            return sh.X[:, :, bass.ds(b, 1), :].rearrange("p c o d -> p c (o d)")

        def by_chunk(ap):
            return ap.rearrange("p (c d) -> p c d", c=C)

        @block.sync
        def _(sp):
            sp.dma_start(acol[:, :], d["L3_gnn_a"].rearrange("h (e o) -> (h e) o", o=1)).then_inc(S["w_in"], 16)
            ov = out.rearrange("b (c p) d -> p c b d", p=P)

            def store(i):
                for c in range(C):
                    sp.dma_start(ov[:, c, bass.ds(2 * i, 2), :], sh.X[:, c, bass.ds(2 * i, 2), :])\
                        .then_inc(S["stored"], 16)

            with sp.Fori(0, NP - 2) as i:
                sp.wait_ge(S["x_done"], QB + 2 * (i + 1))
                store(i)
            sp.wait_ge(S["xd_done"], 2)
            store(NP - 2)
            sp.wait_ge(S["x_done"], QB + NB - 3)
            sp.wait_ge(S["xd_done"], 3)
            store(NP - 1)
            sp.wait_ge(S["stored"], 16 * C * NP)

        @block.gpsimd
        def _(pool):
            pool.memset(wide[:, :], 0.0).then_inc(S["wide0"], 1)

            def split_x(b, s, n):
                pool.wait_ge(S["xh_done"], n)
                low_part(pool, by_chunk(XL[:, s, :]), xb(b), by_chunk(XH[:, s, :])).then_inc(S["xl_done"], 1)

            for n in range(2):
                split_x(n, n % 2, n + 1)
            norm.finish_scales(pool, 2)
            pool.wait_ge(norm.ready, 3)
            with pool.Fori(0, NP - 1) as i:
                for s in (0, 1):
                    split_x(2 * i + 2 + s, s, 2 * i + s + 3)

            def quad_norm(g):
                pool.wait_ge(S["stat_done"], QB * (g + 1))
                wait(pool, S["rstd_done"], g)
                norm.scales(pool, g, S["norm_own"], SHIFT_LINKS * g,
                            free=lambda: pool.wait_ge(S["x_done"], QB * (g + 1))).then_inc(S["rstd_done"], 1)

            def attend(i, last):
                for b in range(QB):
                    n = QB * i + b
                    wait(pool, S["va_lo"], n - QB + 1)
                    for k in range(K):
                        ins = pool.tensor_tensor(
                            va[:, b, k, :].rearrange("p (h e) -> p h e", h=NH),
                            V[:, bass.ds(n, 1), k, :].rearrange("p o (h e) -> p (o h) e", h=NH),
                            aT[:, k, bass.ds(n, 1), :].rearrange("p o h -> p (o h)").unsqueeze(2)
                            .broadcast_to([P, NH, DH]), ALU.mult)
                    ins.then_inc(S["va_done"], 1)
                    if b == 1 and (not isinstance(i, int) or i > 1):
                        quad_norm(i - 2)

            pool.wait_ge(S["at_done"], 1)
            peeled_two(pool, NQ, attend)
            quad_norm(NQ - 2)
            for h in (0, 1):
                pool.wait_ge(S["stat_done"], NB - QB + 2 * (h + 1))
                pool.wait_ge(S["rstd_done"], NQ - 1 + h)
                rows = slice(2 * h * C, 2 * (h + 1) * C)
                norm_scales(pool, sh, 2 * C, norm.stats[:, (NB - QB) * C + rows.start:(NB - QB) * C + rows.stop, :],
                            norm.work, last_mean[:, rows], last_norm[0][:, rows], S["norm_own"],
                            SHIFT_LINKS * (NQ - 1 + h), last_norm[1][:, rows]).then_inc(S["rstd_done"], 1)

        @block.scalar
        def _(act):
            for s in (0, 1):
                act.activation(by_chunk(XH[:, s, :]), xb(s), ACT.Copy).then_inc(S["xh_done"], 1)

            def split_x(b, s):
                act.activation(by_chunk(XH[:, s, :]), xb(b), ACT.Copy).then_inc(S["xh_done"], 1)

            def gather(g, h, last):
                for s in (0, 1):
                    n = QB * g + 2 * h + s
                    act.wait_ge(S["z_mm"], n + 1)
                    act.activation(ZH[:, s, :], sh.psum[:, s, :], ACT.Copy).then_inc(S["z_hi"], 1)
                    if not last:
                        split_x(n + 2, s)
                for s in (0, 1):
                    n = QB * g + 2 * h + s
                    act.wait_ge(S["uv_mm"], n + 1)
                    wait(act, S["lr_done"], QB * g + 2 * h)
                    act.activation(uq[:, s, :], sh.psum[:, 2 + s, 0:NE], ACT.Copy).then_inc(S["uv_out"], 1)
                    act.activation(V[:, bass.ds(n, 1), :, :],
                                   sh.psum[:, 2 + s, NE:2 * NE].rearrange("p (k d) -> p k d", k=K), ACT.Copy)\
                        .then_inc(S["uv_out"], 1)

            def exponentials(part):
                act.wait_ge(S["sd_done"], part + 1)
                act.activation(s2[:, QUADS[part], :], s1[:, QUADS[part], :], ACT.Exp).then_inc(S["ex_done"], 1)

            def gather_quad(g, last):
                gather(g, 0, False)
                if isinstance(g, int) and g == 0:
                    norm.finish(act, 2, S["x_done"], range(2))
                if last:
                    exponentials(0)
                gather(g, 1, last)
                if isinstance(g, int) and g == 0:
                    norm.finish(act, 2, S["x_done"], range(2, 4))

            peeled(act, NQ, gather_quad)
            exponentials(1)

            def scattered_high(n, b):
                act.wait_ge(S["y_mm"], n + 1)
                act.activation(ZH[:, b, :], sh.psum[:, b, :], ACT.Copy).then_inc(S["y_hi"], 1)

            def attend(i, last):
                for b in range(QB):
                    n = QB * i + b
                    act.wait_ge(S["va_done"], n + 1)
                    wait(act, S["y_mm"], n - QB + 1)
                    act.activation(vah[:, b, :, :], va[:, b, :, :], ACT.Copy).then_inc(S["va_hi"], 1)
                    if not isinstance(i, int) or n >= 1:
                        scattered_high(n - 1, (b - 1) % QB)
                    if b > 0 and (not isinstance(i, int) or i > 1):
                        if b == 1:
                            act.wait_ge(S["rstd_done"], i - 1)
                        for m in (b - 1,) if b < QB - 1 else (b - 1, b):
                            norm.apply(act, QB * (i - 2) + m, m).then_inc(S["x_done"], 1)

            peeled_two(act, NQ, attend)
            scattered_high(NB - 1, QB - 1)
            act.wait_ge(S["rstd_done"], NQ - 1)
            for b in range(QB):
                norm.apply(act, NB - 2 * QB + b, b).then_inc(S["x_done"], 1)
            act.wait_ge(S["rstd_done"], NQ + 1)
            norm.apply(act, NB - 2, QB - 2, other=last_norm).then_inc(S["x_done"], 1)

        @block.vector
        def _(dve):
            chain = [0]

            def link(ins):
                chain[0] += 1
                ins.then_inc(S["own"], 1)
                dve.wait_ge(S["own"], chain[0])

            dve.wait_ge(S["wide0"], 1)
            dve.wait_ge(S["w_in"], 16)
            for h in range(NH):
                rows = slice(h * DH, (h + 1) * DH)
                ins = dve.tensor_copy(wide[rows, R - NH + h:R - NH + h + 1], acol[rows, 0:1])
            ins.then_inc(S["wide_done"], 1)
            link(dve.tensor_tensor(ne[:, 1:NE], ss[0:R, 0, 1:NE], ss[0:R, 0, 0:NE - 1], ALU.not_equal))
            for q in range(QB):
                dve.tensor_scalar(pf[:, q, 1:NE], ne[:, 1:NE], LOWEST, None, ALU.mult)
                dve.tensor_scalar(kf[:, q, 1:NE], ne[:, 1:NE], -1.0, 1.0, ALU.mult, ALU.add)
                dve.tensor_scalar(pr[:, q, 0:NE - 1], ne[:, 1:NE], LOWEST, None, ALU.mult)
            dve.memset(pf[:, :, 0:1], LOWEST)
            dve.memset(kf[:, :, 0:1], 0.0)
            dve.memset(pr[:, :, NE - 1:NE], LOWEST)

            soft = [0]

            def then(ins):
                soft[0] += 1
                ins.then_inc(S["soft"], 1)
                dve.wait_ge(S["soft"], soft[0])

            def softmax_steps(part):
                quads = QUADS[part]

                def flat(t):
                    return t[:, quads, :].rearrange("p q e -> p (q e)")

                def maximum():
                    dve.wait_ge(S["sc_done"], quads.stop)
                    then(dve.tensor_tensor_scan(flat(s1), flat(pf), flat(sco), LOWEST, ALU.add, ALU.max))

                def spread_maximum():
                    then(dve.tensor_tensor_scan(flat(s2)[:, ::-1], flat(pr)[:, ::-1], flat(s1)[:, ::-1], LOWEST,
                                                ALU.add, ALU.max))

                def differences():
                    dve.tensor_tensor(flat(s1), flat(sco), flat(s2), ALU.subtract).then_inc(S["sd_done"], 1)

                def sums():
                    dve.wait_ge(S["ex_done"], part + 1)
                    then(dve.tensor_tensor_scan(flat(s1), flat(kf), flat(s2), 0.0, ALU.mult, ALU.add))

                def spread_sums():
                    then(dve.tensor_tensor_scan(flat(sco)[:, ::-1], flat(pr)[:, ::-1], flat(s1)[:, ::-1], 0.0,
                                                ALU.add, ALU.max))

                return maximum, spread_maximum, differences, sums, spread_sums

            early = softmax_steps(0)

            def gather(g, h, last):
                for s in (0, 1):
                    n = QB * g + 2 * h + s
                    dve.wait_ge(S["z_hi"], n + 1)
                    low_part(dve, ZL[:, s, :], sh.psum[:, s, :], ZH[:, s, :]).then_inc(S["z_lo"], 1)
                if last:
                    for step in early[0:2] if h == 0 else early[3:4]:
                        step()
                for s in (0, 1):
                    n = QB * g + 2 * h + s
                    dve.wait_ge(S["uv_out"], 2 * n + 1)
                    dve.scalar_tensor_tensor(lr[:, s, :], uq[:, s, :], 0.2, uq[:, s, :], ALU.mult, ALU.max)\
                        .then_inc(S["lr_done"], 1)
                if last:
                    early[2 if h == 0 else 4]()

            def scores(g):
                dve.wait_ge(S["sc_mm"], QB * g + QB)
                dve.tensor_tensor(sco[:, bass.ds(g, 1), :].rearrange("p o e -> p (o e)"), sh.psum[0:R, 4, 0:NE],
                                  lg[:, :], ALU.add).then_inc(S["sc_done"], 1)

            def gather_quad(g, last):
                for h in (0, 1):
                    wait(dve, S["sc_mm"], QB * g + 2 * h)
                    gather(g, h, last)
                scores(g)

            peeled(dve, NQ, gather_quad)
            for step in softmax_steps(1):
                step()
            dve.wait_ge(S["at_mm"], 1)
            sums = sh.psum[:, 6, 0:NQ * K * R]
            then(dve.reciprocal(inverse[:, :], sums))
            dve.tensor_tensor(aT[:, :, :, :].rearrange("p k (q b) h -> p k q (b h)", q=NQ),
                              sh.psum[:, 5, 0:NQ * K * R].rearrange("p (k q r) -> p k q r", k=K, q=NQ),
                              inverse[:, :].rearrange("p (k q r) -> p k q r", k=K, q=NQ), ALU.mult)\
                .then_inc(S["at_done"], 1)

            def weighted_low(n, b):
                dve.wait_ge(S["va_hi"], n + 1)
                low_part(dve, val[:, b, :, :], va[:, b, :, :], vah[:, b, :, :]).then_inc(S["va_lo"], 1)

            def scattered_low(n, b):
                dve.wait_ge(S["y_hi"], n + 1)
                low_part(dve, ZL[:, b, :], sh.psum[:, b, :], ZH[:, b, :]).then_inc(S["y_lo"], 1)

            def residual(n, b):
                dve.wait_ge(S["o_mm"], n + 1)
                dve.tensor_tensor(xb(n), by_chunk(sh.psum[:, 4 + b, :]), xb(n), ALU.add).then_inc(S["o_add"], 1)

            def out_stats(n):
                dve.wait_ge(S["o_add"], n + 1)
                norm.take_stats(dve, n).then_inc(S["stat_done"], 1)

            def attend(i, last):
                for b in range(QB):
                    n = QB * i + b
                    first = isinstance(i, int) and i == 0
                    weighted_low(n, b)
                    if not first or b >= 2:
                        scattered_low(n - 2, (b - 2) % QB)
                    if not first or b >= 3:
                        residual(n - 3, (b - 3) % QB)
                        out_stats(n - 3)

            peeled(dve, NQ, attend)
            for n in (NB - 2, NB - 1):
                scattered_low(n, n % QB)
            for n in range(NB - 3, NB):
                residual(n, n % QB)
                out_stats(n)
            for n, made in ((NB - QB, NQ), (NB - QB + 1, NQ), (NB - 1, NQ + 1)):
                dve.wait_ge(S["rstd_done"], made)
                norm.apply_on_dve(dve, n, n % QB, other=last_norm).then_inc(S["xd_done"], 1)

        @block.tensor
        def _(pe):
            def gather_quad(g, last):
                for h in (0, 1):
                    n = QB * g + 2 * h
                    for s in (0, 1):
                        pe.wait_ge(S["xl_done"], n + s + 1)
                        for c in range(C):
                            cols = slice(c * D, (c + 1) * D)
                            for part in (XH, XL):
                                ins = pe.matmul(sh.psum[:, s, :], part[:, s, cols], GZ[:, c, :, :],
                                                start=(c == 0 and part is XH), stop=(c == C - 1 and part is XL))
                        ins.then_inc(S["z_mm"], 1)
                    wait(pe, S["uv_out"], 2 * n)
                    for s in (0, 1):
                        pe.wait_ge(S["z_lo"], n + s + 1)
                        product(pe, sh.psum[:, 2 + s, 0:NE], (WT[0][:, 0, :], WT[1][:, 0, :]),
                                (ZH[:, s, 0:NE], ZL[:, s, 0:NE]))
                        for k in range(K):
                            cols = slice(NE + k * P, NE + (k + 1) * P)
                            ins = product(pe, sh.psum[:, 2 + s, cols], (ZH[:, s, cols], ZL[:, s, cols]),
                                          (WT[0][:, 1, :], WT[1][:, 1, :]))
                        ins.then_inc(S["uv_mm"], 1)
                    if h == 0:
                        wait(pe, S["sc_done"], g)
                    if isinstance(g, int) and n == 0:
                        pe.wait_ge(S["wide_done"], 1)
                    for s in (0, 1):
                        pe.wait_ge(S["lr_done"], n + s + 1)
                        b = 2 * h + s
                        pe.matmul(sh.psum[0:R, 4, 0:NE], wide[:, R - NH - NH * b:2 * R - NH - NH * b], lr[:, s, :],
                                  start=(b == 0), stop=(b == QB - 1)).then_inc(S["sc_mm"], 1)

            peeled(pe, NQ, gather_quad)
            for part, quads in enumerate(QUADS):
                for bk, rows, ready, count in ((5, s2, "ex_done", part + 1), (6, sco, "soft", 4 * (part + 1))):
                    pe.wait_ge(S[ready], count)
                    for k in range(K):
                        for q in range(quads.start, quads.stop):
                            at = (k * NQ + q) * R
                            ins = pe.transpose(sh.psum[:, bk, at:at + R], rows[:, q, k * P:(k + 1) * P],
                                               sh.ident[0:R, 0:R])
            ins.then_inc(S["at_mm"], 1)

            def project(n, b):
                pe.wait_ge(S["y_lo"], n + 1)
                wait(pe, S["o_add"], n - 1)
                for c in range(C):
                    cols = slice(c * P, (c + 1) * P)
                    ins = product(pe, sh.psum[:, 4 + b, cols], (ZH[:, b, cols], ZL[:, b, cols]),
                                  (WT[0][:, 2, :], WT[1][:, 2, :]))
                ins.then_inc(S["o_mm"], 1)

            def attend(i, last):
                for b in range(QB):
                    n = QB * i + b
                    pe.wait_ge(S["va_lo"], n + 1)
                    wait(pe, S["y_lo"], n - QB + 1)
                    for k in range(K):
                        for part in (vah, val):
                            ins = pe.matmul(sh.psum[:, b, :], part[:, b, k, :], GsT[:, k, :],
                                            start=(k == 0 and part is vah), stop=(k == K - 1 and part is val))
                    ins.then_inc(S["y_mm"], 1)
                    if not isinstance(i, int) or n >= 2:
                        project(n - 2, (b - 2) % QB)

            peeled(pe, NQ, attend)
            for n in (NB - 2, NB - 1):
                project(n, n % QB)


def diffusion_gnn_stack(nc, out, **d):
    sh = Shared()
    sh.NB, sh.N, sh.D = d["x"].shape
    sh.C = sh.N // P
    assert sh.D == P and sh.NB % QB == 0 and sh.N == 512
    with ExitStack() as ctx:
        ctx.enter_context(nc.allow_non_contiguous_dma(reason="a few hundred elements of columns"))
        sb, sem = allocators(nc, ctx)
        sh.X = sb("X", [P, sh.C, sh.NB, sh.D])
        sh.ident = sb("ident", [P, P])
        sh.HALF, sh.PER_D, sh.QUARTER, sh.EPS, sh.ROOT, sh.MINUS, sh.ONE = range(7)
        sh.const_values = (0.5, 1.0 / sh.D, 0.25, EPS, -0.5, -1.0, 1.0)
        sh.const = sb("const", [P, len(sh.const_values), sh.C * QB])
        sh.psum = ctx.enter_context(nc.psum_tensor("psum", [P, 8, 512], F32))
        sh.norm = NormBuffers(sb, sem, sh)
        sh.A = sb("A", [P, sh.C, sh.N])
        sh.NE = d["L3_gnn_src"].shape[0]
        assert sh.NE % P == 0 and 2 * sh.NE == sh.N
        sh.R = QB * d["L3_gnn_a"].shape[0]
        sh.dinv = sb("dinv", [P, sh.C])
        sh.rs = sb("rs", [P, sh.C])
        sh.drow = sb("drow", [P, sh.N])
        sh.ioc = sb("ioc", [P, sh.C])
        sh.ss = sb("ss", [P, 2, sh.NE])
        sh.sc = sb("sc", [P, sh.NE // P])
        sh.lg = sb("lg", [sh.R, sh.NE])
        with ExitStack() as early:
            esb, _ = allocators(nc, early)
            sh.bias0 = esb("bias0", [P, sh.C, sh.D])
            sh.LT = [(esb(f"LT{r}h", [P, sh.C, sh.N], F32R), esb(f"LT{r}l", [P, sh.C, sh.N], F32R))
                     for r in range(BABY)]
            sh.E = (esb("Eh", [P, BABY, NCO // BABY, sh.D], F32R), esb("El", [P, BABY, NCO // BABY, sh.D], F32R))
            sh.Xh = esb("Xh", [P, sh.C, QB, sh.D], F32R)
            sh.Xl = esb("Xl", [P, sh.C, QB, sh.D], F32R)
            phase_operators(nc, sh, d)
            phase_diffusion(nc, sh, d)

        phase_recurrent(nc, sh, d)
        sh.GZ = sb("GZ", [P, sh.C, 2, sh.NE], F32R)
        sh.GsT = sb("GsT", [P, sh.NE // P, sh.N], F32R)
        sh.aWT = (sb("aWTh", [P, 3, P], F32R), sb("aWTl", [P, 3, P], F32R))
        phase_batchnorm(nc, sh, d)
        phase_attention(nc, sh, d, out)


OUTPUT_SHAPE = (16, 512, 128)


def kernel(**inputs):
    import numpy as np
    import concourse.bacc as bacc
    from concourse.bass_utils import run_bass_kernel_spmd

    nc = bacc.Bacc("TRN2", target_bir_lowering=False, num_devices=1)
    arrays, tensors = {}, {}
    for name, value in inputs.items():
        a = np.ascontiguousarray(value)
        arrays[f"in_{name}"] = a
        tensors[name] = nc.dram_tensor(f"in_{name}", a.shape, mybir.dt.from_np(a.dtype), kind="ExternalInput").ap()
    out = nc.dram_tensor("out", OUTPUT_SHAPE, F32, kind="ExternalOutput").ap()
    diffusion_gnn_stack(nc, out, **tensors)
    results = run_bass_kernel_spmd(nc, [arrays], core_ids=[0])
    return results.results[0]["out"]
```
